# Optimizing a Trainium2 kernel written in Bass

```python
import numpy as np
import jax
import jax.numpy as jnp

def _softmax(x, axis=-1):
    return jax.nn.softmax(x, axis=axis)

def _gelu(x):
    return jax.nn.gelu(x, approximate=True)

def _silu(x):
    return jax.nn.silu(x)

def _sigmoid(x):
    return jax.nn.sigmoid(x)

def _layernorm(x, axis=-1, eps=1e-05):
    m = jnp.mean(x, axis=axis, keepdims=True)
    v = jnp.var(x, axis=axis, keepdims=True)
    return (x - m) / jnp.sqrt(v + eps)

def _scatter_add(tgt, idx, src, axis=0):
    return tgt.at[idx].add(src)

def _segment_sum(src, seg, n):
    return jax.ops.segment_sum(src, seg, n)
kernel_name = 'mk_metaformer_d2_conv_nchw256_r4_7bec02'

def setup_inputs(seed: int=0):
    np.random.seed(seed)
    _w = jnp.asarray

    def _rec_inputs():
        import jax
        import jax.numpy as jnp
        _gk = jax.random.key(seed)
        x = -0.0003929 + 0.9999 * jax.random.normal(jax.random.fold_in(_gk, 1), (16, 64, 16, 16), jnp.float32)
        return x
    x = _rec_inputs()

    def _L0_conv_setup():
        import jax, jax.numpy as jnp
        import numpy as np
        HEADS = 8
        DIM_HEAD = 32
        key = jax.random.key(seed)
        k1, k2, k3 = jax.random.split(key, 3)
        b, c, h, w = (16, 64, 16, 16)
        hidden = HEADS * DIM_HEAD
        x = jax.random.normal(k1, (b, c, h, w), dtype=jnp.float32)
        w_qkv = jax.random.normal(k2, (3 * hidden, c), dtype=jnp.float32) * (1.0 / np.sqrt(c))
        w_out = jax.random.normal(k3, (c, hidden), dtype=jnp.float32) * (1.0 / np.sqrt(hidden))
        b_out = jnp.zeros((c,), dtype=jnp.float32)
        return {'x': x, 'w_qkv': w_qkv, 'w_out': w_out, 'b_out': b_out}
    _L0_conv_all = _L0_conv_setup()
    _L0_conv_in = {k: v for k, v in _L0_conv_all.items() if k in ('w_qkv', 'w_out', 'b_out')}
    del _L0_conv_all

    def _L0_ffn_setup():
        import jax, jax.numpy as jnp
        import numpy as np
        B, N, D = (16, 1024, 64)
        NUM_EXPERTS, TOP_K, HEADS = (4, 2, 4)
        N_EDGES = 262144
        LN_EPS = 1e-05

        def _layernorm(x, g, b):
            mu = x.mean(-1, keepdims=True)
            var = ((x - mu) ** 2).mean(-1, keepdims=True)
            return (x - mu) * jax.lax.rsqrt(var + LN_EPS) * g + b

        def _forward(x, edge_index, W_gat, att_src, att_dst, b_gat, ln_gamma, ln_beta, W1, b1, W2, b2):
            Bc, Nc, Dc = x.shape
            M = Bc * Nc
            x_flat = x.reshape(M, Dc)
            h = (x_flat @ W_gat).reshape(M, HEADS, NUM_EXPERTS)
            loops = jnp.arange(M, dtype=edge_index.dtype)
            src = jnp.concatenate([edge_index[0], loops])
            dst = jnp.concatenate([edge_index[1], loops])
            a_src = (h * att_src).sum(-1)
            a_dst = (h * att_dst).sum(-1)
            e = jax.nn.leaky_relu(a_src[src] + a_dst[dst], negative_slope=0.2)
            e_max = jax.ops.segment_max(e, dst, num_segments=M)
            ee = jnp.exp(e - e_max[dst])
            denom = jax.ops.segment_sum(ee, dst, num_segments=M)
            alpha = ee / (denom[dst] + 1e-16)
            msg = h[src] * alpha[:, :, None]
            agg = jax.ops.segment_sum(msg, dst, num_segments=M).reshape(M, HEADS * NUM_EXPERTS) + b_gat
            scores = _layernorm(agg, ln_gamma, ln_beta).reshape(M, HEADS, NUM_EXPERTS).mean(1)
            scores = scores.reshape(Bc, Nc, NUM_EXPERTS)
            topk_s, topk_i = jax.lax.top_k(scores, TOP_K)
            w = jax.nn.softmax(topk_s, axis=-1)
            out = jnp.zeros_like(x)
            for ei in range(NUM_EXPERTS):
                g = jnp.where(topk_i == ei, w, 0.0).sum(-1)
                hh = jax.nn.gelu(x @ W1[ei] + b1[ei], approximate=False)
                out = out + g[..., None] * (hh @ W2[ei] + b2[ei])
            return out
        key = jax.random.key(seed)
        ks = jax.random.split(key, 8)
        s = 0.05
        return {'x': jax.random.normal(ks[0], (B, N, D), jnp.float32), 'W_gat': jax.random.normal(ks[1], (D, HEADS * NUM_EXPERTS), jnp.float32) * s, 'att_src': jax.random.normal(ks[2], (HEADS, NUM_EXPERTS), jnp.float32) * s, 'att_dst': jax.random.normal(ks[3], (HEADS, NUM_EXPERTS), jnp.float32) * s, 'b_gat': jnp.zeros((HEADS * NUM_EXPERTS,), jnp.float32), 'ln_gamma': jnp.ones((HEADS * NUM_EXPERTS,), jnp.float32), 'ln_beta': jnp.zeros((HEADS * NUM_EXPERTS,), jnp.float32), 'W1': jax.random.normal(ks[4], (NUM_EXPERTS, D, 2 * D), jnp.float32) * s, 'b1': jnp.zeros((NUM_EXPERTS, 2 * D), jnp.float32), 'W2': jax.random.normal(ks[5], (NUM_EXPERTS, 2 * D, D), jnp.float32) * s, 'b2': jnp.zeros((NUM_EXPERTS, D), jnp.float32), 'edge_index': jax.random.randint(ks[6], (2, N_EDGES), 0, B * N, jnp.int32)}
    _L0_ffn_all = _L0_ffn_setup()
    _L0_ffn_in = {k: v for k, v in _L0_ffn_all.items() if k in ('W_gat', 'att_src', 'att_dst', 'b_gat', 'ln_gamma', 'ln_beta', 'W1', 'b1', 'W2', 'b2', 'edge_index')}
    del _L0_ffn_all

    def _L1_conv_setup():
        import jax, jax.numpy as jnp
        import numpy as np
        HEADS = 4
        HEAD_DIM = 32
        DIM = 64
        HIDDEN = HEADS * HEAD_DIM
        SCALE = HEAD_DIM ** (-0.5)

        def rmsnorm(x, g):
            inv = jax.lax.rsqrt(jnp.sum(x * x, axis=1, keepdims=True) + 1e-12)
            return x * inv * (g * x.shape[1] ** 0.5)[None, :, None, None]
        key = jax.random.key(seed)
        k1, k2, k3 = jax.random.split(key, 3)
        b, H, W = (16, 16, 16)
        x = jax.random.normal(k1, (b, DIM, H, W), dtype=jnp.float32)
        W_qkv = jax.random.normal(k2, (3 * HIDDEN, DIM), dtype=jnp.float32) * DIM ** (-0.5)
        W_out = jax.random.normal(k3, (DIM, HIDDEN), dtype=jnp.float32) * HIDDEN ** (-0.5)
        b_out = jnp.zeros((DIM,), dtype=jnp.float32)
        g_norm = jnp.ones((DIM,), dtype=jnp.float32)
        g_out = jnp.ones((DIM,), dtype=jnp.float32)
        return {'x': x, 'W_qkv': W_qkv, 'W_out': W_out, 'b_out': b_out, 'g_norm': g_norm, 'g_out': g_out}
    _L1_conv_all = _L1_conv_setup()
    _L1_conv_in = {k: v for k, v in _L1_conv_all.items() if k in ('W_qkv', 'W_out', 'b_out', 'g_norm', 'g_out')}
    del _L1_conv_all

    def _L1_ffn_setup():
        import jax, jax.numpy as jnp
        import numpy as np
        TOP_K = 2
        key = jax.random.key(seed)
        ks = jax.random.split(key, 4)
        B, L, D, H, E = (8, 1024, 64, 256, 8)
        s = 0.02
        return {'x': jax.random.normal(ks[0], (B, L, D), jnp.float32), 'Wg': jax.random.normal(ks[1], (D, E), jnp.float32) * s, 'bg': jnp.zeros((E,), jnp.float32), 'W1': jax.random.normal(ks[2], (E, D, H), jnp.float32) * s, 'b1': jnp.zeros((E, H), jnp.float32), 'W2': jax.random.normal(ks[3], (E, H, D), jnp.float32) * s, 'b2': jnp.zeros((E, D), jnp.float32)}
    _L1_ffn_all = _L1_ffn_setup()
    _L1_ffn_in = {k: v for k, v in _L1_ffn_all.items() if k in ('Wg', 'bg', 'W1', 'b1', 'W2', 'b2')}
    del _L1_ffn_all
    return {'x': x, 'L0_conv_w_qkv': _L0_conv_in['w_qkv'], 'L0_conv_w_out': _L0_conv_in['w_out'], 'L0_conv_b_out': _L0_conv_in['b_out'], 'L0_ffn_W_gat': _L0_ffn_in['W_gat'], 'L0_ffn_att_src': _L0_ffn_in['att_src'], 'L0_ffn_att_dst': _L0_ffn_in['att_dst'], 'L0_ffn_b_gat': _L0_ffn_in['b_gat'], 'L0_ffn_ln_gamma': _L0_ffn_in['ln_gamma'], 'L0_ffn_ln_beta': _L0_ffn_in['ln_beta'], 'L0_ffn_W1': _L0_ffn_in['W1'], 'L0_ffn_b1': _L0_ffn_in['b1'], 'L0_ffn_W2': _L0_ffn_in['W2'], 'L0_ffn_b2': _L0_ffn_in['b2'], 'L0_ffn_edge_index': _L0_ffn_in['edge_index'], 'L1_conv_W_qkv': _L1_conv_in['W_qkv'], 'L1_conv_W_out': _L1_conv_in['W_out'], 'L1_conv_b_out': _L1_conv_in['b_out'], 'L1_conv_g_norm': _L1_conv_in['g_norm'], 'L1_conv_g_out': _L1_conv_in['g_out'], 'L1_ffn_Wg': _L1_ffn_in['Wg'], 'L1_ffn_bg': _L1_ffn_in['bg'], 'L1_ffn_W1': _L1_ffn_in['W1'], 'L1_ffn_b1': _L1_ffn_in['b1'], 'L1_ffn_W2': _L1_ffn_in['W2'], 'L1_ffn_b2': _L1_ffn_in['b2']}

def reference(x, L0_conv_w_qkv, L0_conv_w_out, L0_conv_b_out, L0_ffn_W_gat, L0_ffn_att_src, L0_ffn_att_dst, L0_ffn_b_gat, L0_ffn_ln_gamma, L0_ffn_ln_beta, L0_ffn_W1, L0_ffn_b1, L0_ffn_W2, L0_ffn_b2, L0_ffn_edge_index, L1_conv_W_qkv, L1_conv_W_out, L1_conv_b_out, L1_conv_g_norm, L1_conv_g_out, L1_ffn_Wg, L1_ffn_bg, L1_ffn_W1, L1_ffn_b1, L1_ffn_W2, L1_ffn_b2):
    import jax
    import jax.numpy as jnp

    def _L0_conv_ref(x, w_qkv, w_out, b_out):
        import jax, jax.numpy as jnp
        import numpy as np
        HEADS = 8
        DIM_HEAD = 32
        b, c, h, w = x.shape
        n = h * w
        qkv = jnp.einsum('oc,bchw->bohw', w_qkv, x)
        qkv = qkv.reshape(b, 3, HEADS, DIM_HEAD, n)
        q, k, v = (qkv[:, 0], qkv[:, 1], qkv[:, 2])
        k = jax.nn.softmax(k, axis=-1)
        context = jnp.einsum('bhdn,bhen->bhde', k, v)
        out = jnp.einsum('bhde,bhdn->bhen', context, q)
        out = out.reshape(b, HEADS * DIM_HEAD, h, w)
        return jnp.einsum('oc,bchw->bohw', w_out, out) + b_out[None, :, None, None]

    def _L0_ffn_ref(x, W_gat, att_src, att_dst, b_gat, ln_gamma, ln_beta, W1, b1, W2, b2, edge_index):
        import jax, jax.numpy as jnp
        import numpy as np
        B, N, D = (16, 1024, 64)
        NUM_EXPERTS, TOP_K, HEADS = (4, 2, 4)
        N_EDGES = 262144
        LN_EPS = 1e-05

        def _layernorm(x, g, b):
            mu = x.mean(-1, keepdims=True)
            var = ((x - mu) ** 2).mean(-1, keepdims=True)
            return (x - mu) * jax.lax.rsqrt(var + LN_EPS) * g + b

        def _forward(x, edge_index, W_gat, att_src, att_dst, b_gat, ln_gamma, ln_beta, W1, b1, W2, b2):
            Bc, Nc, Dc = x.shape
            M = Bc * Nc
            x_flat = x.reshape(M, Dc)
            h = (x_flat @ W_gat).reshape(M, HEADS, NUM_EXPERTS)
            loops = jnp.arange(M, dtype=edge_index.dtype)
            src = jnp.concatenate([edge_index[0], loops])
            dst = jnp.concatenate([edge_index[1], loops])
            a_src = (h * att_src).sum(-1)
            a_dst = (h * att_dst).sum(-1)
            e = jax.nn.leaky_relu(a_src[src] + a_dst[dst], negative_slope=0.2)
            e_max = jax.ops.segment_max(e, dst, num_segments=M)
            ee = jnp.exp(e - e_max[dst])
            denom = jax.ops.segment_sum(ee, dst, num_segments=M)
            alpha = ee / (denom[dst] + 1e-16)
            msg = h[src] * alpha[:, :, None]
            agg = jax.ops.segment_sum(msg, dst, num_segments=M).reshape(M, HEADS * NUM_EXPERTS) + b_gat
            scores = _layernorm(agg, ln_gamma, ln_beta).reshape(M, HEADS, NUM_EXPERTS).mean(1)
            scores = scores.reshape(Bc, Nc, NUM_EXPERTS)
            topk_s, topk_i = jax.lax.top_k(scores, TOP_K)
            w = jax.nn.softmax(topk_s, axis=-1)
            out = jnp.zeros_like(x)
            for ei in range(NUM_EXPERTS):
                g = jnp.where(topk_i == ei, w, 0.0).sum(-1)
                hh = jax.nn.gelu(x @ W1[ei] + b1[ei], approximate=False)
                out = out + g[..., None] * (hh @ W2[ei] + b2[ei])
            return out
        return _forward(x, edge_index, W_gat, att_src, att_dst, b_gat, ln_gamma, ln_beta, W1, b1, W2, b2)

    def _L1_conv_ref(x, W_qkv, W_out, b_out, g_norm, g_out):
        import jax, jax.numpy as jnp
        import numpy as np
        HEADS = 4
        HEAD_DIM = 32
        DIM = 64
        HIDDEN = HEADS * HEAD_DIM
        SCALE = HEAD_DIM ** (-0.5)

        def rmsnorm(x, g):
            inv = jax.lax.rsqrt(jnp.sum(x * x, axis=1, keepdims=True) + 1e-12)
            return x * inv * (g * x.shape[1] ** 0.5)[None, :, None, None]
        b, c, H, W = x.shape
        n = H * W
        xn = rmsnorm(x, g_norm)
        qkv = jnp.einsum('bchw,oc->bohw', xn, W_qkv)
        qkv = qkv.reshape(b, 3, HEADS, HEAD_DIM, n)
        q, k, v = (qkv[:, 0], qkv[:, 1], qkv[:, 2])
        q = jax.nn.softmax(q, axis=-2)
        k = jax.nn.softmax(k, axis=-1)
        context = jnp.einsum('bhdn,bhen->bhde', k, v)
        out = jnp.einsum('bhde,bhdn->bhen', context, q) * SCALE
        out = out.reshape(b, HIDDEN, H, W)
        out = jnp.einsum('bchw,oc->bohw', out, W_out) + b_out[None, :, None, None]
        return rmsnorm(out, g_out)

    def _L1_ffn_ref(x, Wg, bg, W1, b1, W2, b2):
        import jax, jax.numpy as jnp
        import numpy as np
        TOP_K = 2
        B, L, D = x.shape
        E = W1.shape[0]
        xf = x.reshape(-1, D)
        gate_logits = xf @ Wg + bg
        top_w, top_i = jax.lax.top_k(gate_logits, TOP_K)
        top_w = jax.nn.softmax(top_w, axis=-1)
        w_dense = jnp.sum(jax.nn.one_hot(top_i, E, dtype=xf.dtype) * top_w[..., None], axis=1)
        out = jnp.zeros_like(xf)
        for e in range(E):
            h = jax.nn.gelu(xf @ W1[e] + b1[e], approximate=False)
            out = out + w_dense[:, e:e + 1] * (h @ W2[e] + b2[e])
        return out.reshape(B, L, D)

    def _gn(v, G=32, eps=1e-05):
        B_, C_, H_, W_ = v.shape
        g = v.reshape(B_, G, C_ // G, H_, W_)
        m = jnp.mean(g, axis=(2, 3, 4), keepdims=True)
        s = jnp.var(g, axis=(2, 3, 4), keepdims=True)
        return ((g - m) / jnp.sqrt(s + eps)).reshape(v.shape)

    def _ln_c(v, eps=1e-06):
        m = jnp.mean(v, axis=1, keepdims=True)
        s = jnp.var(v, axis=1, keepdims=True)
        return (v - m) / jnp.sqrt(s + eps)

    def _ln_t(v, eps=1e-05):
        m = jnp.mean(v, axis=-1, keepdims=True)
        s = jnp.var(v, axis=-1, keepdims=True)
        return (v - m) / jnp.sqrt(s + eps)

    def _to_tokens(v):
        B_, C_, H_, W_ = v.shape
        return v.reshape(B_, C_, H_ * W_).transpose(0, 2, 1)

    def _from_tokens(t, like):
        B_, C_, H_, W_ = like.shape
        return t.transpose(0, 2, 1).reshape(B_, C_, H_, W_)
    x = x + _L0_conv_ref(_ln_c(x), L0_conv_w_qkv, L0_conv_w_out, L0_conv_b_out)
    t = _to_tokens(x)
    t = t + _L0_ffn_ref(_ln_t(t), L0_ffn_W_gat, L0_ffn_att_src, L0_ffn_att_dst, L0_ffn_b_gat, L0_ffn_ln_gamma, L0_ffn_ln_beta, L0_ffn_W1, L0_ffn_b1, L0_ffn_W2, L0_ffn_b2, L0_ffn_edge_index)
    x = _from_tokens(t, x)
    x = x + _L1_conv_ref(_ln_c(x), L1_conv_W_qkv, L1_conv_W_out, L1_conv_b_out, L1_conv_g_norm, L1_conv_g_out)
    t = _to_tokens(x)
    t = t + _L1_ffn_ref(_ln_t(t), L1_ffn_Wg, L1_ffn_bg, L1_ffn_W1, L1_ffn_b1, L1_ffn_W2, L1_ffn_b2)
    x = _from_tokens(t, x)
    return x

_drawn_inputs = setup_inputs


def setup_inputs(seed=0):
    import zlib

    import numpy as np

    out = dict(_drawn_inputs(seed))
    spreads = {'L0_conv_b_out': (0.0, 0.1),
     'L0_ffn_b_gat': (0.0, 0.446),
     'L0_ffn_ln_gamma': (1.0, 0.6),
     'L0_ffn_ln_beta': (0.0, 0.415),
     'L0_ffn_b1': (0.0, 0.413),
     'L0_ffn_b2': (0.0, 0.1),
     'L1_conv_b_out': (0.0, 0.1),
     'L1_conv_g_norm': (1.0, 0.2),
     'L1_conv_g_out': (1.0, 0.2),
     'L1_ffn_bg': (0.0, 0.292),
     'L1_ffn_b1': (0.0, 0.8),
     'L1_ffn_b2': (0.0, 0.1)}
    factors = {'L0_ffn_att_src': 8.0, 'L0_ffn_att_dst': 8.0, 'L1_ffn_W1': 5.23, 'L1_ffn_W2': 4.465}
    for name, (base, spread) in spreads.items():
        noise = np.random.default_rng([zlib.crc32(name.encode()), seed]).standard_normal(out[name].shape)
        drawn = base * np.exp(spread * noise) if base else spread * noise
        out[name] = jnp.asarray(drawn.astype(out[name].dtype))
    for name, factor in factors.items():
        out[name] = (out[name] * factor).astype(out[name].dtype)
    return out
```

```python
from contextlib import ExitStack

import concourse.bass as bass
from concourse import mybir

F32 = mybir.dt.float32
BF16 = mybir.dt.bfloat16
I32 = mybir.dt.int32
ALU = mybir.AluOpType
ACT = mybir.ActivationFunctionType
X = mybir.AxisListType.X
RMAX = bass.bass_isa.ReduceOp.max

P = 128
B, C, HW = 16, 64, 256
NODES = B * HW
NT = NODES // P
QT = 8
NQ = NT // QT
QB = 4
HEADS, NE0 = 4, 4
F0 = HEADS * NE0
HID0 = 128
NE1, HID1 = 8, 256
NH1 = HID1 // P
NEDGE = 262144
EC = NEDGE // P
SEGS, ROUNDS, TOP = 4, 8, 8
SEG = EC // SEGS
GC = SEGS * ROUNDS * TOP
EB = 8
ITC = 2 * EB
ITERS = GC // ITC
REST = EC // GC
HC = 16
HB = EC // HC // ITERS
LO = NODES // P
FV = F0 + HEADS
FS = HEADS + F0
FD = 2 * HEADS
FH = FV // 2
HEAD_DIM = 32
LN_C_EPS, LN_T_EPS, LN_EPS, RMS_EPS = 1e-6, 1e-5, 1e-5, 1e-12
SLOPE = 0.2


def metaformer(nc, ins, table_s, table_d, out):
    (x, w_qkv0, w_out0, b_out0, W_gat, att_src, att_dst, b_gat, ln_gamma, ln_beta, W1_0, b1_0, W2_0, b2_0,
     edges, w_qkv1, w_out1, b_out1, g_norm, g_out, Wg, bg, W1_1, b1_1, W2_1, b2_1) = ins

    with ExitStack() as ctx:
        def sb(name, shape, dt=F32):
            return ctx.enter_context(nc.sbuf_tensor(name, shape, dt))

        sems = {}

        def sem(name):
            if name not in sems:
                sems[name] = ctx.enter_context(nc.semaphore(name))
            return sems[name]

        PS = ctx.enter_context(nc.psum_tensor("PS", [P, 8, 512], F32))
        ident = sb("ident", [P, P])
        zeros = sb("zeros", [P, P])
        iota_i = sb("iota_i", [P, P], I32)
        iota = sb("iota", [P, P])
        iota_h = sb("iota_h", [P, P, HC], BF16)
        blocks = sb("blocks", [P, P])
        before = sb("before", [P, NE1, NE1])
        mhalf = sb("mhalf", [P, NT])
        wkv0 = sb("wkv0", [P, 4, C])
        wq0 = sb("wq0", [P, 2, C])
        wqkv1 = sb("wqkv1", [P, 3, C])
        wo0 = sb("wo0", [C, 256])
        wo1 = sb("wo1", [C, P])
        b1r0 = sb("b1r0", [NE0, P])
        b1r1 = sb("b1r1", [NE1 * NH1, P])
        wkvT0 = sb("wkvT0", [C, 512])
        wqkvT1 = sb("wqkvT1", [C, 384])
        cols = sb("cols", [P, 3 * C + NE0 + NE1 * NH1])
        woT0 = cols[:, 0:2 * C].rearrange("p (g c) -> p g c", g=2)
        woT1 = cols[:, 2 * C:3 * C].rearrange("p (g c) -> p g c", g=1)
        b1c0 = cols[:, 3 * C:3 * C + NE0]
        b1c1 = cols[:, 3 * C + NE0:]
        wgat = sb("wgat", [C, FS + HEADS])
        attr = sb("attr", [C, 2, F0])
        attm = sb("attm", [C, 2, F0])
        w1_0 = sb("w1_0", [C, NE0, HID0])
        w2_0 = sb("w2_0", [HID0, NE0, C])
        b2b0 = sb("b2b0", [P, NE0 * C])
        b2b1 = sb("b2b1", [P, NE1 * C])
        wg = sb("wg", [C, NE1])
        bgb = sb("bgb", [P, NE1])
        bo0 = sb("bo0", [P, C])
        bo1 = sb("bo1", [P, C])
        go1 = sb("go1", [P, C])
        gn1 = sb("gn1", [C, 1])
        gat_rows = sb("gat_rows", [P, 3, F0])
        xt = sb("xt", [P, NT, C])
        xn = sb("xn", [P, NT, C])
        sq = sb("sq", [P, NT, C])
        red = sb("red", [P, 8, NT])
        xc = sb("xc", [C, NODES])
        nmx = sb("nmx", [P, 8, QB])
        ksum = sb("ksum", [P, 2, B])
        rks = sb("rks", [P, 2, B])
        big = sb("big", [P, 12800])
        oute = sb("oute", [P, NT, NE0, C])
        wide = oute[:, :, :, :].rearrange("p t e c -> p (t e c)")
        Ys = [wide[0:C, 4096 * k:4096 * (k + 1)].rearrange("p (g b n) -> p g b n", g=2, b=B) for k in range(2)]
        ek = big[:, 0:2048].rearrange("p (a n) -> p a n", a=2)
        ekt = big[:, 2048:4096].rearrange("p (a t n) -> p a t n", a=2, t=QT)
        ctxT = big[:, 4096:8192].rearrange("p (g b n) -> p g b n", g=2, b=B)
        T = big[:, 8192:10240].rearrange("p (g b n) -> p g b n", g=2, b=B)
        MT = big[0:C, 10240:11264].rearrange("p (b n) -> p b n", b=B)
        qc = wide[:, 0:4096]
        prod = big[:, 0:2 * EB * FV * LO].rearrange("p (a j f l) -> p a j f l", a=2, j=EB, f=FV)
        hoff = 2 * EB * FV * LO
        hw, hl = P * HC // 2, LO * HC // 2
        hist_hi = [big[:, hoff + (hw + hl) * a:hoff + (hw + hl) * a + hw].bitcast(BF16)
                   .rearrange("p (h c) -> p h c", c=HC) for a in range(2)]
        hist_lo = [big[:, hoff + (hw + hl) * a + hw:hoff + (hw + hl) * (a + 1)].bitcast(BF16)
                   .rearrange("p (h c) -> p h c", c=HC) for a in range(2)]
        hid1 = [r.rearrange("p (k n) -> p k n", k=NE1 * NH1) for r in (big[:, 0:8192], wide)]
        ob = big[:, 8192:12288]
        keys = sb("keys", [P, GC + EC])
        rows = keys[:, GC:]
        big2 = sb("hist_dst", [P, EC // 2])
        dhi_h = big2[:, :].bitcast(BF16)
        dlo_h = sb("dlo_h", [P, EC], BF16)
        w1_1 = keys[0:C, 0:NE1 * HID1].rearrange("p (e n) -> p e n", e=NE1)
        w2_1 = big2[:, :].rearrange("p (e k n) -> p e k n", e=NE1, k=NH1)
        ebi = big[:, 8192:12288].bitcast(I32).rearrange("p (a n) -> p a n", a=2)
        etmp = wide.rearrange("p (a n) -> p a n", a=4)
        m8 = sb("m8", [P, SEGS, TOP])
        dec = sb("dec", [P, 2, GC])
        deci = sb("deci", [P, 3, GC], I32)
        idx_s = sb("idx_s", [P, GC], I32)
        idx_d = sb("idx_d", [P, GC], I32)
        dhi = sb("dhi", [P, GC])
        dlo = sb("dlo", [P, GC])
        stage_s = sb("stage_s", [P, ITC], I32)
        stage_d = sb("stage_d", [P, ITC], I32)
        flagf = sb("flagf", [P, 2])
        flagi = sb("flagi", [P, 1], I32)
        tab_s = sb("tab_s", [P, NT, FS])
        tab_d = sb("tab_d", [P, NT, FD])
        gmax = sb("gmax", [P, 2, HEADS])
        last = sb("last", [P, FS])
        gs = sb("gs", [P, 2, EB, FS])
        gd = sb("gd", [P, 2, EB, FD])
        es = sb("es", [P, 2, 3, EB, HEADS])
        val = sb("val", [P, 2, EB, FV])
        one_hi = sb("one_hi", [P, 2, EB, P])
        one_lo = sb("one_lo", [P, 2, EB, LO])
        nod = sb("nod", [P, 6, NT, HEADS])
        num = sb("num", [P, 2, NT, FV])
        cnt = sb("cnt", [P, NT])
        sc = sb("sc", [P, 4, NT, NE1])
        hid0 = xn[:, :, :].rearrange("p t c -> p (t c)").rearrange("p (e n) -> p e n", e=NE0)

        block = ctx.enter_context(nc.Block())

        def qe(u):
            return big[:, 4096 + 512 * (u % 4):4096 + 512 * (u % 4 + 1)].rearrange("p (k d) -> p k d", d=HEAD_DIM)

        def bc(ap, axis, n):
            a = ap.unsqueeze(axis)
            shape = list(a.shape)
            shape[axis] = n
            return a.broadcast_to(shape)

        def row(v, n=P):
            return v.unsqueeze(0).broadcast_to([n, v.shape[0]])

        @block.sync
        def _(sp):
            ei = edges.rearrange("a (p n) -> p a n", p=P)
            sp.dma_start(ebi, ei).then_inc(sem("edges_in"), 16)
            sp.dma_start(xc[:, :].rearrange("c (b n) -> c b n", b=B),
                         x.rearrange("b c h w -> c b (h w)")).then_inc(sem("x_in"), 16)
            n = 0
            for dst, src in (
                (wkv0[:, :, :], w_qkv0[256:768, :].rearrange("(g p) c -> p g c", p=P)),
                (wq0[:, :, :], w_qkv0[0:256, :].rearrange("(g p) c -> p g c", p=P)),
                (wqkv1[:, :, :], w_qkv1.rearrange("(g p) c -> p g c", p=P)),
                (wo0[:, :], w_out0), (wo1[:, :], w_out1),
                (b1r0[:, :], b1_0), (b1r1[:, :], b1_1.rearrange("e (k n) -> (e k) n", n=P)),
                (bo0[:, :], row(b_out0)),
            ):
                sp.dma_start(dst, src).then_inc(sem("conv_weights_in"), 16)
                n += 1
            assert n == 8
            for dst, src in (
                (wgat[:, HEADS:FS], W_gat),
                (attr[:, 0, :], row(att_src.rearrange("a b -> (a b)"), C)),
                (attr[:, 1, :], row(att_dst.rearrange("a b -> (a b)"), C)),
                (w1_0[:, :, :], W1_0.rearrange("e c n -> c e n")),
                (w2_0[:, :, :], W2_0.rearrange("e n c -> n e c")),
                (b2b0[:, :], row(b2_0.rearrange("e c -> (e c)"))),
                (gat_rows[:, 0, :], row(b_gat)), (gat_rows[:, 1, :], row(ln_gamma)),
                (gat_rows[:, 2, :], row(ln_beta)),
            ):
                sp.dma_start(dst, src).then_inc(sem("ffn0_weights_in"), 16)
                n += 1
            assert n == 17
            for dst, src in (
                (b2b1[:, :], row(b2_1.rearrange("e c -> (e c)"))),
                (wg[:, :], Wg), (bgb[:, :], row(bg)),
                (bo1[:, :], row(b_out1)), (go1[:, :], row(g_out)),
                (gn1[:, :], g_norm.unsqueeze(1)),
            ):
                sp.dma_start(dst, src).then_inc(sem("layer1_weights_in"), 16)
                n += 1
            assert n == 23
            sp.wait_ge(sem("tables_made"), 1)
            sp.dma_start(table_s.rearrange("(t p) f -> p t f", p=P), tab_s[:, :, :]).then_inc(sem("tables_out"), 16)
            sp.dma_start(table_d.rearrange("(t p) f -> p t f", p=P), tab_d[:, :, :]).then_inc(sem("tables_out"), 16)
            sp.wait_ge(sem("tables_out"), 32)
            sp.dma_start(last[:, :], table_s[NODES - 1:NODES, :].broadcast_to([P, FS])).then_inc(sem("last_in"), 16)
            sp.wait_ge(sem("sums_read"), 1)
            sp.dma_start(w1_1, W1_1.rearrange("e c n -> c e n")).then_inc(sem("experts1_in"), 16)
            sp.dma_start(w2_1.rearrange("p e k c -> p (e k) c"), W2_1.rearrange("e (k p) c -> p (e k) c", p=P))\
                .then_inc(sem("experts1_in"), 16)
            for q in range(8):
                sp.wait_ge(sem("yc_made"), q + 1)
                sp.dma_start(out.rearrange("b c h w -> c b (h w)")[:, 2 * q:2 * q + 2, :],
                             xc[:, 512 * q:512 * (q + 1)].rearrange("c (b n) -> c b n", b=2)).then_inc(sem("y_out"), 16)
            sp.wait_ge(sem("y_out"), 128)

        @block.gpsimd
        def _(pool):
            nc.gpsimd.memset(ident[:, :], 0.0).then_inc(sem("const0"), 1)
            nc.gpsimd.memset(before[:, :, :], 1.0).then_inc(sem("const0"), 1)
            nc.gpsimd.iota(iota_i[:, :], [[1, P]], base=0, channel_multiplier=0).then_inc(sem("const0"), 1)
            nc.gpsimd.memset(zeros[:, :], 0.0).then_inc(sem("zeros_made"), 1)
            nc.gpsimd.memset(mhalf[:, :], -0.5).then_inc(sem("zeros_made"), 1)
            pool.wait_ge(sem("const0"), 3)
            nc.gpsimd.affine_select(out=ident[:, :], in_=ident[:, :], compare_op=ALU.not_equal, fill=1.0, base=0,
                                    pattern=[[-1, P]], channel_multiplier=1).then_inc(sem("ident_made"), 1)
            nc.gpsimd.affine_select(out=before[:, :, :], in_=before[:, :, :], compare_op=ALU.is_gt, fill=0.0, base=0,
                                    pattern=[[1, NE1], [-1, NE1]], channel_multiplier=0).then_inc(sem("before_made"), 1)

            def inverse_roots(stage, q):
                pool.wait_ge(sem(f"{stage}_var"), q + 1)
                nc.gpsimd.tensor_tensor(red[:, 3, QT * q:QT * (q + 1)], red[:, 2, QT * q:QT * (q + 1)], mhalf[:, 0:QT],
                                        ALU.pow).then_inc(sem(f"{stage}_rstd"), 1)

            pool.wait_ge(sem("zeros_made"), 2)
            for q in range(NQ):
                inverse_roots("ln0", q)
            pool.wait_ge(sem("rest_max"), 1)
            nc.gpsimd.partition_all_reduce(flagf[:, 1:2], flagf[:, 0:1], P, RMAX).then_inc(sem("rest_all"), 1)
            for q in range(NQ):
                inverse_roots("ln1", q)
            pool.wait_ge(sem("score_max"), 1)
            nc.gpsimd.partition_all_reduce(gmax[:, 1, :], gmax[:, 0, :], P, RMAX).then_inc(sem("score_all"), 1)

            def gathers(it, t):
                for a in range(2):
                    pool.wait_ge(sem(f"rows_used{a}"), it + 1)
                    c0 = t * ITC + a * EB
                    nc.gpsimd.tensor_copy(stage_s[:, a * EB:(a + 1) * EB], idx_s[:, bass.ds(c0, EB)])\
                        .then_inc(sem(f"staged{a}"), 1)
                    nc.gpsimd.tensor_copy(stage_d[:, a * EB:(a + 1) * EB], idx_d[:, bass.ds(c0, EB)])\
                        .then_inc(sem(f"staged{a}"), 1)
                    pool.wait_ge(sem(f"staged{a}"), it * 2 + 2)
                    nc.gpsimd.sem_inc(sem("staging_seen"), 1)
                    for j in range(EB):
                        c = a * EB + j
                        nc.gpsimd.indirect_dma_start(
                            gs[:, a, j, :], None, table_s,
                            bass.IndirectOffsetOnAxis(stage_s[:, c:c + 1], axis=0)).then_inc(sem(f"rows_in{a}"), 16)
                        nc.gpsimd.indirect_dma_start(
                            gd[:, a, j, :], None, table_d,
                            bass.IndirectOffsetOnAxis(stage_d[:, c:c + 1], axis=0)).then_inc(sem(f"rows_in{a}"), 16)

            pool.wait_ge(sem("tables_out"), 32)
            pool.wait_ge(sem("decoded"), 1)
            with nc.gpsimd.Fori(0, ITERS) as t:
                gathers(t, t)
            pool.wait_ge(sem("flag_made"), 1)
            left = nc.gpsimd.value_load(flagi[0:1, 0:1], min_val=0, max_val=1)
            with nc.gpsimd.If(left > 0):
                with nc.gpsimd.Fori(0, REST) as g:
                    pool.wait_ge(sem("decoded"), g + 2)
                    nc.gpsimd.sem_inc(sem("staging_seen"), 1)
                    with nc.gpsimd.Fori(0, ITERS) as t:
                        gathers((g + 1) * ITERS + t, t)

            pool.wait_ge(sem("gat_var"), 1)
            nc.gpsimd.tensor_tensor(red[:, 3, :], red[:, 2, :], mhalf[:, :], ALU.pow).then_inc(sem("gat_rstd"), 1)
            for stage in ("ln2", "ln2r", "ln3r", "ln4"):
                for q in range(NQ):
                    inverse_roots(stage, q)
            pool.wait_ge(sem("gates1"), 1)
            acc_b = num[:, :, :, :].rearrange("p a t f -> p (a t f)")
            bsum = xn[:, :, :]
            pool.wait_ge(sem("xn4_read"), 1)
            for e in range(NE1):
                dst = bsum if e == 0 else sq[:, :, :]
                if e > 1:
                    pool.wait_ge(sem("bias_sum"), e - 1)
                nc.gpsimd.tensor_tensor(dst, bc(b2b1[:, e * C:(e + 1) * C], 1, NT), bc(sc[:, 3, :, e], 2, C), ALU.mult)\
                    .then_inc(sem("bias_term"), 1)
                if e:
                    pool.wait_ge(sem("bias_term"), e + 1)
                    nc.gpsimd.tensor_tensor(bsum, bsum, sq[:, :, :], ALU.add).then_inc(sem("bias_sum"), 1)

        @block.scalar
        def _(act):
            for q in range(NQ):
                act.wait_ge(sem("xt_turned"), q + 1)
                nc.scalar.copy(xt[:, QT * q:QT * (q + 1), :],
                               PS[:, q % 2, :].rearrange("p (t c) -> p t c", c=C)).then_inc(sem("xt_made"), 1)
            act.wait_ge(sem("weights_turned"), 3)
            nc.scalar.copy(wkvT0[:, :], PS[0:C, 4, :]).then_inc(sem("weights_made"), 1)
            nc.scalar.copy(wqkvT1[:, :], PS[0:C, 5, 0:384]).then_inc(sem("weights_made"), 1)
            nc.scalar.copy(cols[:, 0:3 * C], PS[:, 6, 0:3 * C]).then_inc(sem("weights_made"), 1)
            nc.scalar.copy(cols[:, 3 * C:], PS[:, 6, 3 * C:3 * C + NE0 + NE1 * NH1]).then_inc(sem("weights_made"), 1)

            def channel_major(stage, scale=None):
                for k in range(8):
                    act.wait_ge(sem(f"{stage}_turned"), k + 1)
                    src = PS[0:C, 6 + k % 2, :]
                    dst = xc[:, 512 * k:512 * (k + 1)]
                    if scale is None:
                        ins = nc.scalar.copy(dst, src)
                    else:
                        ins = nc.scalar.activation(dst, src, ACT.Copy, scale=scale)
                    ins.then_inc(sem(f"{stage}_xc"), 1)

            def pixel_softmax(L, G):
                for u in range(NQ * G):
                    q, g = u // G, u % G
                    act.wait_ge(sem(f"{L}_kmax"), u + 1)
                    if u >= 2:
                        act.wait_ge(sem(f"{L}_kturned"), u - 1)
                    for b in range(QB):
                        bank = 2 * (u % 2) + b // 2
                        nc.scalar.activation(ek[:, u % 2, HW * b:HW * (b + 1)], PS[:, bank, HW * (b % 2):HW * (b % 2 + 1)],
                                             ACT.Exp, bias=nmx[:, u, b:b + 1],
                                             accum_out=ksum[:, g, QB * q + b:QB * q + b + 1]).then_inc(sem(f"{L}_kexp"), 1)
                    if u >= 1:
                        second_half(L, u - 1)
                second_half(L, NQ * G - 1)

            def second_half(L, u):
                act.wait_ge(sem(f"{L}_kturned"), u + 1)
                if u >= 2:
                    act.wait_ge(sem(f"{L}_ymade"), u - 1)
                nc.scalar.copy(ekt[:, u % 2, 4:8, :], PS[:, 5, :].rearrange("p (t n) -> p t n", n=P))\
                    .then_inc(sem(f"{L}_ekt_a"), 1)

            channel_major("ln0")
            pixel_softmax("c0", 2)
            for h in range(2):
                act.wait_ge(sem("c0_mmade"), h + 1)
                nc.scalar.copy(MT[:, 8 * h:8 * (h + 1), :], PS[0:C, 6 + h, :].rearrange("p (b n) -> p b n", n=C))\
                    .then_inc(sem("c0_mt"), 1)
            channel_major("ln1")

            for k in range(2):
                act.wait_ge(sem("node_scores"), k + 1)
                nc.scalar.activation(nod[:, 2 + k, :, :], nod[:, k, :, :], ACT.Exp).then_inc(sem("node_exps"), 1)

            def experts0(n):
                for e in range(NE0):
                    m = NE0 * n + e
                    act.wait_ge(sem("h0_made"), m + 1)
                    if n >= 1:
                        act.wait_ge(sem("o0_made"), 2 * n)
                    nc.scalar.activation(hid0[:, e, :], PS[:, 3 + m % 2, :], ACT.Gelu,
                                         bias=b1c0[:, e:e + 1]).then_inc(sem("h0_gelu"), 1)

            for n in range(8):
                experts0(n)

            def edge_exps(it):
                for a in range(2):
                    act.wait_ge(sem(f"edge_scores{a}"), it + 1)
                    act.wait_ge(sem("const0"), 3)
                    nc.scalar.activation(val[:, a, :, F0:FV], es[:, a, 2, :, :], ACT.Exp).then_inc(sem(f"edge_exps{a}"), 1)

            with nc.scalar.Fori(0, ITERS) as t:
                edge_exps(t)
            act.wait_ge(sem("flag_made"), 1)
            left = nc.scalar.value_load(flagi[0:1, 0:1], min_val=0, max_val=1)
            with nc.scalar.If(left > 0):
                with nc.scalar.Fori(0, REST) as g:
                    with nc.scalar.Fori(0, ITERS) as t:
                        edge_exps((g + 1) * ITERS + t)

            act.wait_ge(sem("gate_in0"), 1)
            nc.scalar.activation(sc[:, 2, :, 0:NE0], sc[:, 1, :, 0:NE0], ACT.Exp).then_inc(sem("gate_exp0"), 1)

            channel_major("ln2", gn1[:, 0:1])
            for u in range(8):
                act.wait_ge(sem("q_shifted"), u + 1)
                nc.scalar.activation(qe(u), qe(u), ACT.Exp).then_inc(sem("q_exp"), 1)
                act.wait_ge(sem("q_turned"), u + 1)
                nc.scalar.copy(qc[:, 512 * u:512 * (u + 1)], PS[:, 2 + u % 2, :]).then_inc(sem("qc_made"), 1)
            pixel_softmax("c1", 1)
            channel_major("ln4")
            act.wait_ge(sem("gate_in1"), 1)
            nc.scalar.activation(sc[:, 2, :, :], sc[:, 1, :, :], ACT.Exp).then_inc(sem("gate_exp1"), 1)
            for n in range(8):
                for k in range(NE1 * NH1):
                    m = NE1 * NH1 * n + k
                    act.wait_ge(sem("h1_made"), m + 1)
                    if n >= 2:
                        act.wait_ge(sem("o1_made"), 4 * (n - 1))
                    nc.scalar.activation(hid1[n % 2][:, k, :], PS[:, m % 4, :], ACT.Gelu,
                                         bias=b1c1[:, k:k + 1]).then_inc(sem("h1_gelu"), 1)
            for k in range(8):
                act.wait_ge(sem("y_turned"), k + 1)
                nc.scalar.copy(xc[:, 512 * k:512 * (k + 1)], PS[0:C, k % 2, :]).then_inc(sem("yc_made"), 1)

        @block.tensor
        def _(pe):
            mm, tr = nc.tensor.matmul, nc.tensor.transpose
            pe.wait_ge(sem("ident_made"), 1)
            pe.wait_ge(sem("x_in"), 16)
            for q in range(NQ):
                if q >= 2:
                    pe.wait_ge(sem("xt_made"), q - 1)
                for i in range(QT):
                    t = QT * q + i
                    ins = tr(PS[:, q % 2, C * i:C * (i + 1)], xc[:, P * t:P * (t + 1)], ident[0:C, 0:C])
                ins.then_inc(sem("xt_turned"), 1)
            pe.wait_ge(sem("conv_weights_in"), 128)
            for g in range(4):
                ins = tr(PS[0:C, 4, P * g:P * (g + 1)], wkv0[:, g, :], ident[:, :])
            ins.then_inc(sem("weights_turned"), 1)
            for g in range(3):
                ins = tr(PS[0:C, 5, P * g:P * (g + 1)], wqkv1[:, g, :], ident[:, :])
            ins.then_inc(sem("weights_turned"), 1)
            for g in range(2):
                tr(PS[:, 6, C * g:C * (g + 1)], wo0[:, P * g:P * (g + 1)], ident[0:C, 0:C])
            tr(PS[:, 6, 2 * C:3 * C], wo1[:, :], ident[0:C, 0:C])
            tr(PS[:, 6, 3 * C:3 * C + NE0], b1r0[:, :], ident[0:NE0, 0:NE0])
            n1 = NE1 * NH1
            tr(PS[:, 6, 3 * C + NE0:3 * C + NE0 + n1], b1r1[:, :], ident[0:n1, 0:n1]).then_inc(sem("weights_turned"), 1)

            def channel_major(stage, first):
                for k in range(8):
                    pe.wait_ge(sem(f"{stage}_xn"), k // 2 + 1)
                    if k >= 2:
                        pe.wait_ge(sem(f"{stage}_xc"), k - 1)
                    elif k == 0:
                        first()
                    for i in range(4):
                        ins = tr(PS[0:C, 6 + k % 2, P * i:P * (i + 1)], xn[:, 4 * k + i, :], ident[:, :])
                    ins.then_inc(sem(f"{stage}_turned"), 1)

            def keys_of(L, G, wk, stage, u):
                q, g = u // G, u % G
                pe.wait_ge(sem(f"{stage}_xc"), 2 * q + 2)
                if u >= 2:
                    pe.wait_ge(sem(f"{L}_kexp"), QB * (u - 1))
                for h in range(2):
                    ins = mm(PS[:, 2 * (u % 2) + h, :], wk(g), xc[:, 1024 * q + 512 * h:1024 * q + 512 * (h + 1)],
                             start=True, stop=True)
                ins.then_inc(sem(f"{L}_kmade"), 1)

            def context_of(L, G, u):
                q, g = u // G, u % G
                pe.wait_ge(sem(f"{L}_kexp"), QB * (u + 1))
                if u >= 1:
                    pe.wait_ge(sem(f"{L}_ekt_a"), u)
                    pe.wait_ge(sem(f"{L}_ekt_v"), u)
                for i in range(QT):
                    ins = tr(PS[:, 4 + i // 4, P * (i % 4):P * (i % 4 + 1)], ek[:, u % 2, P * i:P * (i + 1)], ident[:, :])
                ins.then_inc(sem(f"{L}_kturned"), 1)
                pe.wait_ge(sem(f"{L}_ekt_a"), u + 1)
                pe.wait_ge(sem(f"{L}_ekt_v"), u + 1)
                if u >= 1:
                    pe.wait_ge(sem(f"{L}_yv"), u)
                for b in range(QB):
                    for s in range(2):
                        ins = mm(PS[0:C, 6, P * b:P * (b + 1)], xn[:, QT * q + 2 * b + s, :], ekt[:, u % 2, 2 * b + s, :],
                                 start=(s == 0), stop=(s == 1))
                ins.then_inc(sem(f"{L}_ymade"), 1)

            def attention(L, G, wk, wv, wo, stage):
                for u in range(NQ * G):
                    keys_of(L, G, wk, stage, u)
                    if u >= 1:
                        context_of(L, G, u - 1)
                context_of(L, G, NQ * G - 1)
                for c in range(NQ * G + 1):
                    g, q = c // NQ, c % NQ
                    if c < NQ * G:
                        pe.wait_ge(sem(f"{L}_yv"), NQ * G)
                        if c >= 2:
                            pe.wait_ge(sem(f"{L}_ctx"), c - 1)
                        mm(PS[:, 6 + c % 2, :], wv(g), Ys[L == "c1"][:, g, QB * q:QB * (q + 1), :].rearrange("c b n -> c (b n)"),
                           start=True, stop=True).then_inc(sem(f"{L}_cmade"), 1)
                    if c >= 1:
                        g, q = (c - 1) // NQ, (c - 1) % NQ
                        pe.wait_ge(sem(f"{L}_ctx"), c)
                        if c >= 3:
                            pe.wait_ge(sem(f"{L}_t"), c - 2)
                        for b in range(QB):
                            ins = mm(PS[:, 4 + (c - 1) % 2, C * b:C * (b + 1)], ctxT[:, g, QB * q + b, :], wo[:, g, :],
                                     start=True, stop=True)
                        ins.then_inc(sem(f"{L}_tmade"), 1)

            def after_weights():
                pe.wait_ge(sem("weights_made"), 4)

            channel_major("ln0", after_weights)
            attention("c0", 2, lambda g: wkvT0[:, P * g:P * (g + 1)], lambda g: wkvT0[:, 256 + P * g:256 + P * (g + 1)],
                      woT0, "ln0")
            pe.wait_ge(sem("c0_t"), 8)
            pe.wait_ge(sem("c0_ctx"), 8)
            for h in range(2):
                for g in range(2):
                    ins = mm(PS[0:C, 6 + h, :], wq0[:, g, :], T[:, g, 8 * h:8 * (h + 1), :].rearrange("p b n -> p (b n)"),
                             start=(g == 0), stop=(g == 1))
                ins.then_inc(sem("c0_mmade"), 1)
            pe.wait_ge(sem("c0_mt"), 2)
            for q in range(NQ):
                for i in range(QT):
                    t = QT * q + i
                    ins = mm(PS[:, q, C * i:C * (i + 1)], xc[:, P * t:P * (t + 1)], MT[:, t // 2, :], start=True, stop=True)
                ins.then_inc(sem("c0_out"), 1)

            channel_major("ln1", lambda: None)
            pe.wait_ge(sem("ln1_xc"), 8)
            pe.wait_ge(sem("wgat_made"), 2)
            pe.wait_ge(sem("ln1_sum"), NQ)
            W24 = FS + HEADS
            for t in range(NT):
                ins = mm(PS[:, t // 16, W24 * (t % 16):W24 * (t % 16 + 1)], xc[:, P * t:P * (t + 1)], wgat[:, :],
                         start=True, stop=True)
            ins.then_inc(sem("tables_turned"), 1)

            def hidden0(n):
                for e in range(NE0):
                    m = NE0 * n + e
                    if m >= 2:
                        pe.wait_ge(sem("h0_gelu"), m - 1)
                    mm(PS[:, 3 + m % 2, :], w1_0[:, e, :], xc[:, 512 * n:512 * (n + 1)],
                       start=True, stop=True).then_inc(sem("h0_made"), 1)

            def second0(n):
                pe.wait_ge(sem("h0_gelu"), NE0 * (n + 1))
                for i in range(4):
                    k = 2 * n + i // 2
                    if i % 2 == 0 and k >= 2:
                        pe.wait_ge(sem("oute_made"), k - 1)
                    for e in range(NE0):
                        ins = mm(PS[:, 5 + k % 2, 256 * (i % 2) + C * e:256 * (i % 2) + C * (e + 1)],
                                 hid0[:, e, P * i:P * (i + 1)], w2_0[:, e, :], start=True, stop=True)
                    if i % 2 == 1:
                        ins.then_inc(sem("o0_made"), 1)

            pe.wait_ge(sem("ffn0_weights_in"), 144)
            for n in range(8):
                hidden0(n)
                second0(n)

            pe.wait_ge(sem("zeros_made"), 2)
            pe.wait_ge(sem("tables_made"), 1)
            pe.wait_ge(sem("prod_zero"), 1)
            for k in range(2):
                mm(PS[:, k, 0:FH * LO], zeros[:, :], prod[:, 0, 0, 0:FH, :], start=True, stop=False)
            mm(PS[:, 2, 0:LO], zeros[:, :], zeros[:, 0:LO], start=True, stop=False).then_inc(sem("sums_cleared"), 1)
            for name in ("prod_used0", "prod_used1", "hist_used0", "hist_used1"):
                mm(PS[:, 7, 0:P], zeros[:, :], zeros[:, :], start=True, stop=True).then_inc(sem(name), 1)

            def scatter(it, with_hist):
                for a in range(2):
                    pe.wait_ge(sem(f"prod_made{a}"), it + 1)
                    pe.wait_ge(sem("const0"), 3)
                    for j in range(EB):
                        for k in range(2):
                            ins = mm(PS[:, k, 0:FH * LO], one_hi[:, a, j, :], prod[:, a, j, FH * k:FH * (k + 1), :],
                                     start=False, stop=False, skip_group_check=True)
                    ins.then_inc(sem(f"prod_used{a}"), 1)
                    if with_hist:
                        for h in range(HB // 2):
                            k = a * (HB // 2) + h
                            pe.wait_ge(sem(f"hist_made{k % 2}"), 2 * ((HB // 2) * it + k // 2 + 1))
                            pe.wait_ge(sem("const0"), 3)
                            for c in range(HC):
                                ins = mm(PS[:, 2, 0:LO], hist_hi[k % 2][:, :, c], hist_lo[k % 2][:, :, c],
                                         start=False, stop=False, skip_group_check=True)
                            ins.then_inc(sem(f"hist_used{k % 2}"), 1)

            with nc.tensor.Fori(0, ITERS) as t:
                scatter(t, True)
            pe.wait_ge(sem("flag_made"), 1)
            left = nc.tensor.value_load(flagi[0:1, 0:1], min_val=0, max_val=1)
            with nc.tensor.If(left > 0):
                with nc.tensor.Fori(0, REST) as g:
                    with nc.tensor.Fori(0, ITERS) as t:
                        scatter((g + 1) * ITERS + t, False)
            for k in range(2):
                mm(PS[:, k, 0:FH * LO], zeros[:, :], prod[:, 0, 0, 0:FH, :], start=False, stop=True)
            mm(PS[:, 2, 0:LO], zeros[:, :], zeros[:, 0:LO], start=False, stop=True)\
                .then_inc(sem("sums_made"), 1)

            channel_major("ln2", lambda: None)
            for u in range(8 + 1):
                if u < 8:
                    pe.wait_ge(sem("ln2_xc"), u + 1)
                    if u >= 2:
                        pe.wait_ge(sem("q_shifted"), u - 1)
                    for i in range(4):
                        t = 4 * u + i
                        ins = mm(PS[:, u % 2, P * i:P * (i + 1)], xc[:, P * t:P * (t + 1)], wqkvT1[:, 0:P],
                                 start=True, stop=True)
                    ins.then_inc(sem("q_made"), 1)
                if u >= 1:
                    v = u - 1
                    pe.wait_ge(sem("q_soft"), v + 1)
                    if v >= 2:
                        pe.wait_ge(sem("qc_made"), v - 1)
                    for i in range(4):
                        ins = tr(PS[:, 2 + v % 2, P * i:P * (i + 1)],
                                 qe(v)[:, 4 * i:4 * (i + 1), :].rearrange("p k d -> p (k d)"), ident[:, :])
                    ins.then_inc(sem("q_turned"), 1)
            pe.wait_ge(sem("qc_made"), 8)
            attention("c1", 1, lambda g: wqkvT1[:, P:2 * P], lambda g: wqkvT1[:, 2 * P:3 * P], woT1, "ln2")
            pe.wait_ge(sem("c1_t"), 4)
            for q in range(NQ):
                for i in range(QT):
                    t = QT * q + i
                    ins = mm(PS[:, q, C * i:C * (i + 1)], qc[:, P * t:P * (t + 1)], T[:, 0, t // 2, :], start=True, stop=True)
                ins.then_inc(sem("c1_out"), 1)

            channel_major("ln4", lambda: None)
            pe.wait_ge(sem("ln4_xc"), 8)
            pe.wait_ge(sem("ln4_sum"), NQ)
            for t in range(NT):
                ins = mm(PS[:, 7, NE1 * t:NE1 * (t + 1)], xc[:, P * t:P * (t + 1)], wg[:, :], start=True, stop=True)
            ins.then_inc(sem("logits_made"), 1)
            pe.wait_ge(sem("logits_read"), 1)
            pe.wait_ge(sem("experts1_in"), 32)

            def hidden1(n):
                for k in range(NE1 * NH1):
                    m = NE1 * NH1 * n + k
                    if m >= 4:
                        pe.wait_ge(sem("h1_gelu"), m - 3)
                    mm(PS[:, m % 4, :], w1_1[:, k // NH1, P * (k % NH1):P * (k % NH1 + 1)], xc[:, 512 * n:512 * (n + 1)],
                       start=True, stop=True).then_inc(sem("h1_made"), 1)

            def second1(n):
                pe.wait_ge(sem("h1_gelu"), NE1 * NH1 * (n + 1))
                for i in range(4):
                    m = 4 * n + i
                    if m >= 4:
                        pe.wait_ge(sem("o1_gated"), m - 3)
                    for e in range(NE1):
                        for k in range(NH1):
                            ins = mm(PS[:, 4 + m % 4, C * e:C * (e + 1)], hid1[n % 2][:, NH1 * e + k, P * i:P * (i + 1)],
                                     w2_1[:, e, k, :], start=(k == 0), stop=(k == NH1 - 1))
                    ins.then_inc(sem("o1_made"), 1)

            hidden1(0)
            for n in range(8):
                if n < 7:
                    hidden1(n + 1)
                second1(n)
            for k in range(8):
                pe.wait_ge(sem("y_made"), k + 1)
                if k >= 2:
                    pe.wait_ge(sem("yc_made"), k - 1)
                for i in range(4):
                    ins = tr(PS[0:C, k % 2, P * i:P * (i + 1)], xt[:, 4 * k + i, :], ident[:, :])
                ins.then_inc(sem("y_turned"), 1)

        @block.vector
        def _(dve):
            V = nc.vector
            steps = [0]

            def then(ins):
                steps[0] += 1
                ins.then_inc(sem("dve_steps"), 1)
                dve.wait_ge(sem("dve_steps"), steps[0])

            for g in range(4):
                s = slice(32 * g, 32 * g + 32)
                if g == 0:
                    then(V.memset(blocks[:, :], 0.0))
                ins = V.memset(blocks[s, s], 1.0)
            then(ins)
            dve.wait_ge(sem("const0"), 3)
            then(V.tensor_copy(iota[:, :], iota_i[:, :]))
            V.tensor_copy(iota_h[:, :, :], bc(iota[:, :], 2, HC)).then_inc(sem("iota_made"), 1)

            dve.wait_ge(sem("edges_in"), 16)
            srcf, dstf, live, key2 = (etmp[:, k, :] for k in range(4))
            V.tensor_copy(srcf, ebi[:, 0, :])
            then(V.tensor_copy(dstf, ebi[:, 1, :]))
            V.tensor_scalar(live, srcf, float(NODES - 1) - 0.5, None, ALU.is_lt)
            then(V.scalar_tensor_tensor(out=key2, in0=srcf, scalar=float(NODES), in1=dstf, op0=ALU.mult, op1=ALU.add))
            then(V.scalar_tensor_tensor(out=srcf, in0=dstf, scalar=float(NODES) - 0.5, in1=live, op0=ALU.is_lt,
                                        op1=ALU.mult))
            then(V.scalar_tensor_tensor(out=rows, in0=key2, scalar=1.0, in1=srcf, op0=ALU.add, op1=ALU.mult))
            V.tensor_scalar(ebi[:, 0, :], ebi[:, 1, :], P - 1, None, ALU.bitwise_and)
            then(V.tensor_scalar(key2.bitcast(I32), ebi[:, 1, :], 7, None, ALU.logical_shift_right))
            V.scalar_tensor_tensor(out=dhi_h[:, :], in0=live, scalar=256.0, in1=ebi[:, 0, :], op0=ALU.mult, op1=ALU.add)
            then(V.tensor_copy(dlo_h[:, :], key2.bitcast(I32)))

            with V.Fori(0, ROUNDS) as r:
                for s in range(SEGS):
                    V.max(m8[:, s, :], rows[:, SEG * s:SEG * (s + 1)]).then_inc(sem("top_found"), 1)
                dve.wait_ge(sem("top_found"), r * SEGS + SEGS)
                V.tensor_scalar(keys[:, bass.ds(r * (SEGS * TOP), SEGS * TOP)],
                                m8[:, :, :].rearrange("p s k -> p (s k)"), 0.0, None, ALU.add)\
                    .then_inc(sem("top_kept"), 1)
                for s in range(SEGS):
                    seg = rows[:, SEG * s:SEG * (s + 1)]
                    V.match_replace(seg, m8[:, s, :], seg, 0.0).then_inc(sem("top_removed"), 1)
                dve.wait_ge(sem("top_kept"), r + 1)
                dve.wait_ge(sem("top_removed"), r * SEGS + SEGS)
            V.tensor_reduce(flagf[:, 0:1], rows, X, ALU.max).then_inc(sem("rest_max"), 1)

            def decode(col):
                k0 = keys[:, bass.ds(col, GC)]
                k = dec[:, 0, :]
                ki, hi_i, lo_i = deci[:, 0, :], deci[:, 1, :], deci[:, 2, :]
                yield V.tensor_scalar(dec[:, 1, :], k0, 0.5, None, ALU.is_gt)
                yield V.tensor_scalar(ki, k0, -1.0, 0.0, ALU.add, ALU.max)
                yield V.tensor_scalar(idx_s[:, :], ki, 12, None, ALU.logical_shift_right)
                yield V.tensor_scalar(idx_d[:, :], ki, NODES - 1, None, ALU.bitwise_and)
                yield V.tensor_scalar(hi_i, idx_d[:, :], P - 1, None, ALU.bitwise_and)
                yield V.tensor_scalar(lo_i, idx_d[:, :], 7, None, ALU.logical_shift_right)
                yield V.scalar_tensor_tensor(out=k, in0=hi_i, scalar=1.0, in1=dec[:, 1, :], op0=ALU.add, op1=ALU.mult)
                yield V.tensor_scalar(dhi[:, :], k, -1.0, None, ALU.add)
                yield V.tensor_copy(dlo[:, :], lo_i)

            DECODE_STEPS = 8
            for n, ins in enumerate(decode(0)):
                if n < DECODE_STEPS:
                    then(ins)
            ins.then_inc(sem("decoded"), 1)

            def sums(q, src):
                T8 = slice(QT * q, QT * (q + 1))
                then(V.tensor_reduce(red[:, 0, T8], src[:, T8, :], X, ALU.add))
                then(V.tensor_scalar(red[:, 1, T8], red[:, 0, T8], -1.0 / C, None, ALU.mult))
                then(V.tensor_tensor(xn[:, T8, :], src[:, T8, :], bc(red[:, 1, T8], 2, C), ALU.add))

            def squares(q, src, stage, scale, eps):
                T8 = slice(QT * q, QT * (q + 1))
                then(V.tensor_tensor(sq[:, T8, :], src[:, T8, :], src[:, T8, :], ALU.mult))
                then(V.tensor_reduce(red[:, 0, T8], sq[:, T8, :], X, ALU.add))
                V.tensor_scalar(red[:, 2, T8], red[:, 0, T8], scale, eps, ALU.mult, ALU.add)\
                    .then_inc(sem(f"{stage}_var"), 1)

            def scaled(q, stage, signal):
                T8 = slice(QT * q, QT * (q + 1))
                dve.wait_ge(sem(f"{stage}_rstd"), q + 1)
                V.tensor_tensor(xn[:, T8, :], xn[:, T8, :], bc(red[:, 3, T8], 2, C), ALU.mult)\
                    .then_inc(sem(signal), 1)

            def layer_norm(stage, eps, ready, signal=None):
                for q in range(NQ):
                    ready(q)
                    sums(q, xt)
                    squares(q, xn, stage, 1.0 / C, eps)
                for q in range(NQ):
                    scaled(q, stage, signal or f"{stage}_xn")

            layer_norm("ln0", LN_C_EPS, lambda q: dve.wait_ge(sem("xt_made"), q + 1))
            dve.wait_ge(sem("rest_all"), 1)
            V.tensor_scalar(flagi[:, :], flagf[:, 1:2], 0.5, None, ALU.is_gt).then_inc(sem("flag_made"), 1)

            def pixel_attention(L, G, yscale):
                for u in range(NQ * G + 1):
                    if u < NQ * G:
                        dve.wait_ge(sem(f"{L}_kmade"), u + 1)
                        V.tensor_reduce(nmx[:, u, :], PS[:, 2 * (u % 2):2 * (u % 2) + 2, :]
                                        .rearrange("p a (b n) -> p (a b) n", n=HW), X, ALU.max,
                                        negate=True).then_inc(sem(f"{L}_kmax"), 1)
                    if u >= 1:
                        v = u - 1
                        q, g = v // G, v % G
                        dve.wait_ge(sem(f"{L}_kturned"), v + 1)
                        if v >= 2:
                            dve.wait_ge(sem(f"{L}_ymade"), v - 1)
                        V.tensor_copy(ekt[:, v % 2, 0:4, :], PS[:, 4, :].rearrange("p (t n) -> p t n", n=P))\
                            .then_inc(sem(f"{L}_ekt_v"), 1)
                        dve.wait_ge(sem(f"{L}_ymade"), v + 1)
                        dst = Ys[L == "c1"][:, g, QB * q:QB * (q + 1), :]
                        src = PS[0:C, 6, :].rearrange("p (b n) -> p b n", n=P)
                        V.tensor_scalar(dst, src, 1.0 if yscale is None else yscale, None, ALU.mult)\
                            .then_inc(sem(f"{L}_yv"), 1)
                dve.wait_ge(sem(f"{L}_kexp"), QB * NQ * G)
                then(V.reciprocal(rks[:, 0:G, :], ksum[:, 0:G, :]))
                if G == 1:
                    then(V.tensor_scalar(rks[:, 0, :], rks[:, 0, :], HEAD_DIM ** -0.5, None, ALU.mult))
                for c in range(NQ * G + 1):
                    if c < NQ * G:
                        g, q = c // NQ, c % NQ
                        dve.wait_ge(sem(f"{L}_cmade"), c + 1)
                        V.tensor_tensor(ctxT[:, g, QB * q:QB * (q + 1), :],
                                        PS[:, 6 + c % 2, :].rearrange("p (b n) -> p b n", n=P), bc(blocks[:, :], 1, QB),
                                        ALU.mult).then_inc(sem(f"{L}_ctx"), 1)
                    if c >= 1:
                        g, q = (c - 1) // NQ, (c - 1) % NQ
                        dve.wait_ge(sem(f"{L}_tmade"), c)
                        V.tensor_tensor(T[:, g, QB * q:QB * (q + 1), :],
                                        PS[:, 4 + (c - 1) % 2, 0:QB * C].rearrange("p (b n) -> p b n", n=C),
                                        bc(rks[:, g, QB * q:QB * (q + 1)], 2, C), ALU.mult).then_inc(sem(f"{L}_t"), 1)

            pixel_attention("c0", 2, None)
            dve.wait_ge(sem("conv_weights_in"), 128)
            then(V.tensor_tensor(xt[:, :, :], xt[:, :, :], bc(bo0[:, :], 1, NT), ALU.add))

            def add_attention(q):
                dve.wait_ge(sem("c0_out"), q + 1)
                T8 = slice(QT * q, QT * (q + 1))
                then(V.tensor_tensor(xt[:, T8, :], xt[:, T8, :], PS[:, q, :].rearrange("p (t c) -> p t c", c=C), ALU.add))

            dve.wait_ge(sem("ffn0_weights_in"), 144)
            then(V.tensor_tensor(attm[:, :, :], attr[:, :, :], bc(wgat[:, HEADS:FS], 1, 2), ALU.mult))
            for k, c in ((0, 0), (1, FS)):
                V.tensor_reduce(wgat[:, c:c + HEADS], attm[:, k, :].rearrange("p (h e) -> p h e", e=NE0), X, ALU.add)\
                    .then_inc(sem("wgat_made"), 1)
            layer_norm("ln1", LN_T_EPS, add_attention)
            V.memset(val[:, :, :, :], 0.0).then_inc(sem("ln1_sum"), NQ)

            dve.wait_ge(sem("tables_turned"), 1)
            W24 = FS + HEADS
            for k in range(2):
                src = PS[:, k, 0:16 * W24].rearrange("p (t f) -> p t f", f=W24)
                V.tensor_copy(tab_s[:, 16 * k:16 * (k + 1), :], src[:, :, 0:FS])
                ins = V.tensor_copy(tab_d[:, 16 * k:16 * (k + 1), 0:HEADS], src[:, :, FS:W24])
            then(ins)
            V.tensor_reduce(gmax[:, 0, :], tab_s[:, :, 0:HEADS].rearrange("p t h -> p h t"), X, ALU.max)\
                .then_inc(sem("score_max"), 1)

            dve.wait_ge(sem("score_all"), 1)
            then(V.tensor_tensor(nod[:, 4, :, :], tab_d[:, :, 0:HEADS], bc(gmax[:, 1, :], 1, NT), ALU.add))
            V.scalar_tensor_tensor(out=tab_d[:, :, HEADS:FD], in0=nod[:, 4, :, :], scalar=SLOPE, in1=nod[:, 4, :, :],
                                   op0=ALU.mult, op1=ALU.max).then_inc(sem("tables_made"), 1)
            dve.wait_ge(sem("tables_made"), 1)
            ad, guard = tab_d[:, :, 0:HEADS], tab_d[:, :, HEADS:FD]
            for k in range(2):
                if k:
                    dve.wait_ge(sem("last_in"), 16)
                a = tab_s[:, :, 0:HEADS] if k == 0 else bc(last[:, 0:HEADS], 1, NT)
                st = list(leaky_steps(V, nod[:, k, :, :], nod[:, 4, :, :], a, ad, guard))
                for n, f in enumerate(st):
                    ins = f()
                    if n < 2:
                        then(ins)
                    else:
                        ins.then_inc(sem("node_scores"), 1)
                dve.wait_ge(sem("node_scores"), k + 1)

            V.memset(prod[:, :, :, :, :], 0.0).then_inc(sem("prod_zero"), 1)
            for k in range(16):
                dve.wait_ge(sem("o0_made"), k + 1)
                V.tensor_tensor(oute[:, 2 * k:2 * k + 2, :, :].rearrange("p t e c -> p t (e c)"),
                                PS[:, 5 + k % 2, :].rearrange("p (t n) -> p t n", t=2), bc(b2b0[:, :], 1, 2), ALU.add)\
                    .then_inc(sem("oute_made"), 1)

            for a in range(2):
                V.memset(gs[:, a, :, :], 0.0).then_inc(sem("dve_edge"), 1)
                V.memset(gd[:, a, :, :], 0.0).then_inc(sem(f"rows_used{a}"), 1)
            dve.wait_ge(sem("dve_edge"), 2)
            dve.wait_ge(sem("decoded"), 1)
            dve.wait_ge(sem("sums_cleared"), 1)

            EDGE_STEPS = 8

            def edge_block(it, t, with_hist):
                n = [0]

                def step(ins):
                    n[0] += 1
                    ins.then_inc(sem("dve_edge"), 1)

                def settle():
                    dve.wait_ge(sem("dve_edge"), it * EDGE_STEPS + (n[0] + 2))

                for a in range(2):
                    dve.wait_ge(sem(f"rows_in{a}"), it * (32 * EB) + 32 * EB)
                    dve.wait_ge(sem("const0"), 3)
                    e1, e2, e3 = (es[:, a, k, :, :] for k in range(3))
                    step(V.tensor_tensor(e1, gs[:, a, :, 0:HEADS], gd[:, a, :, 0:HEADS], ALU.add))
                    settle()
                    step(V.scalar_tensor_tensor(out=e2, in0=e1, scalar=SLOPE, in1=e1, op0=ALU.mult, op1=ALU.max))
                    settle()
                    V.tensor_tensor(e3, e2, gd[:, a, :, HEADS:FD], ALU.subtract).then_inc(sem(f"edge_scores{a}"), 1)
                for a in range(2):
                    dve.wait_ge(sem(f"prod_used{a}"), it + 1)
                    c0 = t * ITC + a * EB
                    step(V.tensor_tensor(one_hi[:, a, :, :], bc(dhi[:, bass.ds(c0, EB)], 2, P), bc(iota[:, :], 1, EB),
                                         ALU.is_equal))
                    step(V.tensor_tensor(one_lo[:, a, :, :], bc(dlo[:, bass.ds(c0, EB)], 2, LO),
                                         bc(iota[:, 0:LO], 1, EB), ALU.is_equal))
                    dve.wait_ge(sem(f"edge_exps{a}"), it + 1)
                    v = val[:, a, :, :]
                    V.tensor_tensor(v[:, :, 0:F0].rearrange("p j (h e) -> p j h e", e=NE0),
                                    gs[:, a, :, HEADS:FS].rearrange("p j (h e) -> p j h e", e=NE0),
                                    bc(v[:, :, F0:FV], 3, NE0), ALU.mult).then_inc(sem(f"rows_used{a}"), 1)
                    settle()
                    dve.wait_ge(sem(f"rows_used{a}"), it + 2)
                    V.tensor_tensor(prod[:, a, :, :, :], bc(one_lo[:, a, :, :], 2, FV), bc(v, 3, LO), ALU.mult)\
                        .then_inc(sem(f"prod_made{a}"), 1)
                    if with_hist:
                        for h in range(HB // 2):
                            k = a * (HB // 2) + h
                            dve.wait_ge(sem(f"hist_used{k % 2}"), (HB // 2) * it + k // 2 + 1)
                            c = t * (HB * HC) + k * HC
                            V.tensor_tensor(hist_hi[k % 2], bc(dhi_h[:, bass.ds(c, HC)], 1, P), iota_h[:, :, :],
                                            ALU.is_equal).then_inc(sem(f"hist_made{k % 2}"), 1)
                            V.tensor_tensor(hist_lo[k % 2], bc(dlo_h[:, bass.ds(c, HC)], 1, LO), iota_h[:, 0:LO, :],
                                            ALU.is_equal).then_inc(sem(f"hist_made{k % 2}"), 1)
                assert n[0] == EDGE_STEPS

            with V.Fori(0, ITERS) as t:
                edge_block(t, t, True)
            left = V.value_load(flagi[0:1, 0:1], min_val=0, max_val=1)
            with V.If(left > 0):
                with V.Fori(0, REST) as g:
                    for n, ins in enumerate(decode(GC + g * GC)):
                        if n < DECODE_STEPS:
                            ins.then_inc(sem("rest_steps"), 1)
                            dve.wait_ge(sem("rest_steps"), g * DECODE_STEPS + (n + 1))
                    ins.then_inc(sem("decoded"), 1)
                    dve.wait_ge(sem("decoded"), g + 2)
                    V.sem_inc(sem("decode_seen"), 1)
                    with V.Fori(0, ITERS) as t:
                        edge_block((g + 1) * ITERS + t, t, False)

            dve.wait_ge(sem("node_exps"), 2)
            h_self, h_last = tab_s[:, :, HEADS:FS], last[:, HEADS:FS]

            def by_head(ap):
                return ap.rearrange("p t (h e) -> p t h e", e=NE0)

            dve.wait_ge(sem("sums_made"), 1)
            for k in range(2):
                V.tensor_copy(num[:, 0, :, FH * k:FH * (k + 1)], PS[:, k, 0:FH * LO].rearrange("p (f t) -> p t f", t=LO))
            ins = V.tensor_tensor(nod[:, 3, :, :], nod[:, 3, :, :], bc(PS[:, 2, 0:LO], 2, HEADS), ALU.mult)
            ins.then_inc(sem("sums_read"), 1)
            dve.wait_ge(sem("sums_read"), 1)
            then(V.tensor_tensor(by_head(num[:, 1, :, 0:F0]), by_head(h_self), bc(nod[:, 2, :, :], 3, NE0), ALU.mult))
            then(V.tensor_tensor(num[:, 0, :, 0:F0], num[:, 0, :, 0:F0], num[:, 1, :, 0:F0], ALU.add))
            then(V.tensor_tensor(by_head(num[:, 1, :, 0:F0]), by_head(bc(h_last, 1, NT)), bc(nod[:, 3, :, :], 3, NE0),
                                 ALU.mult))
            then(V.tensor_tensor(num[:, 0, :, 0:F0], num[:, 0, :, 0:F0], num[:, 1, :, 0:F0], ALU.add))
            then(V.tensor_tensor(num[:, 0, :, F0:FV], num[:, 0, :, F0:FV], nod[:, 2, :, :], ALU.add))
            then(V.scalar_tensor_tensor(out=num[:, 0, :, F0:FV], in0=num[:, 0, :, F0:FV], scalar=1e-16,
                                        in1=nod[:, 3, :, :], op0=ALU.add, op1=ALU.add))
            then(V.reciprocal(nod[:, 4, :, :], num[:, 0, :, F0:FV]))
            then(V.tensor_tensor(by_head(num[:, 0, :, 0:F0]), by_head(num[:, 0, :, 0:F0]), bc(nod[:, 4, :, :], 3, NE0),
                                 ALU.mult))
            agg = num[:, 0, :, 0:F0]
            tmp = num[:, 1, :, 0:F0]
            then(V.tensor_tensor(agg, agg, bc(gat_rows[:, 0, :], 1, NT), ALU.add))
            then(V.tensor_reduce(red[:, 0, :], agg, X, ALU.add))
            then(V.tensor_scalar(red[:, 1, :], red[:, 0, :], -1.0 / F0, None, ALU.mult))
            then(V.tensor_tensor(agg, agg, bc(red[:, 1, :], 2, F0), ALU.add))
            then(V.tensor_tensor(tmp, agg, agg, ALU.mult))
            then(V.tensor_reduce(red[:, 0, :], tmp, X, ALU.add))
            V.tensor_scalar(red[:, 2, :], red[:, 0, :], 1.0 / F0, LN_EPS, ALU.mult, ALU.add).then_inc(sem("gat_var"), 1)
            dve.wait_ge(sem("gat_rstd"), 1)
            then(V.tensor_tensor(agg, agg, bc(red[:, 3, :], 2, F0), ALU.mult))
            then(V.tensor_tensor(agg, agg, bc(gat_rows[:, 1, :], 1, NT), ALU.mult))
            then(V.tensor_tensor(agg, agg, bc(gat_rows[:, 2, :], 1, NT), ALU.add))
            then(V.tensor_reduce(sc[:, 0, :, 0:NE0], agg.rearrange("p t (h e) -> p t e h", e=NE0), X, ALU.add))
            then(V.tensor_scalar(sc[:, 0, :, 0:NE0], sc[:, 0, :, 0:NE0], 1.0 / HEADS, None, ALU.mult))

            def gates(n, N, s1, s2):
                s = sc[:, 0, :, 0:N]
                over = s1.rearrange("p (t e j) -> p t e j", e=N, j=N)
                same = s2.rearrange("p (t e j) -> p t e j", e=N, j=N)
                V.tensor_tensor(over, bc(s, 2, N), bc(s, 3, N), ALU.is_gt)
                then(V.tensor_tensor(same, bc(s, 2, N), bc(s, 3, N), ALU.is_equal))
                then(V.tensor_tensor(same, same, bc(before[:, 0:N, 0:N], 1, NT), ALU.mult))
                then(V.tensor_tensor(over, over, same, ALU.add))
                then(V.tensor_reduce(sc[:, 3, :, 0:N], over, X, ALU.add))
                then(V.tensor_reduce(red[:, 4, :], s, X, ALU.max))
                V.tensor_tensor(sc[:, 1, :, 0:N], s, bc(red[:, 4, :], 2, N), ALU.subtract).then_inc(sem(f"gate_in{n}"), 1)
                dve.wait_ge(sem(f"gate_exp{n}"), 1)
                then(V.scalar_tensor_tensor(out=sc[:, 2, :, 0:N], in0=sc[:, 3, :, 0:N], scalar=1.5,
                                            in1=sc[:, 2, :, 0:N], op0=ALU.is_lt, op1=ALU.mult))
                then(V.tensor_reduce(red[:, 5, :], sc[:, 2, :, 0:N], X, ALU.add))
                then(V.reciprocal(red[:, 6, :], red[:, 5, :]))
                V.tensor_tensor(sc[:, 3, :, 0:N], sc[:, 2, :, 0:N], bc(red[:, 6, :], 2, N), ALU.mult)\
                    .then_inc(sem(f"gates{n}"), 1)
                dve.wait_ge(sem(f"gates{n}"), 1)

            dve.wait_ge(sem("before_made"), 1)
            gate_tmp = num[:, :, :, :].rearrange("p a t f -> p (a t f)")
            gates(0, NE0, gate_tmp[:, 0:512], gate_tmp[:, 512:1024])
            then(V.tensor_tensor(oute[:, :, :, :], oute[:, :, :, :], bc(sc[:, 3, :, 0:NE0], 3, C), ALU.mult))
            then(V.tensor_reduce(sq[:, :, :], oute[:, :, :, :].rearrange("p t e c -> p t c e"), X, ALU.add))

            def add_experts(q):
                T8 = slice(QT * q, QT * (q + 1))
                then(V.tensor_tensor(xt[:, T8, :], xt[:, T8, :], sq[:, T8, :], ALU.add))

            dve.wait_ge(sem("layer1_weights_in"), 96)
            then(V.tensor_scalar(gn1[:, :], gn1[:, :], float(C) ** 0.5, None, ALU.mult))
            then(V.tensor_scalar(go1[:, :], go1[:, :], float(C) ** 0.5, None, ALU.mult))
            layer_norm("ln2", LN_C_EPS, add_experts, "ln2_centred")
            for q in range(NQ):
                dve.wait_ge(sem("ln2_centred"), q + 1)
                squares(q, xn, "ln2r", 1.0, RMS_EPS)
            for q in range(NQ):
                scaled(q, "ln2r", "ln2_xn")
            for u in range(8):
                dve.wait_ge(sem("q_made"), u + 1)
                if u >= 4:
                    dve.wait_ge(sem("q_turned"), u - 3)
                src = PS[:, u % 2, :].rearrange("p (k d) -> p k d", d=HEAD_DIM)
                then(V.tensor_reduce(red[:, 4, 0:16], src, X, ALU.max))
                V.tensor_tensor(qe(u), src, bc(red[:, 4, 0:16], 2, HEAD_DIM), ALU.subtract).then_inc(sem("q_shifted"), 1)
                dve.wait_ge(sem("q_exp"), u + 1)
                then(V.tensor_reduce(red[:, 5, 0:16], qe(u), X, ALU.add))
                then(V.reciprocal(red[:, 6, 0:16], red[:, 5, 0:16]))
                V.tensor_tensor(qe(u), qe(u), bc(red[:, 6, 0:16], 2, HEAD_DIM), ALU.mult).then_inc(sem("q_soft"), 1)
            pixel_attention("c1", 1, gn1[:, 0:1])
            for q in range(NQ):
                dve.wait_ge(sem("c1_out"), q + 1)
                T8 = slice(QT * q, QT * (q + 1))
                then(V.tensor_tensor(xn[:, T8, :], PS[:, q, :].rearrange("p (t c) -> p t c", c=C),
                                     bc(bo1[:, :], 1, QT), ALU.add))
                squares(q, xn, "ln3r", 1.0, RMS_EPS)
            for q in range(NQ):
                scaled(q, "ln3r", "z_scaled")

            def add_attention1(q):
                dve.wait_ge(sem("z_scaled"), q + 1)
                T8 = slice(QT * q, QT * (q + 1))
                then(V.tensor_tensor(sq[:, T8, :], xn[:, T8, :], bc(go1[:, :], 1, QT), ALU.mult))
                then(V.tensor_tensor(xt[:, T8, :], xt[:, T8, :], sq[:, T8, :], ALU.add))

            layer_norm("ln4", LN_T_EPS, add_attention1)
            V.memset(flagf[:, 0:1], 0.0).then_inc(sem("ln4_sum"), NQ)

            dve.wait_ge(sem("logits_made"), 1)
            V.tensor_tensor(sc[:, 0, :, :], PS[:, 7, 0:NE1 * NT].rearrange("p (t e) -> p t e", e=NE1),
                            bc(bgb[:, :], 1, NT), ALU.add).then_inc(sem("logits_read"), 1)
            dve.wait_ge(sem("logits_read"), 1)
            gates(1, NE1, ob[:, 0:2048], ob[:, 2048:4096])
            V.memset(flagf[:, 0:1], 0.0).then_inc(sem("xn4_read"), 1)

            for m in range(NT):
                dve.wait_ge(sem("o1_made"), m + 1)
                ot = ob[:, 512 * (m % 4):512 * (m % 4 + 1)].rearrange("p (e c) -> p e c", c=C)
                V.tensor_tensor(ot, PS[:, 4 + m % 4, :].rearrange("p (e c) -> p e c", c=C), bc(sc[:, 3, m, :], 2, C),
                                ALU.mult).then_inc(sem("o1_gated"), 1)
                dve.wait_ge(sem("o1_gated"), m + 1)
                then(V.tensor_reduce(ob[:, 2048 + C * m:2048 + C * (m + 1)], ot.rearrange("p e c -> p c e"), X, ALU.add))
            dve.wait_ge(sem("bias_sum"), NE1 - 1)
            for k in range(8):
                T4 = slice(4 * k, 4 * (k + 1))
                then(V.tensor_tensor(xt[:, T4, :], xt[:, T4, :], xn[:, T4, :], ALU.add))
                V.tensor_tensor(xt[:, T4, :], xt[:, T4, :],
                                ob[:, 2048 + 256 * k:2048 + 256 * (k + 1)].rearrange("p (t c) -> p t c", c=C),
                                ALU.add).then_inc(sem("y_made"), 1)


def leaky_steps(V, dst, tmp, a, b, guard):
    return (lambda: V.tensor_tensor(tmp, a, b, ALU.add),
            lambda: V.scalar_tensor_tensor(out=tmp, in0=tmp, scalar=SLOPE, in1=tmp, op0=ALU.mult, op1=ALU.max),
            lambda: V.tensor_tensor(dst, tmp, guard, ALU.subtract))


_INS = ['x', 'L0_conv_w_qkv', 'L0_conv_w_out', 'L0_conv_b_out', 'L0_ffn_W_gat', 'L0_ffn_att_src', 'L0_ffn_att_dst',
        'L0_ffn_b_gat', 'L0_ffn_ln_gamma', 'L0_ffn_ln_beta', 'L0_ffn_W1', 'L0_ffn_b1', 'L0_ffn_W2', 'L0_ffn_b2',
        'L0_ffn_edge_index', 'L1_conv_W_qkv', 'L1_conv_W_out', 'L1_conv_b_out', 'L1_conv_g_norm', 'L1_conv_g_out',
        'L1_ffn_Wg', 'L1_ffn_bg', 'L1_ffn_W1', 'L1_ffn_b1', 'L1_ffn_W2', 'L1_ffn_b2']


def kernel(**inputs):
    import numpy as _np
    import concourse.bacc as _bacc
    from concourse.bass_utils import run_bass_kernel_spmd as _run

    nc = _bacc.Bacc("TRN2", target_bir_lowering=False, num_devices=1)
    arrays, args = {}, []
    for name in _INS:
        a = _np.ascontiguousarray(inputs[name])
        arrays[f"in_{name}_dram"] = a
        args.append(nc.dram_tensor(f"in_{name}_dram", a.shape, mybir.dt.from_np(a.dtype), kind="ExternalInput").ap())
    out = nc.dram_tensor("out_0_dram", (B, C, 16, 16), F32, kind="ExternalOutput").ap()
    table_s = nc.dram_tensor("table_s_dram", (NODES, FS), F32, kind="Internal").ap()
    table_d = nc.dram_tensor("table_d_dram", (NODES, FD), F32, kind="Internal").ap()
    metaformer(nc, args, table_s, table_d, out)
    r = _run(nc, [arrays], core_ids=[0])
    return r.results[0]["out_0_dram"]
```

```python
from contextlib import ExitStack

import concourse.bass as bass
from concourse import mybir

F32 = mybir.dt.float32
BF16 = mybir.dt.bfloat16
I32 = mybir.dt.int32
ALU = mybir.AluOpType
ACT = mybir.ActivationFunctionType
X = mybir.AxisListType.X
RMAX = bass.bass_isa.ReduceOp.max

P = 128
B, C, HW = 16, 64, 256
NODES = B * HW
NT = NODES // P
QT = 8
NQ = NT // QT
QB = 4
HEADS, NE0 = 4, 4
F0 = HEADS * NE0
HID0 = 128
NE1, HID1 = 8, 256
NH1 = HID1 // P
RING = 8
NEDGE = 262144
EC = NEDGE // P
SEGS, ROUNDS, TOP = 2, 12, 8
SEG = EC // SEGS
GC = SEGS * ROUNDS * TOP
EB = 6
NB = 4
ITC = NB * EB
ITERS = GC // ITC
REST = -(-EC // GC)
HC = 16
HB = EC // HC // ITERS // NB
XT0 = NODES // ITERS
LO = NODES // P
FV = F0 + HEADS
FS = HEADS + F0
FD = 2 * HEADS
FH = FV // 2
HEAD_DIM = 32
LN_C_EPS, LN_T_EPS, LN_EPS, RMS_EPS = 1e-6, 1e-5, 1e-5, 1e-12
SLOPE = 0.2


def metaformer(nc, ins, table_s, table_d, out):
    (x, w_qkv0, w_out0, b_out0, W_gat, att_src, att_dst, b_gat, ln_gamma, ln_beta, W1_0, b1_0, W2_0, b2_0,
     edges, w_qkv1, w_out1, b_out1, g_norm, g_out, Wg, bg, W1_1, b1_1, W2_1, b2_1) = ins

    with ExitStack() as ctx:
        def sb(name, shape, dt=F32):
            return ctx.enter_context(nc.sbuf_tensor(name, shape, dt))

        sems = {}

        def sem(name):
            if name not in sems:
                sems[name] = ctx.enter_context(nc.semaphore(name))
            return sems[name]

        PS = ctx.enter_context(nc.psum_tensor("PS", [P, 8, 512], F32))
        ident = sb("ident", [P, P])
        ident_b = sb("ident_b", [P, P], BF16)
        zeros = sb("zeros", [P, FH * LO])
        ones = sb("ones", [1, P])
        b2row = sb("b2row", [1, NE0 * C])
        iota_i = sb("iota_i", [P, P], I32)
        iota = sb("iota", [P, P])
        iota_h = sb("iota_h", [P, P, HC], BF16)
        blocks = sb("blocks", [P, P])
        before = sb("before", [P, NE1, NE1])
        mhalf = sb("mhalf", [P, NT])
        wkv0 = sb("wkv0", [P, 4, C])
        wq0 = sb("wq0", [P, 2, C])
        wqkv1 = sb("wqkv1", [P, 3, C])
        wo0 = sb("wo0", [C, 256])
        wo1 = sb("wo1", [C, P])
        b1r0 = sb("b1r0", [NE0, P])
        b1r1 = sb("b1r1", [NE1 * NH1, P])
        wkvT0 = sb("wkvT0", [C, 512])
        wqkvT1 = sb("wqkvT1", [C, 384])
        cols = sb("cols", [P, 3 * C + NE0 + NE1 * NH1])
        woT0 = cols[:, 0:2 * C].rearrange("p (g c) -> p g c", g=2)
        woT1 = cols[:, 2 * C:3 * C].rearrange("p (g c) -> p g c", g=1)
        b1c0 = cols[:, 3 * C:3 * C + NE0]
        b1c1 = cols[:, 3 * C + NE0:]
        wgat = sb("wgat", [C, FS + HEADS])
        attr = sb("attr", [C, 2, F0])
        attm = sb("attm", [C, 2, F0])
        w1_0 = sb("w1_0", [C, NE0, HID0])
        w2_0 = sb("w2_0", [HID0, NE0, C])
        b2x3 = sb("b2x3", [3 * NE1, C])
        b2s = sb("b2s", [3 * NE1, 3, C], BF16)
        pick = sb("pick", [3 * NE1, NE1, P], BF16)
        wg_s = sb("wg_s", [P, 3, NE1], BF16)
        rsc = sb("rsc", [P, 2, 512])
        gparts = sb("gparts", [P, NT, 3, NE1], BF16)
        wg = sb("wg", [P, NE1])
        bgb = sb("bgb", [P, NE1])
        bo0 = sb("bo0", [P, C])
        bo1 = sb("bo1", [P, C])
        go1 = sb("go1", [P, C])
        gn1 = sb("gn1", [C, 1])
        gat_rows = sb("gat_rows", [P, 3, F0])
        xt = sb("xt", [P, NT, C])
        xn = sb("xn", [P, NT, C])
        sq = sb("sq", [P, NT, C])
        red = sb("red", [P, 8, NT])
        xca = sb("xca", [P, NODES])
        xc = xca[0:C, :]
        xst = xca[:, :].bitcast(BF16).rearrange("p (a n) -> p a n", a=2)
        nmx = sb("nmx", [P, 8, QB])
        ksum = sb("ksum", [P, 2, B])
        rks = sb("rks", [P, 2, B])
        big = sb("big", [P, 12800])
        oute = sb("oute", [P, NT, NE0, C])
        wide = oute[:, :, :, :].rearrange("p t e c -> p (t e c)")
        Ys = [wide[0:C, 4096 * k:4096 * (k + 1)].rearrange("p (g b n) -> p g b n", g=2, b=B) for k in range(2)]
        ek = big[:, 0:2048].rearrange("p (a n) -> p a n", a=2)
        ekt = big[:, 2048:4096].rearrange("p (a t n) -> p a t n", a=2, t=QT)
        ctxT = big[:, 4096:8192].rearrange("p (g b n) -> p g b n", g=2, b=B)
        T = big[:, 8192:10240].rearrange("p (g b n) -> p g b n", g=2, b=B)
        MT = big[0:C, 10240:11264].rearrange("p (b n) -> p b n", b=B)
        qc = wide[:, 0:4096]
        prod = big[:, 0:2 * EB * FV * LO].rearrange("p (a j f l) -> p a j f l", a=2, j=EB, f=FV)
        hoff = 2 * EB * FV * LO
        hw, hl = P * HC // 2, LO * HC // 2
        hist_hi = [big[:, hoff + (hw + hl) * a:hoff + (hw + hl) * a + hw].bitcast(BF16)
                   .rearrange("p (h c) -> p h c", c=HC) for a in range(HB)]
        hist_lo = [big[:, hoff + (hw + hl) * a + hw:hoff + (hw + hl) * (a + 1)].bitcast(BF16)
                   .rearrange("p (h c) -> p h c", c=HC) for a in range(HB)]
        ring = big[:, 0:RING * 512].rearrange("p (k n) -> p k n", n=512)
        ob = big[:, 4096:8192]
        w1s = big[:, 9216:12288].bitcast(BF16).rearrange("p (a n) -> p a n", a=3)
        gT = wide[0:3 * NE1, 6144:8192].bitcast(BF16)
        xs = wide[:, 0:4096].bitcast(BF16).rearrange("p (t a c) -> p t a c", t=NT, a=4)
        keys = sb("keys", [P, GC * (1 + REST)])
        rows = keys[:, GC:GC + EC]
        big2 = sb("hist_dst", [P, EC // 2])
        dhi_h = big2[:, :].bitcast(BF16)
        dlo_h = sb("dlo_h", [P, EC], BF16)
        w1_1 = keys[:, 0:NE1 * HID1]
        w2_1 = big2[:, :].rearrange("p (e k n) -> p e k n", e=NE1, k=NH1)
        ebi = big[:, 8192:12288].bitcast(I32).rearrange("p (a n) -> p a n", a=2)
        live, key2 = wide[:, 2 * EC:3 * EC], wide[:, 3 * EC:]
        m8 = sb("m8", [P, SEGS, TOP])
        dec = sb("dec", [P, 2, GC])
        deci = sb("deci", [P, 3, GC], I32)
        idx_s = sb("idx_s", [P, GC], I32)
        idx_d = sb("idx_d", [P, GC], I32)
        dhi = sb("dhi", [P, GC])
        dlo = sb("dlo", [P, GC])
        stage_s = sb("stage_s", [P, ITC], I32)
        stage_d = sb("stage_d", [P, ITC], I32)
        flagf = sb("flagf", [P, 2])
        flagi = sb("flagi", [P, 1], I32)
        tab_s = sb("tab_s", [P, NT, FS])
        tab_d = sb("tab_d", [P, NT, FD])
        gmax = sb("gmax", [P, 2, HEADS])
        last = sb("last", [P, FS])
        gs = sb("gs", [P, NB, EB, FS])
        gd = sb("gd", [P, NB, EB, FD])
        es = sb("es", [P, 2, 3, EB, HEADS])
        val = sb("val", [P, 2, EB, FV])
        one_hi = sb("one_hi", [P, 2, EB, P])
        one_lo = sb("one_lo", [P, 2, EB, LO])
        nod = sb("nod", [P, 6, NT, HEADS])
        num = sb("num", [P, 2, NT, FV])
        cnt = sb("cnt", [P, NT])
        sc = sb("sc", [P, 4, NT, NE1])
        hid0 = xn[:, 0:XT0 * NE0 // C, :].rearrange("p t c -> p (t c)").rearrange("p (e n) -> p e n", e=NE0)

        block = ctx.enter_context(nc.Block())

        def turned(j):
            return PS[:, 2 + j % 4, 0:256].bitcast(BF16)

        def gates_turned(k):
            return PS[0:3 * NE1, k % 2, :].bitcast(BF16)

        def qe(u):
            return big[:, 4096 + 512 * (u % 4):4096 + 512 * (u % 4 + 1)].rearrange("p (k d) -> p k d", d=HEAD_DIM)

        def bc(ap, axis, n):
            a = ap.unsqueeze(axis)
            shape = list(a.shape)
            shape[axis] = n
            return a.broadcast_to(shape)

        def nth(it, a):
            return it * NB + (a + 1)

        def row(v, n=P):
            return v.unsqueeze(0).broadcast_to([n, v.shape[0]])

        @block.sync
        def _(sp):
            ei = edges.rearrange("a (p n) -> p a n", p=P)
            sp.dma_start(xc.rearrange("c (b n) -> c b n", b=B),
                         x.rearrange("b c h w -> c b (h w)")).then_inc(sem("x_in"), 16)
            sp.dma_start(ebi, ei).then_inc(sem("edges_in"), 16)
            n = 0
            for dst, src in (
                (wkv0[:, :, :], w_qkv0[256:768, :].rearrange("(g p) c -> p g c", p=P)),
                (wq0[:, :, :], w_qkv0[0:256, :].rearrange("(g p) c -> p g c", p=P)),
                (wqkv1[:, :, :], w_qkv1.rearrange("(g p) c -> p g c", p=P)),
                (wo0[:, :], w_out0), (wo1[:, :], w_out1),
                (b1r0[:, :], b1_0), (b1r1[:, :], b1_1.rearrange("e (k n) -> (e k) n", n=P)),
                (bo0[:, :], row(b_out0)),
            ):
                sp.dma_start(dst, src).then_inc(sem("conv_weights_in"), 16)
                n += 1
            assert n == 8
            for dst, src in (
                (wgat[:, HEADS:FS], W_gat),
                (attr[:, 0, :], row(att_src.rearrange("a b -> (a b)"), C)),
                (attr[:, 1, :], row(att_dst.rearrange("a b -> (a b)"), C)),
                (w1_0[:, :, :], W1_0.rearrange("e c n -> c e n")),
                (w2_0[:, :, :], W2_0.rearrange("e n c -> n e c")),
                (b2row[:, :], row(b2_0.rearrange("e c -> (e c)"), 1)),
                (gat_rows[:, 0, :], row(b_gat)), (gat_rows[:, 1, :], row(ln_gamma)),
                (gat_rows[:, 2, :], row(ln_beta)),
            ):
                sp.dma_start(dst, src).then_inc(sem("ffn0_weights_in"), 16)
                n += 1
            assert n == 17
            for dst, src in (
                (b2x3[0:NE1, :], b2_1), (b2x3[NE1:2 * NE1, :], b2_1), (b2x3[2 * NE1:, :], b2_1),
                (wg[0:C, :], Wg), (wg[C:P, :], Wg), (bgb[:, :], row(bg)),
                (bo1[:, :], row(b_out1)), (go1[:, :], row(g_out)),
                (gn1[:, :], g_norm.unsqueeze(1)),
            ):
                sp.dma_start(dst, src).then_inc(sem("layer1_weights_in"), 16)
                n += 1
            assert n == 26
            sp.wait_ge(sem("tables_made"), 1)
            sp.dma_start(table_s.rearrange("(t p) f -> p t f", p=P), tab_s[:, :, :]).then_inc(sem("tables_out"), 16)
            sp.dma_start(table_d.rearrange("(t p) f -> p t f", p=P), tab_d[:, :, :]).then_inc(sem("tables_out"), 16)
            sp.wait_ge(sem("tables_out"), 32)
            sp.dma_start(last[:, :], table_s[NODES - 1:NODES, :].broadcast_to([P, FS])).then_inc(sem("last_in"), 16)
            sp.wait_ge(sem("sums_read"), 1)
            for h in range(2):
                sp.dma_start(w1_1[C * h:C * (h + 1), :].rearrange("p (e n) -> p e n", e=NE1),
                             W1_1.rearrange("e c n -> c e n")).then_inc(sem("experts1_in"), 16)
            sp.dma_start(w2_1.rearrange("p e k c -> p (e k) c"), W2_1.rearrange("e (k p) c -> p (e k) c", p=P))\
                .then_inc(sem("experts1_in"), 16)
            for q in range(8):
                sp.wait_ge(sem("y_made"), q + 1)
                sp.dma_start(out.rearrange("b c h w -> c b (h w)")[:, 2 * q:2 * q + 2, :],
                             ob[0:C, 512 * q:512 * (q + 1)].rearrange("c (b n) -> c b n", b=2)).then_inc(sem("y_out"), 16)
            sp.wait_ge(sem("y_out"), 128)

        @block.gpsimd
        def _(pool):
            nc.gpsimd.memset(ident[:, :], 0.0).then_inc(sem("const0"), 1)
            nc.gpsimd.memset(before[:, :, :], 1.0).then_inc(sem("const0"), 1)
            nc.gpsimd.iota(iota_i[:, :], [[1, P]], base=0, channel_multiplier=0).then_inc(sem("const0"), 1)
            nc.gpsimd.memset(zeros[:, :], 0.0).then_inc(sem("zeros_made"), 1)
            nc.gpsimd.memset(ones[:, :], 1.0).then_inc(sem("ones_made"), 1)
            nc.gpsimd.memset(pick[:, :, :], 0.0).then_inc(sem("pick_steps"), 1)
            nc.gpsimd.memset(keys[:, GC + EC:], 0.0).then_inc(sem("pad_made"), 1)
            nc.gpsimd.memset(mhalf[:, :], -0.5).then_inc(sem("zeros_made"), 1)
            pool.wait_ge(sem("const0"), 3)
            nc.gpsimd.affine_select(out=ident[:, :], in_=ident[:, :], compare_op=ALU.not_equal, fill=1.0, base=0,
                                    pattern=[[-1, P]], channel_multiplier=1).then_inc(sem("ident_made"), 1)
            nc.gpsimd.affine_select(out=before[:, :, :], in_=before[:, :, :], compare_op=ALU.is_gt, fill=0.0, base=0,
                                    pattern=[[1, NE1], [-1, NE1]], channel_multiplier=0).then_inc(sem("before_made"), 1)

            for k in range(3):
                pool.wait_ge(sem("pick_steps"), k + 1)
                nc.gpsimd.affine_select(out=pick[:, :, :], in_=pick[:, :, :], compare_op=ALU.not_equal, fill=1.0,
                                        base=-NE1 * k, pattern=[[-1, NE1], [0, P]], channel_multiplier=1)\
                    .then_inc(sem("pick_steps"), 1)

            def split_weights():
                ws = [0]

                def split_step(ins):
                    ws[0] += 1
                    ins.then_inc(sem("split_steps"), 1)
                    pool.wait_ge(sem("split_steps"), ws[0])

                def split(src, n, parts, r0, r1):
                    split_step(nc.gpsimd.tensor_copy(parts[0], src))
                    split_step(nc.gpsimd.tensor_tensor(r0, src, parts[0], ALU.subtract))
                    split_step(nc.gpsimd.tensor_copy(parts[1], r0))
                    split_step(nc.gpsimd.tensor_tensor(r1, r0, parts[1], ALU.subtract))
                    split_step(nc.gpsimd.tensor_copy(parts[2], r1))

                pool.wait_ge(sem("layer1_weights_in"), 144)
                n3 = 3 * NE1
                split(b2x3[:, :], C, [b2s[:, k, :] for k in range(3)], rsc[0:n3, 0, 0:C], rsc[0:n3, 1, 0:C])
                split(wg[:, :], NE1, [wg_s[:, k, :] for k in range(3)], rsc[:, 0, 0:NE1], rsc[:, 1, 0:NE1])
                split_step(nc.gpsimd.tensor_copy(wg_s[C:P, 2, :], wg_s[C:P, 0, :]))
                pool.wait_ge(sem("experts1_in"), 48)
                for k in range(4):
                    cs = slice(512 * k, 512 * (k + 1))
                    split(w1_1[:, cs], 512, [w1s[:, j, cs] for j in range(3)], rsc[:, 0, :], rsc[:, 1, :])
                    split_step(nc.gpsimd.tensor_copy(w1s[C:P, 2, cs], w1s[C:P, 0, cs]))
                nc.gpsimd.memset(rsc[:, 0, 0:1], 0.0).then_inc(sem("weights_split"), 1)

            def inverse_roots(stage, q):
                pool.wait_ge(sem(f"{stage}_var"), q + 1)
                nc.gpsimd.tensor_tensor(red[:, 3, QT * q:QT * (q + 1)], red[:, 2, QT * q:QT * (q + 1)], mhalf[:, 0:QT],
                                        ALU.pow).then_inc(sem(f"{stage}_rstd"), 1)

            pool.wait_ge(sem("zeros_made"), 2)
            for q in range(NQ):
                inverse_roots("ln0", q)
            pool.wait_ge(sem("rest_max"), 1)
            nc.gpsimd.partition_all_reduce(flagf[:, 1:2], flagf[:, 0:1], P, RMAX).then_inc(sem("rest_all"), 1)
            for q in range(NQ):
                inverse_roots("ln1", q)
            pool.wait_ge(sem("score_max"), 1)
            nc.gpsimd.partition_all_reduce(gmax[:, 1, :], gmax[:, 0, :], P, RMAX).then_inc(sem("score_all"), 1)

            def gathers(it, t):
                for a in range(NB):
                    pool.wait_ge(sem("rows_used"), nth(it, a))
                    c0 = t * ITC + a * EB
                    nc.gpsimd.tensor_copy(stage_s[:, a * EB:(a + 1) * EB], idx_s[:, bass.ds(c0, EB)])\
                        .then_inc(sem("staged"), 1)
                    nc.gpsimd.tensor_copy(stage_d[:, a * EB:(a + 1) * EB], idx_d[:, bass.ds(c0, EB)])\
                        .then_inc(sem("staged"), 1)
                    pool.wait_ge(sem("staged"), it * (2 * NB) + (2 * a + 2))
                    nc.gpsimd.sem_inc(sem("staging_seen"), 1)
                    for j in range(EB):
                        c = a * EB + j
                        nc.gpsimd.indirect_dma_start(
                            gs[:, a, j, :], None, table_s,
                            bass.IndirectOffsetOnAxis(stage_s[:, c:c + 1], axis=0)).then_inc(sem(f"rows_in{a}"), 16)
                        nc.gpsimd.indirect_dma_start(
                            gd[:, a, j, :], None, table_d,
                            bass.IndirectOffsetOnAxis(stage_d[:, c:c + 1], axis=0)).then_inc(sem(f"rows_in{a}"), 16)

            pool.wait_ge(sem("tables_out"), 32)
            pool.wait_ge(sem("decoded"), 1)
            with nc.gpsimd.Fori(0, ITERS) as t:
                gathers(t, t)
            pool.wait_ge(sem("flag_made"), 1)
            left = nc.gpsimd.value_load(flagi[0:1, 0:1], min_val=0, max_val=1)
            with nc.gpsimd.If(left > 0):
                with nc.gpsimd.Fori(0, REST) as g:
                    pool.wait_ge(sem("decoded"), g + 2)
                    nc.gpsimd.sem_inc(sem("staging_seen"), 1)
                    with nc.gpsimd.Fori(0, ITERS) as t:
                        gathers((g + 1) * ITERS + t, t)

            pool.wait_ge(sem("gat_var"), 1)
            nc.gpsimd.tensor_tensor(red[:, 3, :], red[:, 2, :], mhalf[:, :], ALU.pow).then_inc(sem("gat_rstd"), 1)
            for stage in ("ln2", "ln2r"):
                for q in range(NQ):
                    inverse_roots(stage, q)
            split_weights()
            for stage in ("ln3r", "ln4"):
                for q in range(NQ):
                    inverse_roots(stage, q)

        @block.scalar
        def _(act):
            for q in range(NQ):
                act.wait_ge(sem("xt_turned"), q + 1)
                nc.scalar.copy(xt[:, QT * q:QT * (q + 1), :],
                               PS[:, q % 2, :].rearrange("p (t c) -> p t c", c=C)).then_inc(sem("xt_made"), 1)
            act.wait_ge(sem("weights_turned"), 3)
            nc.scalar.copy(wkvT0[:, :], PS[0:C, 4, :]).then_inc(sem("weights_made"), 1)
            nc.scalar.copy(wqkvT1[:, :], PS[0:C, 5, 0:384]).then_inc(sem("weights_made"), 1)
            nc.scalar.copy(cols[:, 0:3 * C], PS[:, 6, 0:3 * C]).then_inc(sem("weights_made"), 1)
            nc.scalar.copy(cols[:, 3 * C:], PS[:, 6, 3 * C:3 * C + NE0 + NE1 * NH1]).then_inc(sem("weights_made"), 1)

            def channel_major(stage, scale=None):
                for k in range(8):
                    act.wait_ge(sem(f"{stage}_turned"), k + 1)
                    src = PS[0:C, 6 + k % 2, :]
                    dst = xc[:, 512 * k:512 * (k + 1)]
                    if scale is None:
                        ins = nc.scalar.copy(dst, src)
                    else:
                        ins = nc.scalar.activation(dst, src, ACT.Copy, scale=scale)
                    ins.then_inc(sem(f"{stage}_xc"), 1)

            def pixel_softmax(L, G):
                for u in range(NQ * G):
                    q, g = u // G, u % G
                    act.wait_ge(sem(f"{L}_kmax"), u + 1)
                    if u >= 2:
                        act.wait_ge(sem(f"{L}_kturned"), u - 1)
                    for b in range(QB):
                        bank = 2 * (u % 2) + b // 2
                        nc.scalar.activation(ek[:, u % 2, HW * b:HW * (b + 1)], PS[:, bank, HW * (b % 2):HW * (b % 2 + 1)],
                                             ACT.Exp, bias=nmx[:, u, b:b + 1],
                                             accum_out=ksum[:, g, QB * q + b:QB * q + b + 1]).then_inc(sem(f"{L}_kexp"), 1)
                    if u >= 1:
                        second_half(L, u - 1)
                second_half(L, NQ * G - 1)

            def second_half(L, u):
                act.wait_ge(sem(f"{L}_kturned"), u + 1)
                if u >= 2:
                    act.wait_ge(sem(f"{L}_ymade"), u - 1)
                nc.scalar.copy(ekt[:, u % 2, 4:8, :], PS[:, 5, :].rearrange("p (t n) -> p t n", n=P))\
                    .then_inc(sem(f"{L}_ekt_a"), 1)

            channel_major("ln0")
            pixel_softmax("c0", 2)
            for h in range(2):
                act.wait_ge(sem("c0_mmade"), h + 1)
                nc.scalar.copy(MT[:, 8 * h:8 * (h + 1), :], PS[0:C, 6 + h, :].rearrange("p (b n) -> p b n", n=C))\
                    .then_inc(sem("c0_mt"), 1)
            channel_major("ln1")

            for k in range(2):
                act.wait_ge(sem("node_scores"), k + 1)
                nc.scalar.activation(nod[:, 2 + k, :, :], nod[:, k, :, :], ACT.Exp).then_inc(sem("node_exps"), 1)

            def edge_exps(it, a):
                act.wait_ge(sem("edge_scores"), nth(it, a))
                act.wait_ge(sem("const0"), 3)
                nc.scalar.activation(val[:, a % 2, :, F0:FV], es[:, a % 2, 2, :, :], ACT.Exp)\
                    .then_inc(sem("edge_exps"), 1)

            with nc.scalar.Fori(0, ITERS) as t:
                for a in range(NB):
                    edge_exps(t, a)
                    for e in range(2 * a, 2 * a + 2) if a < 2 else ():
                        act.wait_ge(sem("h0_made"), t * NE0 + (e + 1))
                        act.wait_ge(sem("const0"), 3)
                        nc.scalar.activation(hid0[:, e, :], PS[:, 3 + e % 2, 0:XT0], ACT.Gelu,
                                             bias=b1c0[:, e:e + 1]).then_inc(sem("h0_gelu"), 1)
                    for i in range(2 * a - 4, 2 * a - 2) if a >= 2 else ():
                        act.wait_ge(sem("o0_made"), t * (XT0 // P) + (i + 1))
                        nc.scalar.copy(wide[:, bass.ds(t * (XT0 * 2) + i * (NE0 * C), NE0 * C)],
                                       PS[:, 5 + i % 2, 0:NE0 * C]).then_inc(sem("oute_made"), 1)
            act.wait_ge(sem("flag_made"), 1)
            left = nc.scalar.value_load(flagi[0:1, 0:1], min_val=0, max_val=1)
            with nc.scalar.If(left > 0):
                with nc.scalar.Fori(0, REST) as g:
                    with nc.scalar.Fori(0, ITERS) as t:
                        for a in range(NB):
                            edge_exps((g + 1) * ITERS + t, a)

            act.wait_ge(sem("gate_in0"), 1)
            nc.scalar.activation(sc[:, 2, :, 0:NE0], sc[:, 1, :, 0:NE0], ACT.Exp).then_inc(sem("gate_exp0"), 1)

            channel_major("ln2", gn1[:, 0:1])
            for u in range(8):
                act.wait_ge(sem("q_shifted"), u + 1)
                nc.scalar.activation(qe(u), qe(u), ACT.Exp).then_inc(sem("q_exp"), 1)
                act.wait_ge(sem("q_turned"), u + 1)
                nc.scalar.copy(qc[:, 512 * u:512 * (u + 1)], PS[:, 2 + u % 2, :]).then_inc(sem("qc_made"), 1)
            pixel_softmax("c1", 1)
            def copy_out(k):
                act.wait_ge(sem("x3_turned"), k + 1)
                nc.scalar.copy(ob[0:C, 512 * k:512 * (k + 1)], PS[0:C, k % 2, :]).then_inc(sem("x3_made"), 1)

            for k in range(8):
                copy_out(k)
                for a in range(2):
                    act.wait_ge(sem("xs_turned"), 2 * k + a + 1)
                    nc.scalar.copy(xst[:, a, 512 * k:512 * (k + 1)], turned(2 * k + a)).then_inc(sem("xst_made"), 1)
            act.wait_ge(sem("gate_in1"), 1)
            nc.scalar.activation(sc[:, 2, :, :], sc[:, 1, :, :], ACT.Exp).then_inc(sem("gate_exp1"), 1)
            for k in range(4):
                act.wait_ge(sem("g_turned"), k + 1)
                nc.scalar.copy(gT[:, 1024 * k:1024 * (k + 1)], gates_turned(k)).then_inc(sem("gT_made"), 1)
            for m in range(8 * NE1 * NH1):
                act.wait_ge(sem("h1_made"), m + 1)
                if m >= RING:
                    act.wait_ge(sem("h1_used"), m - RING + 1)
                k = m % (NE1 * NH1)
                nc.scalar.activation(ring[:, m % RING, :], PS[:, m % 3, :], ACT.Gelu,
                                     bias=b1c1[:, k:k + 1]).then_inc(sem("h1_gelu"), 1)

        @block.tensor
        def _(pe):
            mm, tr = nc.tensor.matmul, nc.tensor.transpose
            pe.wait_ge(sem("ident_made"), 1)
            pe.wait_ge(sem("x_in"), 16)
            for q in range(NQ):
                if q >= 2:
                    pe.wait_ge(sem("xt_made"), q - 1)
                for i in range(QT):
                    t = QT * q + i
                    ins = tr(PS[:, q % 2, C * i:C * (i + 1)], xc[:, P * t:P * (t + 1)], ident[0:C, 0:C])
                ins.then_inc(sem("xt_turned"), 1)
            pe.wait_ge(sem("conv_weights_in"), 128)
            for g in range(4):
                ins = tr(PS[0:C, 4, P * g:P * (g + 1)], wkv0[:, g, :], ident[:, :])
            ins.then_inc(sem("weights_turned"), 1)
            for g in range(3):
                ins = tr(PS[0:C, 5, P * g:P * (g + 1)], wqkv1[:, g, :], ident[:, :])
            ins.then_inc(sem("weights_turned"), 1)
            for g in range(2):
                tr(PS[:, 6, C * g:C * (g + 1)], wo0[:, P * g:P * (g + 1)], ident[0:C, 0:C])
            tr(PS[:, 6, 2 * C:3 * C], wo1[:, :], ident[0:C, 0:C])
            tr(PS[:, 6, 3 * C:3 * C + NE0], b1r0[:, :], ident[0:NE0, 0:NE0])
            n1 = NE1 * NH1
            tr(PS[:, 6, 3 * C + NE0:3 * C + NE0 + n1], b1r1[:, :], ident[0:n1, 0:n1]).then_inc(sem("weights_turned"), 1)

            def channel_major(stage, first):
                for k in range(8):
                    pe.wait_ge(sem(f"{stage}_xn"), k // 2 + 1)
                    if k >= 2:
                        pe.wait_ge(sem(f"{stage}_xc"), k - 1)
                    elif k == 0:
                        first()
                    for i in range(4):
                        ins = tr(PS[0:C, 6 + k % 2, P * i:P * (i + 1)], xn[:, 4 * k + i, :], ident[:, :])
                    ins.then_inc(sem(f"{stage}_turned"), 1)

            def keys_of(L, G, wk, stage, u):
                q, g = u // G, u % G
                pe.wait_ge(sem(f"{stage}_xc"), 2 * q + 2)
                if u >= 2:
                    pe.wait_ge(sem(f"{L}_kexp"), QB * (u - 1))
                for h in range(2):
                    ins = mm(PS[:, 2 * (u % 2) + h, :], wk(g), xc[:, 1024 * q + 512 * h:1024 * q + 512 * (h + 1)],
                             start=True, stop=True)
                ins.then_inc(sem(f"{L}_kmade"), 1)

            def context_of(L, G, u):
                q, g = u // G, u % G
                pe.wait_ge(sem(f"{L}_kexp"), QB * (u + 1))
                if u >= 1:
                    pe.wait_ge(sem(f"{L}_ekt_a"), u)
                    pe.wait_ge(sem(f"{L}_ekt_v"), u)
                for i in range(QT):
                    ins = tr(PS[:, 4 + i // 4, P * (i % 4):P * (i % 4 + 1)], ek[:, u % 2, P * i:P * (i + 1)], ident[:, :])
                ins.then_inc(sem(f"{L}_kturned"), 1)
                pe.wait_ge(sem(f"{L}_ekt_a"), u + 1)
                pe.wait_ge(sem(f"{L}_ekt_v"), u + 1)
                if u >= 1:
                    pe.wait_ge(sem(f"{L}_yv"), u)
                for b in range(QB):
                    for s in range(2):
                        ins = mm(PS[0:C, 6, P * b:P * (b + 1)], xn[:, QT * q + 2 * b + s, :], ekt[:, u % 2, 2 * b + s, :],
                                 start=(s == 0), stop=(s == 1))
                ins.then_inc(sem(f"{L}_ymade"), 1)

            def attention(L, G, wk, wv, wo, stage):
                for u in range(NQ * G):
                    keys_of(L, G, wk, stage, u)
                    if u >= 1:
                        context_of(L, G, u - 1)
                context_of(L, G, NQ * G - 1)
                for c in range(NQ * G + 1):
                    g, q = c // NQ, c % NQ
                    if c < NQ * G:
                        pe.wait_ge(sem(f"{L}_yv"), NQ * G)
                        if c >= 2:
                            pe.wait_ge(sem(f"{L}_ctx"), c - 1)
                        mm(PS[:, 6 + c % 2, :], wv(g), Ys[L == "c1"][:, g, QB * q:QB * (q + 1), :].rearrange("c b n -> c (b n)"),
                           start=True, stop=True).then_inc(sem(f"{L}_cmade"), 1)
                    if c >= 1:
                        g, q = (c - 1) // NQ, (c - 1) % NQ
                        pe.wait_ge(sem(f"{L}_ctx"), c)
                        if c >= 3:
                            pe.wait_ge(sem(f"{L}_t"), c - 2)
                        for b in range(QB):
                            ins = mm(PS[:, 4 + (c - 1) % 2, C * b:C * (b + 1)], ctxT[:, g, QB * q + b, :], wo[:, g, :],
                                     start=True, stop=True)
                        ins.then_inc(sem(f"{L}_tmade"), 1)

            def after_weights():
                pe.wait_ge(sem("weights_made"), 4)

            channel_major("ln0", after_weights)
            attention("c0", 2, lambda g: wkvT0[:, P * g:P * (g + 1)], lambda g: wkvT0[:, 256 + P * g:256 + P * (g + 1)],
                      woT0, "ln0")
            pe.wait_ge(sem("c0_t"), 8)
            pe.wait_ge(sem("c0_ctx"), 8)
            for h in range(2):
                for g in range(2):
                    ins = mm(PS[0:C, 6 + h, :], wq0[:, g, :], T[:, g, 8 * h:8 * (h + 1), :].rearrange("p b n -> p (b n)"),
                             start=(g == 0), stop=(g == 1))
                ins.then_inc(sem("c0_mmade"), 1)
            pe.wait_ge(sem("c0_mt"), 2)
            for q in range(NQ):
                for i in range(QT):
                    t = QT * q + i
                    ins = mm(PS[:, q, C * i:C * (i + 1)], xc[:, P * t:P * (t + 1)], MT[:, t // 2, :], start=True, stop=True)
                ins.then_inc(sem("c0_out"), 1)

            channel_major("ln1", lambda: None)
            pe.wait_ge(sem("ln1_xc"), 8)
            pe.wait_ge(sem("wgat_made"), 2)
            W24 = FS + HEADS
            for t in range(NT):
                ins = mm(PS[:, t // 16, W24 * (t % 16):W24 * (t % 16 + 1)], xc[:, P * t:P * (t + 1)], wgat[:, :],
                         start=True, stop=True)
            ins.then_inc(sem("tables_turned"), 1)

            pe.wait_ge(sem("ffn0_weights_in"), 144)
            pe.wait_ge(sem("ones_made"), 1)
            pe.wait_ge(sem("tables_read"), 4)
            for k in range(2):
                mm(PS[:, k, 0:FH * LO], zeros[:, 0:P], zeros[:, :], start=True, stop=False)
            mm(PS[:, 2, 0:LO], zeros[:, 0:P], zeros[:, 0:LO], start=True, stop=False).then_inc(sem("sums_cleared"), 1)
            for name in ["prod_used"] * 2 + ["hist_used"] * HB:
                mm(PS[:, 7, 0:P], zeros[:, 0:P], zeros[:, 0:P], start=True, stop=True).then_inc(sem(name), 1)

            def scatter(it, a):
                pe.wait_ge(sem("prod_made"), nth(it, a))
                pe.wait_ge(sem("const0"), 3)
                for j in range(EB):
                    for k in range(2):
                        ins = mm(PS[:, k, 0:FH * LO], one_hi[:, a % 2, j, :], prod[:, a % 2, j, FH * k:FH * (k + 1), :],
                                 start=False, stop=False, skip_group_check=True)
                ins.then_inc(sem("prod_used"), 1)

            def histogram(it, a):
                for h in range(HB):
                    pe.wait_ge(sem("hist_made"), it * (2 * HB * NB) + 2 * (a * HB + h + 1))
                    pe.wait_ge(sem("const0"), 3)
                    for c in range(HC):
                        ins = mm(PS[:, 2, 0:LO], hist_hi[h][:, :, c], hist_lo[h][:, :, c],
                                 start=False, stop=False, skip_group_check=True)
                    ins.then_inc(sem("hist_used"), 1)

            with nc.tensor.Fori(0, ITERS) as t:
                for a in range(NB):
                    for e in range(2 * a, 2 * a + 2) if a < 2 else ():
                        if e >= 2:
                            pe.wait_ge(sem("h0_gelu"), t * NE0 + (e - 1))
                            nc.tensor.sem_inc(sem("h0_room"), 1)
                        mm(PS[:, 3 + e % 2, 0:XT0], w1_0[:, e, :], xc[:, bass.ds(t * XT0, XT0)],
                           start=True, stop=True).then_inc(sem("h0_made"), 1)
                    for i in range(2 * a - 4, 2 * a - 2) if a >= 2 else ():
                        pe.wait_ge(sem("h0_gelu"), t * NE0 + NE0)
                        if i >= 2:
                            pe.wait_ge(sem("oute_made"), t * (XT0 // P) + (i - 1))
                        mm(PS[:, 5 + i % 2, 0:NE0 * C], ones[:, :], b2row[:, :], start=True, stop=False,
                           skip_group_check=True)
                        for e in range(NE0):
                            ins = mm(PS[:, 5 + i % 2, C * e:C * (e + 1)], hid0[:, e, P * i:P * (i + 1)], w2_0[:, e, :],
                                     start=False, stop=(e == NE0 - 1), skip_group_check=True)
                        ins.then_inc(sem("o0_made"), 1)
                    histogram(t, a)
                    scatter(t, a)
                pe.wait_ge(sem("oute_made"), t * (XT0 // P) + XT0 // P)
            pe.wait_ge(sem("flag_made"), 1)
            left = nc.tensor.value_load(flagi[0:1, 0:1], min_val=0, max_val=1)
            with nc.tensor.If(left > 0):
                with nc.tensor.Fori(0, REST) as g:
                    with nc.tensor.Fori(0, ITERS) as t:
                        for a in range(NB):
                            scatter((g + 1) * ITERS + t, a)
            for k in range(2):
                mm(PS[:, k, 0:FH * LO], zeros[:, 0:P], zeros[:, :], start=False, stop=True)
            mm(PS[:, 2, 0:LO], zeros[:, 0:P], zeros[:, 0:LO], start=False, stop=True)\
                .then_inc(sem("sums_made"), 1)

            channel_major("ln2", lambda: None)
            for u in range(8 + 1):
                if u < 8:
                    pe.wait_ge(sem("ln2_xc"), u + 1)
                    if u >= 2:
                        pe.wait_ge(sem("q_shifted"), u - 1)
                    for i in range(4):
                        t = 4 * u + i
                        ins = mm(PS[:, u % 2, P * i:P * (i + 1)], xc[:, P * t:P * (t + 1)], wqkvT1[:, 0:P],
                                 start=True, stop=True)
                    ins.then_inc(sem("q_made"), 1)
                if u >= 1:
                    v = u - 1
                    pe.wait_ge(sem("q_soft"), v + 1)
                    if v >= 2:
                        pe.wait_ge(sem("qc_made"), v - 1)
                    for i in range(4):
                        ins = tr(PS[:, 2 + v % 2, P * i:P * (i + 1)],
                                 qe(v)[:, 4 * i:4 * (i + 1), :].rearrange("p k d -> p (k d)"), ident[:, :])
                    ins.then_inc(sem("q_turned"), 1)
            pe.wait_ge(sem("qc_made"), 8)
            attention("c1", 1, lambda g: wqkvT1[:, P:2 * P], lambda g: wqkvT1[:, 2 * P:3 * P], woT1, "ln2")
            pe.wait_ge(sem("c1_t"), 4)
            for q in range(NQ):
                for i in range(QT):
                    t = QT * q + i
                    ins = mm(PS[:, q, C * i:C * (i + 1)], qc[:, P * t:P * (t + 1)], T[:, 0, t // 2, :], start=True, stop=True)
                ins.then_inc(sem("c1_out"), 1)

            pe.wait_ge(sem("ident_b_made"), 1)
            for k in range(8):
                pe.wait_ge(sem("ln4_sum"), k // 2 + 1)
                if k >= 2:
                    pe.wait_ge(sem("x3_made"), k - 1)
                for i in range(4):
                    ins = tr(PS[0:C, k % 2, P * i:P * (i + 1)], xt[:, 4 * k + i, :], ident[:, :])
                ins.then_inc(sem("x3_turned"), 1)
                pe.wait_ge(sem("xs_made"), k // 2 + 1)
                for a in range(2):
                    j = 2 * k + a
                    if j >= 4:
                        pe.wait_ge(sem("xst_made"), j - 3)
                    for i in range(4):
                        ins = tr(turned(j)[:, P * i:P * (i + 1)],
                                 xs[:, 4 * k + i, 2 * a:2 * a + 2, :].rearrange("p a c -> p (a c)"), ident_b[:, :])
                    ins.then_inc(sem("xs_turned"), 1)
            pe.wait_ge(sem("xst_made"), 16)
            pe.wait_ge(sem("weights_split"), 1)
            PARTS = ((0, 0), (0, 1), (1, 2))
            for t in range(NT):
                for n, (a, k) in enumerate(PARTS):
                    ins = mm(PS[:, 7, NE1 * t:NE1 * (t + 1)], xst[:, a, P * t:P * (t + 1)], wg_s[:, k, :],
                             start=(n == 0), stop=(n == 2))
            ins.then_inc(sem("logits_made"), 1)
            pe.wait_ge(sem("gates1"), 1)
            pe.wait_ge(sem("x3_made"), 8)
            for k in range(4):
                if k >= 2:
                    pe.wait_ge(sem("gT_made"), k - 1)
                for i in range(8):
                    ins = tr(gates_turned(k)[:, P * i:P * (i + 1)],
                             gparts[:, 8 * k + i, :, :].rearrange("p a e -> p (a e)"), ident_b[:, :])
                ins.then_inc(sem("g_turned"), 1)
            pe.wait_ge(sem("gT_made"), 4)

            def hidden1(m):
                n, k = m // (NE1 * NH1), m % (NE1 * NH1)
                if m >= 3:
                    pe.wait_ge(sem("h1_gelu"), m - 2)
                for j, (a, w) in enumerate(PARTS):
                    ins = mm(PS[:, m % 3, :], w1s[:, w, P * k:P * (k + 1)], xst[:, a, 512 * n:512 * (n + 1)],
                             start=(j == 0), stop=(j == 2))
                ins.then_inc(sem("h1_made"), 1)
                if k % NH1 == 0:
                    g = m // NH1
                    if g >= 2:
                        pe.wait_ge(sem("h1_gated"), NH1 * (g - 1))
                    mm(PS[:, 3 + g % 2, :], pick[:, k // NH1, :], gT[:, 512 * n:512 * (n + 1)],
                       start=True, stop=True).then_inc(sem("g_spread"), 1)

            def second1(m):
                n, k = m // (NE1 * NH1), m % (NE1 * NH1)
                if k == 0:
                    if n >= 2:
                        pe.wait_ge(sem("y_made"), n - 1)
                    for j in range(3):
                        mm(PS[0:C, 5 + n % 2, :], b2s[:, j, :], gT[:, 512 * n:512 * (n + 1)], start=(j == 0), stop=False)
                pe.wait_ge(sem("h1_gated"), m + 1)
                ins = mm(PS[0:C, 5 + n % 2, :], w2_1[:, k // NH1, k % NH1, :], ring[:, m % RING, :],
                         start=False, stop=(k == NE1 * NH1 - 1))
                ins.then_inc(sem("h1_used"), 1)

            M1 = 8 * NE1 * NH1
            LAG = 4
            for m in range(M1 + LAG):
                if m < M1:
                    hidden1(m)
                if m >= LAG:
                    second1(m - LAG)

        @block.vector
        def _(dve):
            V = nc.vector
            steps = [0]

            def then(ins):
                steps[0] += 1
                ins.then_inc(sem("dve_steps"), 1)
                dve.wait_ge(sem("dve_steps"), steps[0])

            for g in range(4):
                s = slice(32 * g, 32 * g + 32)
                if g == 0:
                    then(V.memset(blocks[:, :], 0.0))
                ins = V.memset(blocks[s, s], 1.0)
            then(ins)
            dve.wait_ge(sem("const0"), 3)
            then(V.tensor_copy(iota[:, :], iota_i[:, :]))
            V.tensor_copy(iota_h[:, :, :], bc(iota[:, :], 2, HC)).then_inc(sem("iota_made"), 1)

            dve.wait_ge(sem("ident_made"), 1)
            V.tensor_copy(ident_b[:, :], ident[:, :]).then_inc(sem("ident_b_made"), 1)
            for a in range(NB):
                V.memset(gs[:, a, :, :], 0.0).then_inc(sem("rows_used"), 1)

            tops = [0, 0]

            def compact(r):
                if r == 0:
                    dve.wait_ge(sem("pad_made"), 1)
                for s in range(SEGS):
                    V.max(m8[:, s, :], rows[:, SEG * s:SEG * (s + 1)]).then_inc(sem("top_found"), 1)
                dve.wait_ge(sem("top_found"), SEGS * (r + 1))
                c = r * SEGS * TOP
                V.tensor_copy(keys[:, c:c + SEGS * TOP], m8[:, :, :].rearrange("p s k -> p (s k)"))\
                    .then_inc(sem("top_kept"), 1)
                for s in range(SEGS):
                    seg = rows[:, SEG * s:SEG * (s + 1)]
                    V.match_replace(seg, m8[:, s, :], seg, 0.0).then_inc(sem("top_removed"), 1)
                dve.wait_ge(sem("top_kept"), r + 1)
                dve.wait_ge(sem("top_removed"), SEGS * (r + 1))

            def decode(col):
                k0 = keys[:, bass.ds(col, GC)]
                k = dec[:, 0, :]
                ki, hi_i, lo_i = deci[:, 0, :], deci[:, 1, :], deci[:, 2, :]
                yield V.tensor_scalar(dec[:, 1, :], k0, 0.5, None, ALU.is_gt)
                yield V.tensor_scalar(ki, k0, -1.0, 0.0, ALU.add, ALU.max)
                yield V.tensor_scalar(idx_s[:, :], ki, 12, None, ALU.logical_shift_right)
                yield V.tensor_scalar(idx_d[:, :], ki, NODES - 1, None, ALU.bitwise_and)
                yield V.tensor_scalar(hi_i, idx_d[:, :], P - 1, None, ALU.bitwise_and)
                yield V.tensor_scalar(lo_i, idx_d[:, :], 7, None, ALU.logical_shift_right)
                yield V.scalar_tensor_tensor(out=k, in0=hi_i, scalar=1.0, in1=dec[:, 1, :], op0=ALU.add, op1=ALU.mult)
                yield V.tensor_scalar(dhi[:, :], k, -1.0, None, ALU.add)
                yield V.tensor_copy(dlo[:, :], lo_i)

            DECODE_STEPS = 8

            def edges_ready():
                V.tensor_reduce(flagf[:, 0:1], rows, X, ALU.max).then_inc(sem("rest_max"), 1)
                for n, ins in enumerate(decode(0)):
                    if n < DECODE_STEPS:
                        then(ins)
                ins.then_inc(sem("decoded"), 1)

            def histogram_indices():
                raw = key2.bitcast(I32)
                then(V.tensor_scalar(raw, ebi[:, 1, :], P - 1, None, ALU.bitwise_and))
                then(V.scalar_tensor_tensor(out=dhi_h[:, :], in0=live, scalar=256.0, in1=raw, op0=ALU.mult, op1=ALU.add))
                then(V.tensor_scalar(raw, ebi[:, 1, :], 7, None, ALU.logical_shift_right))
                then(V.tensor_copy(dlo_h[:, :], raw))

            def sums(q, src):
                T8 = slice(QT * q, QT * (q + 1))
                then(V.tensor_reduce(red[:, 0, T8], src[:, T8, :], X, ALU.add))
                then(V.tensor_scalar(red[:, 1, T8], red[:, 0, T8], -1.0 / C, None, ALU.mult))
                then(V.tensor_tensor(xn[:, T8, :], src[:, T8, :], bc(red[:, 1, T8], 2, C), ALU.add))

            def squares(q, src, stage, scale, eps):
                T8 = slice(QT * q, QT * (q + 1))
                then(V.tensor_tensor(sq[:, T8, :], src[:, T8, :], src[:, T8, :], ALU.mult))
                then(V.tensor_reduce(red[:, 0, T8], sq[:, T8, :], X, ALU.add))
                V.tensor_scalar(red[:, 2, T8], red[:, 0, T8], scale, eps, ALU.mult, ALU.add)\
                    .then_inc(sem(f"{stage}_var"), 1)

            def scaled(q, stage, signal):
                T8 = slice(QT * q, QT * (q + 1))
                dve.wait_ge(sem(f"{stage}_rstd"), q + 1)
                V.tensor_tensor(xn[:, T8, :], xn[:, T8, :], bc(red[:, 3, T8], 2, C), ALU.mult)\
                    .then_inc(sem(signal), 1)

            def layer_norm(stage, eps, ready, signal=None, after=None):
                for q in range(NQ):
                    ready(q)
                    if after:
                        after(q)
                    sums(q, xt)
                    squares(q, xn, stage, 1.0 / C, eps)
                for q in range(NQ):
                    scaled(q, stage, signal or f"{stage}_xn")

            layer_norm("ln0", LN_C_EPS, lambda q: dve.wait_ge(sem("xt_made"), q + 1))
            dve.wait_ge(sem("edges_in"), 16)
            src_i, dst_i = ebi[:, 0, :], ebi[:, 1, :]
            V.tensor_scalar(live, src_i, float(NODES - 1) - 0.5, None, ALU.is_lt)
            then(V.scalar_tensor_tensor(out=rows, in0=src_i, scalar=float(NODES), in1=dst_i, op0=ALU.mult, op1=ALU.add))
            then(V.scalar_tensor_tensor(out=key2, in0=dst_i, scalar=float(NODES) - 0.5, in1=live, op0=ALU.is_lt,
                                        op1=ALU.mult))
            then(V.scalar_tensor_tensor(out=rows, in0=rows, scalar=1.0, in1=key2, op0=ALU.add, op1=ALU.mult))

            def pixel_attention(L, G, yscale, between=lambda u: None):
                for u in range(NQ * G + 1):
                    if u < NQ * G:
                        dve.wait_ge(sem(f"{L}_kmade"), u + 1)
                        V.tensor_reduce(nmx[:, u, :], PS[:, 2 * (u % 2):2 * (u % 2) + 2, :]
                                        .rearrange("p a (b n) -> p (a b) n", n=HW), X, ALU.max,
                                        negate=True).then_inc(sem(f"{L}_kmax"), 1)
                    if u >= 1:
                        v = u - 1
                        q, g = v // G, v % G
                        dve.wait_ge(sem(f"{L}_kturned"), v + 1)
                        if v >= 2:
                            dve.wait_ge(sem(f"{L}_ymade"), v - 1)
                        V.tensor_copy(ekt[:, v % 2, 0:4, :], PS[:, 4, :].rearrange("p (t n) -> p t n", n=P))\
                            .then_inc(sem(f"{L}_ekt_v"), 1)
                        dve.wait_ge(sem(f"{L}_ymade"), v + 1)
                        dst = Ys[L == "c1"][:, g, QB * q:QB * (q + 1), :]
                        src = PS[0:C, 6, :].rearrange("p (b n) -> p b n", n=P)
                        V.tensor_scalar(dst, src, 1.0 if yscale is None else yscale, None, ALU.mult)\
                            .then_inc(sem(f"{L}_yv"), 1)
                    between(u)
                dve.wait_ge(sem(f"{L}_kexp"), QB * NQ * G)
                then(V.reciprocal(rks[:, 0:G, :], ksum[:, 0:G, :]))
                if G == 1:
                    then(V.tensor_scalar(rks[:, 0, :], rks[:, 0, :], HEAD_DIM ** -0.5, None, ALU.mult))
                for c in range(NQ * G + 1):
                    if c < NQ * G:
                        g, q = c // NQ, c % NQ
                        dve.wait_ge(sem(f"{L}_cmade"), c + 1)
                        V.tensor_tensor(ctxT[:, g, QB * q:QB * (q + 1), :],
                                        PS[:, 6 + c % 2, :].rearrange("p (b n) -> p b n", n=P), bc(blocks[:, :], 1, QB),
                                        ALU.mult).then_inc(sem(f"{L}_ctx"), 1)
                    if c >= 1:
                        g, q = (c - 1) // NQ, (c - 1) % NQ
                        dve.wait_ge(sem(f"{L}_tmade"), c)
                        V.tensor_tensor(T[:, g, QB * q:QB * (q + 1), :],
                                        PS[:, 4 + (c - 1) % 2, 0:QB * C].rearrange("p (b n) -> p b n", n=C),
                                        bc(rks[:, g, QB * q:QB * (q + 1)], 2, C), ALU.mult).then_inc(sem(f"{L}_t"), 1)

            def between0(u):
                if u == 8:
                    histogram_indices()
                else:
                    for r in range(ROUNDS * u // 8, ROUNDS * (u + 1) // 8):
                        compact(r)

            pixel_attention("c0", 2, None, between0)
            edges_ready()
            dve.wait_ge(sem("conv_weights_in"), 128)
            then(V.tensor_tensor(xt[:, :, :], xt[:, :, :], bc(bo0[:, :], 1, NT), ALU.add))

            def add_attention(q):
                dve.wait_ge(sem("c0_out"), q + 1)
                T8 = slice(QT * q, QT * (q + 1))
                then(V.tensor_tensor(xt[:, T8, :], xt[:, T8, :], PS[:, q, :].rearrange("p (t c) -> p t c", c=C), ALU.add))

            dve.wait_ge(sem("ffn0_weights_in"), 144)
            then(V.tensor_tensor(attm[:, :, :], attr[:, :, :], bc(wgat[:, HEADS:FS], 1, 2), ALU.mult))
            for k, c in ((0, 0), (1, FS)):
                V.tensor_reduce(wgat[:, c:c + HEADS], attm[:, k, :].rearrange("p (h e) -> p h e", e=NE0), X, ALU.add)\
                    .then_inc(sem("wgat_made"), 1)
            layer_norm("ln1", LN_T_EPS, add_attention)

            dve.wait_ge(sem("tables_turned"), 1)
            W24 = FS + HEADS
            for k in range(2):
                src = PS[:, k, 0:16 * W24].rearrange("p (t f) -> p t f", f=W24)
                V.tensor_copy(tab_s[:, 16 * k:16 * (k + 1), :], src[:, :, 0:FS]).then_inc(sem("tables_read"), 1)
                V.tensor_copy(tab_d[:, 16 * k:16 * (k + 1), 0:HEADS], src[:, :, FS:W24]).then_inc(sem("tables_read"), 1)
            dve.wait_ge(sem("tables_read"), 4)
            V.tensor_reduce(gmax[:, 0, :], tab_s[:, :, 0:HEADS].rearrange("p t h -> p h t"), X, ALU.max)\
                .then_inc(sem("score_max"), 1)

            dve.wait_ge(sem("score_all"), 1)
            then(V.tensor_tensor(nod[:, 4, :, :], tab_d[:, :, 0:HEADS], bc(gmax[:, 1, :], 1, NT), ALU.add))
            V.scalar_tensor_tensor(out=tab_d[:, :, HEADS:FD], in0=nod[:, 4, :, :], scalar=SLOPE, in1=nod[:, 4, :, :],
                                   op0=ALU.mult, op1=ALU.max).then_inc(sem("tables_made"), 1)
            dve.wait_ge(sem("rest_all"), 1)
            V.tensor_scalar(flagi[:, :], flagf[:, 1:2], 0.5, None, ALU.is_gt).then_inc(sem("flag_made"), 1)
            dve.wait_ge(sem("tables_made"), 1)
            ad, guard = tab_d[:, :, 0:HEADS], tab_d[:, :, HEADS:FD]
            for k in range(2):
                if k:
                    dve.wait_ge(sem("last_in"), 16)
                a = tab_s[:, :, 0:HEADS] if k == 0 else bc(last[:, 0:HEADS], 1, NT)
                st = list(leaky_steps(V, nod[:, k, :, :], nod[:, 4, :, :], a, ad, guard))
                for n, f in enumerate(st):
                    ins = f()
                    if n < 2:
                        then(ins)
                    else:
                        ins.then_inc(sem("node_scores"), 1)
                dve.wait_ge(sem("node_scores"), k + 1)

            dve.wait_ge(sem("sums_cleared"), 1)

            EDGE_STEPS = 4 * NB

            def edge_block(it, t, with_hist):
                n = [0]

                def step(ins):
                    n[0] += 1
                    ins.then_inc(sem("dve_edge"), 1)

                def settle():
                    dve.wait_ge(sem("dve_edge"), it * EDGE_STEPS + n[0])

                for a in range(NB):
                    b = a % 2
                    dve.wait_ge(sem(f"rows_in{a}"), it * (32 * EB) + 32 * EB)
                    dve.wait_ge(sem("const0"), 3)
                    e1, e2, e3 = (es[:, b, k, :, :] for k in range(3))
                    step(V.tensor_tensor(e1, gs[:, a, :, 0:HEADS], gd[:, a, :, 0:HEADS], ALU.add))
                    settle()
                    step(V.scalar_tensor_tensor(out=e2, in0=e1, scalar=SLOPE, in1=e1, op0=ALU.mult, op1=ALU.max))
                    settle()
                    V.tensor_tensor(e3, e2, gd[:, a, :, HEADS:FD], ALU.subtract).then_inc(sem("edge_scores"), 1)
                    if with_hist:
                        for h in range(HB):
                            dve.wait_ge(sem("hist_used"), it * (HB * NB) + (a * HB + h + 1))
                            c = t * (NB * HB * HC) + (a * HB + h) * HC
                            V.tensor_tensor(hist_hi[h], bc(dhi_h[:, bass.ds(c, HC)], 1, P), iota_h[:, :, :],
                                            ALU.is_equal).then_inc(sem("hist_made"), 1)
                            V.tensor_tensor(hist_lo[h], bc(dlo_h[:, bass.ds(c, HC)], 1, LO), iota_h[:, 0:LO, :],
                                            ALU.is_equal).then_inc(sem("hist_made"), 1)
                    dve.wait_ge(sem("prod_used"), nth(it, a))
                    c0 = t * ITC + a * EB
                    step(V.tensor_tensor(one_hi[:, b, :, :], bc(dhi[:, bass.ds(c0, EB)], 2, P), bc(iota[:, :], 1, EB),
                                         ALU.is_equal))
                    step(V.tensor_tensor(one_lo[:, b, :, :], bc(dlo[:, bass.ds(c0, EB)], 2, LO),
                                         bc(iota[:, 0:LO], 1, EB), ALU.is_equal))
                    dve.wait_ge(sem("edge_exps"), nth(it, a))
                    v = val[:, b, :, :]
                    V.tensor_tensor(v[:, :, 0:F0].rearrange("p j (h e) -> p j h e", e=NE0),
                                    gs[:, a, :, HEADS:FS].rearrange("p j (h e) -> p j h e", e=NE0),
                                    bc(v[:, :, F0:FV], 3, NE0), ALU.mult).then_inc(sem("rows_used"), 1)
                    settle()
                    dve.wait_ge(sem("rows_used"), nth(it, a) + NB)
                    V.tensor_tensor(prod[:, b, :, :, :], bc(one_lo[:, b, :, :], 2, FV), bc(v, 3, LO), ALU.mult)\
                        .then_inc(sem("prod_made"), 1)
                assert n[0] == EDGE_STEPS

            with V.Fori(0, ITERS) as t:
                edge_block(t, t, True)
            left = V.value_load(flagi[0:1, 0:1], min_val=0, max_val=1)
            with V.If(left > 0):
                with V.Fori(0, REST) as g:
                    for n, ins in enumerate(decode(GC + g * GC)):
                        if n < DECODE_STEPS:
                            ins.then_inc(sem("rest_steps"), 1)
                            dve.wait_ge(sem("rest_steps"), g * DECODE_STEPS + (n + 1))
                    ins.then_inc(sem("decoded"), 1)
                    dve.wait_ge(sem("decoded"), g + 2)
                    V.sem_inc(sem("decode_seen"), 1)
                    with V.Fori(0, ITERS) as t:
                        edge_block((g + 1) * ITERS + t, t, False)

            dve.wait_ge(sem("node_exps"), 2)
            h_self, h_last = tab_s[:, :, HEADS:FS], last[:, HEADS:FS]

            def by_head(ap):
                return ap.rearrange("p t (h e) -> p t h e", e=NE0)

            dve.wait_ge(sem("sums_made"), 1)
            for k in range(2):
                V.tensor_copy(num[:, 0, :, FH * k:FH * (k + 1)], PS[:, k, 0:FH * LO].rearrange("p (f t) -> p t f", t=LO))
            ins = V.tensor_tensor(nod[:, 3, :, :], nod[:, 3, :, :], bc(PS[:, 2, 0:LO], 2, HEADS), ALU.mult)
            ins.then_inc(sem("sums_read"), 1)
            dve.wait_ge(sem("sums_read"), 1)
            then(V.tensor_tensor(by_head(num[:, 1, :, 0:F0]), by_head(h_self), bc(nod[:, 2, :, :], 3, NE0), ALU.mult))
            then(V.tensor_tensor(num[:, 0, :, 0:F0], num[:, 0, :, 0:F0], num[:, 1, :, 0:F0], ALU.add))
            then(V.tensor_tensor(by_head(num[:, 1, :, 0:F0]), by_head(bc(h_last, 1, NT)), bc(nod[:, 3, :, :], 3, NE0),
                                 ALU.mult))
            then(V.tensor_tensor(num[:, 0, :, 0:F0], num[:, 0, :, 0:F0], num[:, 1, :, 0:F0], ALU.add))
            then(V.tensor_tensor(num[:, 0, :, F0:FV], num[:, 0, :, F0:FV], nod[:, 2, :, :], ALU.add))
            then(V.scalar_tensor_tensor(out=num[:, 0, :, F0:FV], in0=num[:, 0, :, F0:FV], scalar=1e-16,
                                        in1=nod[:, 3, :, :], op0=ALU.add, op1=ALU.add))
            then(V.reciprocal(nod[:, 4, :, :], num[:, 0, :, F0:FV]))
            then(V.tensor_tensor(by_head(num[:, 0, :, 0:F0]), by_head(num[:, 0, :, 0:F0]), bc(nod[:, 4, :, :], 3, NE0),
                                 ALU.mult))
            agg = num[:, 0, :, 0:F0]
            tmp = num[:, 1, :, 0:F0]
            then(V.tensor_tensor(agg, agg, bc(gat_rows[:, 0, :], 1, NT), ALU.add))
            then(V.tensor_reduce(red[:, 0, :], agg, X, ALU.add))
            then(V.tensor_scalar(red[:, 1, :], red[:, 0, :], -1.0 / F0, None, ALU.mult))
            then(V.tensor_tensor(agg, agg, bc(red[:, 1, :], 2, F0), ALU.add))
            then(V.tensor_tensor(tmp, agg, agg, ALU.mult))
            then(V.tensor_reduce(red[:, 0, :], tmp, X, ALU.add))
            V.tensor_scalar(red[:, 2, :], red[:, 0, :], 1.0 / F0, LN_EPS, ALU.mult, ALU.add).then_inc(sem("gat_var"), 1)
            dve.wait_ge(sem("gat_rstd"), 1)
            then(V.tensor_tensor(agg, agg, bc(red[:, 3, :], 2, F0), ALU.mult))
            then(V.tensor_tensor(agg, agg, bc(gat_rows[:, 1, :], 1, NT), ALU.mult))
            then(V.tensor_tensor(agg, agg, bc(gat_rows[:, 2, :], 1, NT), ALU.add))
            then(V.tensor_reduce(sc[:, 0, :, 0:NE0], agg.rearrange("p t (h e) -> p t e h", e=NE0), X, ALU.add))
            then(V.tensor_scalar(sc[:, 0, :, 0:NE0], sc[:, 0, :, 0:NE0], 1.0 / HEADS, None, ALU.mult))

            def gates(n, N, s1, s2, parts=False):
                s = sc[:, 0, :, 0:N]
                over = s1.rearrange("p (t e j) -> p t e j", e=N, j=N)
                same = s2.rearrange("p (t e j) -> p t e j", e=N, j=N)
                V.tensor_tensor(over, bc(s, 2, N), bc(s, 3, N), ALU.is_gt)
                then(V.tensor_tensor(same, bc(s, 2, N), bc(s, 3, N), ALU.is_equal))
                then(V.tensor_tensor(same, same, bc(before[:, 0:N, 0:N], 1, NT), ALU.mult))
                then(V.tensor_tensor(over, over, same, ALU.add))
                then(V.tensor_reduce(sc[:, 3, :, 0:N], over, X, ALU.add))
                then(V.tensor_reduce(red[:, 4, :], s, X, ALU.max))
                V.tensor_tensor(sc[:, 1, :, 0:N], s, bc(red[:, 4, :], 2, N), ALU.subtract).then_inc(sem(f"gate_in{n}"), 1)
                dve.wait_ge(sem(f"gate_exp{n}"), 1)
                then(V.scalar_tensor_tensor(out=sc[:, 2, :, 0:N], in0=sc[:, 3, :, 0:N], scalar=1.5,
                                            in1=sc[:, 2, :, 0:N], op0=ALU.is_lt, op1=ALU.mult))
                then(V.tensor_reduce(red[:, 5, :], sc[:, 2, :, 0:N], X, ALU.add))
                then(V.reciprocal(red[:, 6, :], red[:, 5, :]))
                g = sc[:, 3, :, 0:N]
                then(V.tensor_tensor(g, sc[:, 2, :, 0:N], bc(red[:, 6, :], 2, N), ALU.mult))
                if parts:
                    then(V.tensor_copy(gparts[:, :, 0, :], g))
                    then(V.tensor_tensor(sc[:, 1, :, :], g, gparts[:, :, 0, :], ALU.subtract))
                    then(V.tensor_copy(gparts[:, :, 1, :], sc[:, 1, :, :]))
                    V.tensor_tensor(gparts[:, :, 2, :], sc[:, 1, :, :], gparts[:, :, 1, :], ALU.subtract)\
                        .then_inc(sem("gates1"), 1)

            dve.wait_ge(sem("before_made"), 1)
            gate_tmp = num[:, :, :, :].rearrange("p a t f -> p (a t f)")
            gates(0, NE0, gate_tmp[:, 0:512], gate_tmp[:, 512:1024])
            dve.wait_ge(sem("oute_made"), ITERS * XT0 // P)
            then(V.tensor_tensor(oute[:, :, :, :], oute[:, :, :, :], bc(sc[:, 3, :, 0:NE0], 3, C), ALU.mult))
            then(V.tensor_reduce(sq[:, :, :], oute[:, :, :, :].rearrange("p t e c -> p t c e"), X, ALU.add))

            def add_experts(q):
                T8 = slice(QT * q, QT * (q + 1))
                then(V.tensor_tensor(xt[:, T8, :], xt[:, T8, :], sq[:, T8, :], ALU.add))

            dve.wait_ge(sem("layer1_weights_in"), 144)
            then(V.tensor_scalar(gn1[:, :], gn1[:, :], float(C) ** 0.5, None, ALU.mult))
            then(V.tensor_scalar(go1[:, :], go1[:, :], float(C) ** 0.5, None, ALU.mult))
            layer_norm("ln2", LN_C_EPS, add_experts, "ln2_centred")
            for q in range(NQ):
                dve.wait_ge(sem("ln2_centred"), q + 1)
                squares(q, xn, "ln2r", 1.0, RMS_EPS)
            for q in range(NQ):
                scaled(q, "ln2r", "ln2_xn")
            for u in range(8):
                dve.wait_ge(sem("q_made"), u + 1)
                if u >= 4:
                    dve.wait_ge(sem("q_turned"), u - 3)
                src = PS[:, u % 2, :].rearrange("p (k d) -> p k d", d=HEAD_DIM)
                then(V.tensor_reduce(red[:, 4, 0:16], src, X, ALU.max))
                V.tensor_tensor(qe(u), src, bc(red[:, 4, 0:16], 2, HEAD_DIM), ALU.subtract).then_inc(sem("q_shifted"), 1)
                dve.wait_ge(sem("q_exp"), u + 1)
                then(V.tensor_reduce(red[:, 5, 0:16], qe(u), X, ALU.add))
                then(V.reciprocal(red[:, 6, 0:16], red[:, 5, 0:16]))
                V.tensor_tensor(qe(u), qe(u), bc(red[:, 6, 0:16], 2, HEAD_DIM), ALU.mult).then_inc(sem("q_soft"), 1)
            pixel_attention("c1", 1, gn1[:, 0:1])
            for q in range(NQ):
                dve.wait_ge(sem("c1_out"), q + 1)
                T8 = slice(QT * q, QT * (q + 1))
                then(V.tensor_tensor(xn[:, T8, :], PS[:, q, :].rearrange("p (t c) -> p t c", c=C),
                                     bc(bo1[:, :], 1, QT), ALU.add))
                squares(q, xn, "ln3r", 1.0, RMS_EPS)
            for q in range(NQ):
                scaled(q, "ln3r", "z_scaled")

            def add_attention1(q):
                dve.wait_ge(sem("z_scaled"), q + 1)
                T8 = slice(QT * q, QT * (q + 1))
                then(V.tensor_tensor(sq[:, T8, :], xn[:, T8, :], bc(go1[:, :], 1, QT), ALU.mult))
                then(V.tensor_tensor(xt[:, T8, :], xt[:, T8, :], sq[:, T8, :], ALU.add))

            layer_norm("ln4", LN_T_EPS, add_attention1, after=lambda q: V.memset(red[:, 7, 0:1], 0.0)
                       .then_inc(sem("ln4_sum"), 1))
            for q in range(NQ):
                T8 = slice(QT * q, QT * (q + 1))
                dve.wait_ge(sem("ln4_xn"), q + 1)
                V.tensor_copy(xs[:, T8, 2, :], xn[:, T8, :])
                then(V.tensor_copy(xs[:, T8, 0, :], xn[:, T8, :]))
                then(V.tensor_tensor(sq[:, T8, :], xn[:, T8, :], xs[:, T8, 0, :], ALU.subtract))
                then(V.tensor_copy(xs[:, T8, 1, :], sq[:, T8, :]))
                V.tensor_tensor(xs[:, T8, 3, :], sq[:, T8, :], xs[:, T8, 1, :], ALU.subtract).then_inc(sem("xs_made"), 1)

            dve.wait_ge(sem("logits_made"), 1)
            then(V.tensor_tensor(sc[:, 0, :, :], PS[:, 7, 0:NE1 * NT].rearrange("p (t e) -> p t e", e=NE1),
                                 bc(bgb[:, :], 1, NT), ALU.add))
            gates(1, NE1, big[:, 0:2048], big[:, 2048:4096], parts=True)

            def last_sum(n):
                dve.wait_ge(sem("h1_used"), NE1 * NH1 * (n + 1))
                y = ob[0:C, 512 * n:512 * (n + 1)]
                V.tensor_tensor(y, y, PS[0:C, 5 + n % 2, :], ALU.add).then_inc(sem("y_made"), 1)

            for m in range(8 * NE1 * NH1):
                dve.wait_ge(sem("h1_gelu"), m + 1)
                dve.wait_ge(sem("g_spread"), m // NH1 + 1)
                h = ring[:, m % RING, :]
                V.tensor_tensor(h, h, PS[:, 3 + (m // NH1) % 2, :], ALU.mult).then_inc(sem("h1_gated"), 1)
                n, k = m // (NE1 * NH1), m % (NE1 * NH1)
                if n >= 1 and k == 6 or m == 8 * NE1 * NH1 - 1:
                    last_sum(n - 1 if m < 8 * NE1 * NH1 - 1 else n)


def leaky_steps(V, dst, tmp, a, b, guard):
    return (lambda: V.tensor_tensor(tmp, a, b, ALU.add),
            lambda: V.scalar_tensor_tensor(out=tmp, in0=tmp, scalar=SLOPE, in1=tmp, op0=ALU.mult, op1=ALU.max),
            lambda: V.tensor_tensor(dst, tmp, guard, ALU.subtract))


_INS = ['x', 'L0_conv_w_qkv', 'L0_conv_w_out', 'L0_conv_b_out', 'L0_ffn_W_gat', 'L0_ffn_att_src', 'L0_ffn_att_dst',
        'L0_ffn_b_gat', 'L0_ffn_ln_gamma', 'L0_ffn_ln_beta', 'L0_ffn_W1', 'L0_ffn_b1', 'L0_ffn_W2', 'L0_ffn_b2',
        'L0_ffn_edge_index', 'L1_conv_W_qkv', 'L1_conv_W_out', 'L1_conv_b_out', 'L1_conv_g_norm', 'L1_conv_g_out',
        'L1_ffn_Wg', 'L1_ffn_bg', 'L1_ffn_W1', 'L1_ffn_b1', 'L1_ffn_W2', 'L1_ffn_b2']


def kernel(**inputs):
    import numpy as _np
    import concourse.bacc as _bacc
    from concourse.bass_utils import run_bass_kernel_spmd as _run

    nc = _bacc.Bacc("TRN2", target_bir_lowering=False, num_devices=1)
    arrays, args = {}, []
    for name in _INS:
        a = _np.ascontiguousarray(inputs[name])
        arrays[f"in_{name}_dram"] = a
        args.append(nc.dram_tensor(f"in_{name}_dram", a.shape, mybir.dt.from_np(a.dtype), kind="ExternalInput").ap())
    out = nc.dram_tensor("out_0_dram", (B, C, 16, 16), F32, kind="ExternalOutput").ap()
    table_s = nc.dram_tensor("table_s_dram", (NODES, FS), F32, kind="Internal").ap()
    table_d = nc.dram_tensor("table_d_dram", (NODES, FD), F32, kind="Internal").ap()
    metaformer(nc, args, table_s, table_d, out)
    r = _run(nc, [arrays], core_ids=[0])
    return r.results[0]["out_0_dram"]
```

```python
from contextlib import ExitStack

import concourse.bass as bass
from concourse import mybir

F32 = mybir.dt.float32
BF16 = mybir.dt.bfloat16
I32 = mybir.dt.int32
ALU = mybir.AluOpType
ACT = mybir.ActivationFunctionType
X = mybir.AxisListType.X
RMAX = bass.bass_isa.ReduceOp.max

P = 128
B, C, HW = 16, 64, 256
NODES = B * HW
NT = NODES // P
QT = 8
NQ = NT // QT
QB = 4
HEADS, NE0 = 4, 4
F0 = HEADS * NE0
HID0 = 128
NE1, HID1 = 8, 256
NH1 = HID1 // P
RING = 12
NEDGE = 262144
EC = NEDGE // P
TOP = 8
ROUNDS = (2,) * 8 + (1,) * 5
GC = sum(ROUNDS) * TOP
EB = 7
NB = 6
ITC = NB * EB
RB = 3
ITERS = GC // ITC
REST = -(-EC // GC)
HC = 16
HB = 5
HI = NB * HB
HP = EC // HC - ITERS * HI
XT0 = 512
G0 = NODES // XT0 // ITERS
OT = XT0 // P
LO = NODES // P
FV = F0 + HEADS
FS = HEADS + F0
FD = 2 * HEADS
FH = FV // 2
HEAD_DIM = 32
LN_C_EPS, LN_T_EPS, LN_EPS, RMS_EPS = 1e-6, 1e-5, 1e-5, 1e-12
SLOPE = 0.2


def metaformer(nc, ins, table_s, table_d, out):
    (x, w_qkv0, w_out0, b_out0, W_gat, att_src, att_dst, b_gat, ln_gamma, ln_beta, W1_0, b1_0, W2_0, b2_0,
     edges, w_qkv1, w_out1, b_out1, g_norm, g_out, Wg, bg, W1_1, b1_1, W2_1, b2_1) = ins

    with ExitStack() as ctx:
        def sb(name, shape, dt=F32):
            return ctx.enter_context(nc.sbuf_tensor(name, shape, dt))

        sems = {}

        def sem(name):
            if name not in sems:
                sems[name] = ctx.enter_context(nc.semaphore(name))
            return sems[name]

        PS = ctx.enter_context(nc.psum_tensor("PS", [P, 8, 512], F32))
        ident = sb("ident", [P, P])
        ident_b = sb("ident_b", [P, P], BF16)
        zeros = sb("zeros", [P, FH * LO])
        ones = sb("ones", [3, P], BF16)
        b2row = sb("b2row", [3, NE0 * C])
        b2bias = sb("b2bias", [3, NE0 * C], BF16)
        iota_i = sb("iota_i", [P, P], I32)
        iota = sb("iota", [P, P])
        iota_h = sb("iota_h", [P, P, HC], BF16)
        blocks = sb("blocks", [P, P])
        mhalf = sb("mhalf", [P, NT])
        wkv0 = sb("wkv0", [P, 4, C])
        wq0 = sb("wq0", [P, 2, C])
        wqkv1 = sb("wqkv1", [P, 3, C])
        wo0 = sb("wo0", [C, 256])
        wo1 = sb("wo1", [C, P])
        b1r0 = sb("b1r0", [NE0, P])
        b1r1 = sb("b1r1", [NE1 * NH1, P])
        wkvT0 = sb("wkvT0", [C, 512])
        wqkvT1 = sb("wqkvT1", [C, 384])
        cols = sb("cols", [P, 3 * C + NE0 + NE1 * NH1])
        woT0 = cols[:, 0:2 * C].rearrange("p (g c) -> p g c", g=2)
        woT1 = cols[:, 2 * C:3 * C].rearrange("p (g c) -> p g c", g=1)
        b1c0 = cols[:, 3 * C:3 * C + NE0]
        b1c1 = cols[:, 3 * C + NE0:]
        wgat = sb("wgat", [C, FS + HEADS])
        attr = sb("attr", [C, 2, F0])
        attm = sb("attm", [C, 2, F0])
        w1_0 = sb("w1_0", [C, NE0, HID0])
        w2_0 = sb("w2_0", [HID0, NE0, C])
        b2x3 = sb("b2x3", [3 * NE1, C])
        b2s = sb("b2s", [3 * NE1, 3, C], BF16)
        pick = sb("pick", [3 * NE1, NE1, P], BF16)
        wg_s = sb("wg_s", [P, 3, NE1], BF16)
        rsc = sb("rsc", [P, 2, 512])
        b2rest = rsc[0:3, 0, 0:NE0 * C]
        b2parts = rsc[0:3, 1, 0:NE0 * C * 3 // 2].bitcast(BF16).rearrange("p (k n) -> p k n", k=3)
        gparts = sb("gparts", [P, NT, 3, NE1], BF16)
        wg = sb("wg", [P, NE1])
        bgb = sb("bgb", [P, NE1])
        bo0 = sb("bo0", [P, C])
        bo1 = sb("bo1", [P, C])
        go1 = sb("go1", [P, C])
        gn1 = sb("gn1", [C, 1])
        gat_rows = sb("gat_rows", [P, 3, F0])
        xt = sb("xt", [P, NT, C])
        xn = sb("xn", [P, NT, C])
        sq = sb("sq", [P, NT, C])
        num = sb("num", [P, 2, NT, FV])
        red = sb("red", [P, 8, NT])
        xca = sb("xca", [P, NODES])
        xc = xca[0:C, :]
        xst = xca[:, :].bitcast(BF16).rearrange("p (a n) -> p a n", a=2)
        nmx = sb("nmx", [P, 8, QB])
        ksum = sb("ksum", [P, 2, B])
        rks = sb("rks", [P, 2, B])
        big = sb("big", [P, 12800])
        oute = sb("oute", [P, NT, NE0, C])
        wide = oute[:, :, :, :].rearrange("p t e c -> p (t e c)")
        Ys = [wide[0:C, 4096 * k:4096 * (k + 1)].rearrange("p (g b n) -> p g b n", g=2, b=B) for k in range(2)]
        ek = big[:, 0:2048].rearrange("p (a n) -> p a n", a=2)
        ekt = big[:, 2048:4096].rearrange("p (a t n) -> p a t n", a=2, t=QT)
        ctxT = big[:, 4096:8192].rearrange("p (g b n) -> p g b n", g=2, b=B)
        T = big[:, 8192:10240].rearrange("p (g b n) -> p g b n", g=2, b=B)
        MT = big[0:C, 0:1024].rearrange("p (b n) -> p b n", b=B)
        qc = wide[:, 0:4096]
        prod = big[:, 0:2 * EB * FV * LO].rearrange("p (a j f l) -> p a j f l", a=2, j=EB, f=FV)
        hoff = 2 * EB * FV * LO
        hw = (P + LO) * HC // 2
        free = [big[:, hoff + hw * k:hoff + hw * (k + 1)] for k in range(3)]
        free += [sq[:, :, :].rearrange("p t c -> p (t c)")[:, 0:hw], num[:, :, :, :].rearrange("p a t f -> p (a t f)")]
        assert len(free) == HB
        hist = [f.bitcast(BF16).rearrange("p (h c) -> p h c", c=HC) for f in free]
        hist_hi, hist_lo = [h[:, 0:P, :] for h in hist], [h[:, P:, :] for h in hist]
        rings = [big[:, 512 * k:512 * (k + 1)] for k in range(8)] + [wide[:, 4096 + 512 * k:4096 + 512 * (k + 1)]
                                                                     for k in range(RING - 8)]
        ob = big[:, 4096:8192]
        w1s = big[:, 9216:12288].bitcast(BF16).rearrange("p (a n) -> p a n", a=3)
        gT = wide[0:3 * NE1, 6144:8192].bitcast(BF16)
        xs = wide[:, 0:4096].bitcast(BF16).rearrange("p (t a c) -> p t a c", t=NT, a=4)
        keys = sb("keys", [P, GC * (1 + REST)])
        rows = keys[:, GC:GC + EC]
        big2 = sb("hist_dst", [P, EC // 2])
        dhi_h = big2[:, :].bitcast(BF16)
        dlo_h = sb("dlo_h", [P, EC], BF16)
        w1_1 = keys[:, 0:NE1 * HID1]
        w2_1 = big2[:, :].rearrange("p (e k n) -> p e k n", e=NE1, k=NH1)
        ebi = big[:, 8192:12288].bitcast(I32).rearrange("p (a n) -> p a n", a=2)
        live, key2 = wide[:, 2 * EC:3 * EC], wide[:, 3 * EC:]
        dec = sb("dec", [P, 2, GC])
        deci = sb("deci", [P, 3, GC], I32)
        idx = sb("idx", [P, 2, GC], I32)
        idx_s, idx_d = idx[:, 0, :], idx[:, 1, :]
        dhi = sb("dhi", [P, GC])
        dlo = sb("dlo", [P, GC])
        stage = sb("stage", [P, RB, 2, EB], I32)
        flagf = sb("flagf", [P, 2])
        flagi = sb("flagi", [P, 1], I32)
        tab_s = sb("tab_s", [P, NT, FS])
        tab_d = sb("tab_d", [P, NT, FD])
        gmax = sb("gmax", [P, 2, HEADS])
        last = sb("last", [P, FS])
        gs = sb("gs", [P, RB, EB, FS])
        gd = sb("gd", [P, RB, EB, FD])
        es = sb("es", [P, 2, 3, EB, HEADS])
        val = sb("val", [P, 2, EB, FV])
        one_hi = sb("one_hi", [P, 2, EB, P])
        one_lo = sb("one_lo", [P, 2, EB, LO])
        nod = sb("nod", [P, 6, NT, HEADS])
        cnt = sb("cnt", [P, NT])
        sc = sb("sc", [P, 4, NT, NE1])
        hid0 = xn[:, 0:XT0 * NE0 // C, :].rearrange("p t c -> p (t c)").rearrange("p (e n) -> p e n", e=NE0)

        block = ctx.enter_context(nc.Block())

        def turned(j):
            return PS[:, 2 + j % 4, 0:256].bitcast(BF16)

        def gates_turned(k):
            return PS[0:3 * NE1, 7 - k % 2, :].bitcast(BF16)

        def queries(u):
            return PS[:, (0, 1, 4)[u % 3], :]

        def qe(u):
            return big[:, 4096 + 512 * (u % 4):4096 + 512 * (u % 4 + 1)].rearrange("p (k d) -> p k d", d=HEAD_DIM)

        def bc(ap, axis, n):
            a = ap.unsqueeze(axis)
            shape = list(a.shape)
            shape[axis] = n
            return a.broadcast_to(shape)

        def nth(it, a):
            return it * NB + (a + 1)

        def row(v, n=P):
            return v.unsqueeze(0).broadcast_to([n, v.shape[0]])

        @block.sync
        def _(sp):
            ei = edges.rearrange("a (p n) -> p a n", p=P)
            sp.dma_start(xc.rearrange("c (b n) -> c b n", b=B),
                         x.rearrange("b c h w -> c b (h w)")).then_inc(sem("x_in"), 16)
            sp.dma_start(ebi, ei).then_inc(sem("edges_in"), 16)
            n = 0
            for dst, src in (
                (wkv0[:, :, :], w_qkv0[256:768, :].rearrange("(g p) c -> p g c", p=P)),
                (wq0[:, :, :], w_qkv0[0:256, :].rearrange("(g p) c -> p g c", p=P)),
                (wqkv1[:, :, :], w_qkv1.rearrange("(g p) c -> p g c", p=P)),
                (wo0[:, :], w_out0), (wo1[:, :], w_out1),
                (b1r0[:, :], b1_0), (b1r1[:, :], b1_1.rearrange("e (k n) -> (e k) n", n=P)),
                (bo0[:, :], row(b_out0)),
            ):
                sp.dma_start(dst, src).then_inc(sem("conv_weights_in"), 16)
                n += 1
            assert n == 8
            for dst, src in (
                (wgat[:, HEADS:FS], W_gat),
                (attr[:, 0, :], row(att_src.rearrange("a b -> (a b)"), C)),
                (attr[:, 1, :], row(att_dst.rearrange("a b -> (a b)"), C)),
                (w1_0[:, :, :], W1_0.rearrange("e c n -> c e n")),
                (w2_0[:, :, :], W2_0.rearrange("e n c -> n e c")),
                (b2row[:, :], row(b2_0.rearrange("e c -> (e c)"), 3)),
                (gat_rows[:, 0, :], row(b_gat)), (gat_rows[:, 1, :], row(ln_gamma)),
                (gat_rows[:, 2, :], row(ln_beta)),
            ):
                sp.dma_start(dst, src).then_inc(sem("ffn0_weights_in"), 16)
                n += 1
            assert n == 17
            for dst, src in (
                (b2x3[0:NE1, :], b2_1), (b2x3[NE1:2 * NE1, :], b2_1), (b2x3[2 * NE1:, :], b2_1),
                (wg[0:C, :], Wg), (wg[C:P, :], Wg), (bgb[:, :], row(bg)),
                (bo1[:, :], row(b_out1)), (go1[:, :], row(g_out)),
                (gn1[:, :], g_norm.unsqueeze(1)),
            ):
                sp.dma_start(dst, src).then_inc(sem("layer1_weights_in"), 16)
                n += 1
            assert n == 26
            sp.wait_ge(sem("tables_made"), 1)
            sp.dma_start(table_s.rearrange("(t p) f -> p t f", p=P), tab_s[:, :, :]).then_inc(sem("tables_out"), 16)
            sp.dma_start(table_d.rearrange("(t p) f -> p t f", p=P), tab_d[:, :, :]).then_inc(sem("tables_out"), 16)
            sp.wait_ge(sem("tables_out"), 32)
            sp.dma_start(last[:, :], table_s[NODES - 1:NODES, :].broadcast_to([P, FS])).then_inc(sem("last_in"), 16)
            sp.wait_ge(sem("sums_read"), 1)
            for h in range(2):
                sp.dma_start(w1_1[C * h:C * (h + 1), :].rearrange("p (e n) -> p e n", e=NE1),
                             W1_1.rearrange("e c n -> c e n")).then_inc(sem("experts1_in"), 16)
            sp.dma_start(w2_1.rearrange("p e k c -> p (e k) c"), W2_1.rearrange("e (k p) c -> p (e k) c", p=P))\
                .then_inc(sem("experts1_in"), 16)
            for q in range(8):
                sp.wait_ge(sem("y_made"), q + 1)
                sp.dma_start(out.rearrange("b c h w -> c b (h w)")[:, 2 * q:2 * q + 2, :],
                             ob[0:C, 512 * q:512 * (q + 1)].rearrange("c (b n) -> c b n", b=2)).then_inc(sem("y_out"), 16)
            sp.wait_ge(sem("y_out"), 128)

        @block.gpsimd
        def _(pool):
            nc.gpsimd.memset(ident[:, :], 0.0).then_inc(sem("const0"), 1)
            nc.gpsimd.iota(iota_i[:, :], [[1, P]], base=0, channel_multiplier=0).then_inc(sem("const0"), 1)
            nc.gpsimd.memset(zeros[:, :], 0.0).then_inc(sem("zeros_made"), 1)
            nc.gpsimd.memset(ones[:, :], 1.0).then_inc(sem("ones_made"), 1)
            nc.gpsimd.memset(pick[:, :, :], 0.0).then_inc(sem("pick_steps"), 1)
            nc.gpsimd.memset(keys[:, GC + EC:], 0.0).then_inc(sem("pad_made"), 1)
            nc.gpsimd.memset(mhalf[:, :], -0.5).then_inc(sem("zeros_made"), 1)
            pool.wait_ge(sem("const0"), 2)
            nc.gpsimd.affine_select(out=ident[:, :], in_=ident[:, :], compare_op=ALU.not_equal, fill=1.0, base=0,
                                    pattern=[[-1, P]], channel_multiplier=1).then_inc(sem("ident_made"), 1)
            for k in range(3):
                pool.wait_ge(sem("pick_steps"), k + 1)
                nc.gpsimd.affine_select(out=pick[:, :, :], in_=pick[:, :, :], compare_op=ALU.not_equal, fill=1.0,
                                        base=-NE1 * k, pattern=[[-1, NE1], [0, P]], channel_multiplier=1)\
                    .then_inc(sem("pick_steps"), 1)

            def split_weights():
                ws = [0]

                def split_step(ins):
                    ws[0] += 1
                    ins.then_inc(sem("split_steps"), 1)
                    pool.wait_ge(sem("split_steps"), ws[0])

                def split(src, n, parts, r0, r1):
                    split_step(nc.gpsimd.tensor_copy(parts[0], src))
                    split_step(nc.gpsimd.tensor_tensor(r0, src, parts[0], ALU.subtract))
                    split_step(nc.gpsimd.tensor_copy(parts[1], r0))
                    split_step(nc.gpsimd.tensor_tensor(r1, r0, parts[1], ALU.subtract))
                    split_step(nc.gpsimd.tensor_copy(parts[2], r1))

                pool.wait_ge(sem("layer1_weights_in"), 144)
                n3 = 3 * NE1
                split(b2x3[:, :], C, [b2s[:, k, :] for k in range(3)], rsc[0:n3, 0, 0:C], rsc[0:n3, 1, 0:C])
                split(wg[:, :], NE1, [wg_s[:, k, :] for k in range(3)], rsc[:, 0, 0:NE1], rsc[:, 1, 0:NE1])
                split_step(nc.gpsimd.tensor_copy(wg_s[C:P, 2, :], wg_s[C:P, 0, :]))
                pool.wait_ge(sem("experts1_in"), 48)
                for k in range(4):
                    cs = slice(512 * k, 512 * (k + 1))
                    split(w1_1[:, cs], 512, [w1s[:, j, cs] for j in range(3)], rsc[:, 0, :], rsc[:, 1, :])
                    split_step(nc.gpsimd.tensor_copy(w1s[C:P, 2, cs], w1s[C:P, 0, cs]))
                nc.gpsimd.memset(rsc[:, 0, 0:1], 0.0).then_inc(sem("weights_split"), 1)

            ps = [0]

            def pool_step(ins):
                ps[0] += 1
                ins.then_inc(sem("pool_steps"), 1)
                pool.wait_ge(sem("pool_steps"), ps[0])

            def inverse_roots(stage, scale, eps):
                for q in range(NQ):
                    pool.wait_ge(sem(f"{stage}_sq"), q + 1)
                    ss, var, r = (red[:, k, QT * q:QT * (q + 1)] for k in (0, 2, 3))
                    pool_step(nc.gpsimd.tensor_scalar(var, ss, scale, eps, ALU.mult, ALU.add))
                    nc.gpsimd.tensor_tensor(r, var, mhalf[:, 0:QT], ALU.pow).then_inc(sem(f"{stage}_rstd"), 1)

            pool.wait_ge(sem("zeros_made"), 2)
            inverse_roots("ln0", 1.0 / C, LN_C_EPS)
            pool.wait_ge(sem("conv_weights_in"), 128)
            nc.gpsimd.tensor_tensor(xt[:, :, :], xt[:, :, :], bc(bo0[:, :], 1, NT), ALU.add).then_inc(sem("bias_added"), 1)
            pool.wait_ge(sem("keys_made"), 1)
            ts, big_int = nc.gpsimd.tensor_scalar, float(3 << 22)
            pool_step(ts(live, live, 256.0, None, ALU.mult))
            pool_step(nc.gpsimd.tensor_copy(key2, ebi[:, 1, :]))
            pool_step(nc.gpsimd.tensor_tensor(live, live, key2, ALU.add))
            pool_step(ts(key2, key2, 0.5 - P / 2, 1.0 / P, ALU.add, ALU.mult))
            pool_step(ts(key2, key2, big_int, None, ALU.add))
            pool_step(ts(dlo_h[:, :], key2, -big_int, None, ALU.add))
            pool_step(ts(key2, key2, -big_int, -float(P), ALU.add, ALU.mult))
            nc.gpsimd.tensor_tensor(dhi_h[:, :], live, key2, ALU.add).then_inc(sem("hist_indices"), 1)
            inverse_roots("ln1", 1.0 / C, LN_T_EPS)
            pool.wait_ge(sem("rest_max"), 1)
            nc.gpsimd.partition_all_reduce(flagf[:, 1:2], flagf[:, 0:1], P, RMAX).then_inc(sem("rest_all"), 1)
            pool.wait_ge(sem("score_max"), 1)
            nc.gpsimd.partition_all_reduce(gmax[:, 1, :], gmax[:, 0, :], P, RMAX).then_inc(sem("score_all"), 1)

            def gathers(it, t):
                for a in range(NB):
                    pool.wait_ge(sem("rows_used"), nth(it, a))
                    c0, r = t * ITC + a * EB, a % RB
                    nc.gpsimd.tensor_copy(stage[:, r, :, :], idx[:, :, bass.ds(c0, EB)]).then_inc(sem("staged"), 1)
                    pool.wait_ge(sem("staged"), nth(it, a))
                    nc.gpsimd.sem_inc(sem("staging_seen"), 1)
                    for j in range(EB):
                        nc.gpsimd.indirect_dma_start(
                            gs[:, r, j, :], None, table_s,
                            bass.IndirectOffsetOnAxis(stage[:, r, 0, j:j + 1], axis=0)).then_inc(sem(f"rows_in{r}"), 16)
                        nc.gpsimd.indirect_dma_start(
                            gd[:, r, j, :], None, table_d,
                            bass.IndirectOffsetOnAxis(stage[:, r, 1, j:j + 1], axis=0)).then_inc(sem(f"rows_in{r}"), 16)

            pool.wait_ge(sem("tables_out"), 32)
            pool.wait_ge(sem("decoded"), 1)
            with nc.gpsimd.Fori(0, ITERS) as t:
                gathers(t, t)
            pool.wait_ge(sem("flag_made"), 1)
            left = nc.gpsimd.value_load(flagi[0:1, 0:1], min_val=0, max_val=1)
            with nc.gpsimd.If(left > 0):
                with nc.gpsimd.Fori(0, REST) as g:
                    pool.wait_ge(sem("decoded"), g + 2)
                    nc.gpsimd.sem_inc(sem("staging_seen"), 1)
                    with nc.gpsimd.Fori(0, ITERS) as t:
                        gathers((g + 1) * ITERS + t, t)

            pool.wait_ge(sem("gat_var"), 1)
            nc.gpsimd.tensor_tensor(red[:, 3, :], red[:, 2, :], mhalf[:, :], ALU.pow).then_inc(sem("gat_rstd"), 1)
            inverse_roots("ln2", 1.0 + RMS_EPS / C, RMS_EPS * LN_C_EPS)
            split_weights()
            inverse_roots("ln3r", 1.0, RMS_EPS)
            inverse_roots("ln4", 1.0 / C, LN_T_EPS)

        @block.scalar
        def _(act):
            for q in range(NQ):
                act.wait_ge(sem("xt_turned"), q + 1)
                nc.scalar.copy(xt[:, QT * q:QT * (q + 1), :],
                               PS[:, q % 2, :].rearrange("p (t c) -> p t c", c=C)).then_inc(sem("xt_made"), 1)
            def squares(stage):
                for q in range(NQ):
                    act.wait_ge(sem(f"{stage}_centred"), q + 1)
                    for t in range(QT * q, QT * (q + 1)):
                        ins = nc.scalar.activation(sq[:, t, :], xn[:, t, :], ACT.Square, accum_out=red[:, 0, t:t + 1])
                    ins.then_inc(sem(f"{stage}_sq"), 1)

            squares("ln0")
            act.wait_ge(sem("weights_turned"), 3)
            nc.scalar.copy(wkvT0[:, :], PS[0:C, 4, :]).then_inc(sem("weights_made"), 1)
            nc.scalar.copy(wqkvT1[:, :], PS[0:C, 5, 0:384]).then_inc(sem("weights_made"), 1)
            nc.scalar.copy(cols[:, 0:3 * C], PS[:, 6, 0:3 * C]).then_inc(sem("weights_made"), 1)
            nc.scalar.copy(cols[:, 3 * C:], PS[:, 6, 3 * C:3 * C + NE0 + NE1 * NH1]).then_inc(sem("weights_made"), 1)

            def channel_major(stage, scale=None):
                for k in range(8):
                    act.wait_ge(sem(f"{stage}_turned"), k + 1)
                    src = PS[0:C, 6 + k % 2, :]
                    dst = xc[:, 512 * k:512 * (k + 1)]
                    if scale is None:
                        ins = nc.scalar.copy(dst, src)
                    else:
                        ins = nc.scalar.activation(dst, src, ACT.Copy, scale=scale)
                    ins.then_inc(sem(f"{stage}_xc"), 1)

            def pixel_softmax(L, G, yscale=1.0):
                N = NQ * G
                for u in range(N + 1):
                    v = u - 1
                    if u >= 1:
                        act.wait_ge(sem(f"{L}_kturned"), v + 1)
                        if v >= 2:
                            act.wait_ge(sem(f"{L}_ymade"), v - 1)
                        nc.scalar.copy(ekt[:, v % 2, 4:8, :], PS[:, 5, :].rearrange("p (t n) -> p t n", n=P))\
                            .then_inc(sem(f"{L}_ekt_a"), 1)
                    if u < N:
                        q, g = u // G, u % G
                        act.wait_ge(sem(f"{L}_kmax"), u + 1)
                        if u >= 2:
                            act.wait_ge(sem(f"{L}_kturned"), u - 1)
                        for b in range(QB):
                            bank = 2 * (u % 2) + b // 2
                            nc.scalar.activation(ek[:, u % 2, HW * b:HW * (b + 1)],
                                                 PS[:, bank, HW * (b % 2):HW * (b % 2 + 1)],
                                                 ACT.Exp, bias=nmx[:, u, b:b + 1],
                                                 accum_out=ksum[:, g, QB * q + b:QB * q + b + 1])\
                                .then_inc(sem(f"{L}_kexp"), 1)
                    if u >= 1:
                        q, g = v // G, v % G
                        act.wait_ge(sem(f"{L}_ymade"), v + 1)
                        nc.scalar.activation(Ys[L == "c1"][:, g, QB * q:QB * (q + 1), :],
                                             PS[0:C, 6, :].rearrange("p (b n) -> p b n", n=P), ACT.Copy, scale=yscale)\
                            .then_inc(sem(f"{L}_yv"), 1)

            channel_major("ln0")
            pixel_softmax("c0", 2)
            for h in range(2):
                act.wait_ge(sem("c0_mmade"), h + 1)
                nc.scalar.copy(MT[:, 8 * h:8 * (h + 1), :], PS[0:C, 6 + h, :].rearrange("p (b n) -> p b n", n=C))\
                    .then_inc(sem("c0_mt"), 1)
            squares("ln1")
            channel_major("ln1")

            for k in range(2):
                act.wait_ge(sem("node_scores"), k + 1)
                nc.scalar.activation(nod[:, 2 + k, :, :], nod[:, k, :, :], ACT.Exp).then_inc(sem("node_exps"), 1)

            def edge_exps(it, a):
                act.wait_ge(sem("edge_scores"), nth(it, a))
                act.wait_ge(sem("const0"), 2)
                nc.scalar.activation(val[:, a % 2, :, F0:FV], es[:, a % 2, 2, :, :], ACT.Exp)\
                    .then_inc(sem("edge_exps"), 1)

            with nc.scalar.Fori(0, ITERS) as t:
                for a in range(NB):
                    edge_exps(t, a)
                    g, part = a * G0 // NB, a % (NB // G0)
                    for e in range(2 * part, 2 * part + 2) if part < 2 else ():
                        act.wait_ge(sem("h0_made"), t * (NE0 * G0) + (NE0 * g + e + 1))
                        act.wait_ge(sem("const0"), 2)
                        nc.scalar.activation(hid0[:, e, :], PS[:, 3 + e % 2, 0:XT0], ACT.Gelu,
                                             bias=b1c0[:, e:e + 1]).then_inc(sem("h0_gelu"), 1)
                    for i in range(OT) if part == 2 else ():
                        act.wait_ge(sem("o0_made"), t * (OT * G0) + (OT * g + i + 1))
                        nc.scalar.copy(wide[:, bass.ds(t * (XT0 * 2 * G0) + (g * OT + i) * (NE0 * C), NE0 * C)],
                                       PS[:, 5 + i % 3, 0:NE0 * C]).then_inc(sem("oute_made"), 1)
            act.wait_ge(sem("flag_made"), 1)
            left = nc.scalar.value_load(flagi[0:1, 0:1], min_val=0, max_val=1)
            with nc.scalar.If(left > 0):
                with nc.scalar.Fori(0, REST) as g:
                    with nc.scalar.Fori(0, ITERS) as t:
                        for a in range(NB):
                            edge_exps((g + 1) * ITERS + t, a)

            act.wait_ge(sem("gate_in0"), 1)
            nc.scalar.activation(sc[:, 2, :, 0:NE0], sc[:, 1, :, 0:NE0], ACT.Exp).then_inc(sem("gate_exp0"), 1)

            squares("ln2")
            channel_major("ln2", gn1[:, 0:1])
            for u in range(8 + 1):
                if u < 8:
                    act.wait_ge(sem("q_shifted"), u + 1)
                    nc.scalar.activation(qe(u), qe(u), ACT.Exp).then_inc(sem("q_exp"), 1)
                if u >= 1:
                    act.wait_ge(sem("q_turned"), u)
                    nc.scalar.copy(qc[:, 512 * (u - 1):512 * u], PS[:, 2 + (u - 1) % 2, :]).then_inc(sem("qc_made"), 1)
            pixel_softmax("c1", 1, gn1[:, 0:1])

            squares("ln3r")
            squares("ln4")
            for j in range(16):
                k, a = j // 2, j % 2
                act.wait_ge(sem("xs_turned"), j + 1)
                nc.scalar.copy(xst[:, a, 512 * k:512 * (k + 1)], turned(j)).then_inc(sem("xst_made"), 1)

            def hidden_gelu(m):
                act.wait_ge(sem("h1_made"), m + 1)
                if m >= RING:
                    act.wait_ge(sem("h1_used"), m - RING + 1)
                k = m % (NE1 * NH1)
                nc.scalar.activation(rings[m % RING], PS[:, m % 3, :], ACT.Gelu,
                                     bias=b1c1[:, k:k + 1]).then_inc(sem("h1_gelu"), 1)

            for m in range(RING):
                hidden_gelu(m)
                if m < 8:
                    act.wait_ge(sem("x3_turned"), m + 1)
                    nc.scalar.copy(ob[0:C, 512 * m:512 * (m + 1)], PS[0:C, 5 + m % 2, :]).then_inc(sem("x3_made"), 1)
            act.wait_ge(sem("gate_in1"), 1)
            nc.scalar.activation(sc[:, 2, :, :], sc[:, 1, :, :], ACT.Exp).then_inc(sem("gate_exp1"), 1)

            def turned_gates(k):
                act.wait_ge(sem("g_turned"), k + 1)
                nc.scalar.copy(gT[:, 1024 * k:1024 * (k + 1)], gates_turned(k)).then_inc(sem("gT_made"), 1)

            turned_gates(0)
            for m in range(RING, 8 * NE1 * NH1):
                hidden_gelu(m)
                if m - RING in (1, 3, 5):
                    turned_gates((m - RING + 1) // 2)

        @block.tensor
        def _(pe):
            mm, tr = nc.tensor.matmul, nc.tensor.transpose
            pe.wait_ge(sem("ident_made"), 1)
            pe.wait_ge(sem("x_in"), 16)
            for q in range(NQ):
                if q >= 2:
                    pe.wait_ge(sem("xt_made"), q - 1)
                for i in range(QT):
                    t = QT * q + i
                    ins = tr(PS[:, q % 2, C * i:C * (i + 1)], xc[:, P * t:P * (t + 1)], ident[0:C, 0:C])
                ins.then_inc(sem("xt_turned"), 1)
            pe.wait_ge(sem("conv_weights_in"), 128)
            for g in range(4):
                ins = tr(PS[0:C, 4, P * g:P * (g + 1)], wkv0[:, g, :], ident[:, :])
            ins.then_inc(sem("weights_turned"), 1)
            for g in range(3):
                ins = tr(PS[0:C, 5, P * g:P * (g + 1)], wqkv1[:, g, :], ident[:, :])
            ins.then_inc(sem("weights_turned"), 1)
            for g in range(2):
                tr(PS[:, 6, C * g:C * (g + 1)], wo0[:, P * g:P * (g + 1)], ident[0:C, 0:C])
            tr(PS[:, 6, 2 * C:3 * C], wo1[:, :], ident[0:C, 0:C])
            tr(PS[:, 6, 3 * C:3 * C + NE0], b1r0[:, :], ident[0:NE0, 0:NE0])
            n1 = NE1 * NH1
            tr(PS[:, 6, 3 * C + NE0:3 * C + NE0 + n1], b1r1[:, :], ident[0:n1, 0:n1]).then_inc(sem("weights_turned"), 1)

            def channel_major(stage, first):
                for k in range(8):
                    pe.wait_ge(sem(f"{stage}_xn"), k // 2 + 1)
                    if k >= 2:
                        pe.wait_ge(sem(f"{stage}_xc"), k - 1)
                    elif k == 0:
                        first()
                    for i in range(4):
                        ins = tr(PS[0:C, 6 + k % 2, P * i:P * (i + 1)], xn[:, 4 * k + i, :], ident[:, :])
                    ins.then_inc(sem(f"{stage}_turned"), 1)

            def keys_of(L, G, wk, stage, u):
                q, g = u // G, u % G
                pe.wait_ge(sem(f"{stage}_xc"), 2 * q + 2)
                if u >= 2:
                    pe.wait_ge(sem(f"{L}_kexp"), QB * (u - 1))
                for h in range(2):
                    ins = mm(PS[:, 2 * (u % 2) + h, :], wk(g), xc[:, 1024 * q + 512 * h:1024 * q + 512 * (h + 1)],
                             start=True, stop=True)
                ins.then_inc(sem(f"{L}_kmade"), 1)

            def context_of(L, G, u):
                q, g = u // G, u % G
                pe.wait_ge(sem(f"{L}_kexp"), QB * (u + 1))
                if u >= 3:
                    pe.wait_ge(sem(f"{L}_t"), u - 2)
                for i in range(QT):
                    ins = tr(PS[:, 4 + i // 4, P * (i % 4):P * (i % 4 + 1)], ek[:, u % 2, P * i:P * (i + 1)], ident[:, :])
                ins.then_inc(sem(f"{L}_kturned"), 1)
                pe.wait_ge(sem(f"{L}_ekt_a"), u + 1)
                pe.wait_ge(sem(f"{L}_ekt_v"), u + 1)
                if u >= 1:
                    pe.wait_ge(sem(f"{L}_yv"), u)
                for b in range(QB):
                    for s in range(2):
                        ins = mm(PS[0:C, 6, P * b:P * (b + 1)], xn[:, QT * q + 2 * b + s, :], ekt[:, u % 2, 2 * b + s, :],
                                 start=(s == 0), stop=(s == 1))
                ins.then_inc(sem(f"{L}_ymade"), 1)

            def attention(L, G, wk, wv, wo, stage, after=lambda u: None):
                N = NQ * G
                for u in range(N + 3):
                    if u < N:
                        keys_of(L, G, wk, stage, u)
                    if 1 <= u <= N:
                        context_of(L, G, u - 1)
                    if 2 <= u <= N + 1:
                        q, g = (u - 2) // G, (u - 2) % G
                        pe.wait_ge(sem(f"{L}_yv"), u - 1)
                        if u >= 3:
                            pe.wait_ge(sem(f"{L}_ctx"), u - 2)
                        mm(PS[:, 7, :], wv(g), Ys[L == "c1"][:, g, QB * q:QB * (q + 1), :].rearrange("c b n -> c (b n)"),
                           start=True, stop=True).then_inc(sem(f"{L}_cmade"), 1)
                    if u >= 3:
                        q, g = (u - 3) // G, (u - 3) % G
                        pe.wait_ge(sem(f"{L}_ctx"), u - 2)
                        if u > N:
                            pe.wait_ge(sem(f"{L}_t"), u - 3)
                        for b in range(QB):
                            ins = mm(PS[:, 4, C * b:C * (b + 1)], ctxT[:, g, QB * q + b, :], wo[:, g, :],
                                     start=True, stop=True)
                        ins.then_inc(sem(f"{L}_tmade"), 1)
                    after(u)

            def after_weights():
                pe.wait_ge(sem("weights_made"), 4)

            channel_major("ln0", after_weights)
            attention("c0", 2, lambda g: wkvT0[:, P * g:P * (g + 1)], lambda g: wkvT0[:, 256 + P * g:256 + P * (g + 1)],
                      woT0, "ln0")
            pe.wait_ge(sem("c0_t"), 8)
            pe.wait_ge(sem("c0_ctx"), 8)
            for h in range(2):
                for g in range(2):
                    ins = mm(PS[0:C, 6 + h, :], wq0[:, g, :], T[:, g, 8 * h:8 * (h + 1), :].rearrange("p b n -> p (b n)"),
                             start=(g == 0), stop=(g == 1))
                ins.then_inc(sem("c0_mmade"), 1)
            pe.wait_ge(sem("c0_mt"), 2)
            for q in range(NQ):
                for i in range(QT):
                    t = QT * q + i
                    ins = mm(PS[:, q, C * i:C * (i + 1)], xc[:, P * t:P * (t + 1)], MT[:, t // 2, :], start=True, stop=True)
                ins.then_inc(sem("c0_out"), 1)

            channel_major("ln1", lambda: None)
            pe.wait_ge(sem("ln1_xc"), 8)
            pe.wait_ge(sem("wgat_made"), 2)
            W24 = FS + HEADS
            for t in range(NT):
                ins = mm(PS[:, t // 16, W24 * (t % 16):W24 * (t % 16 + 1)], xc[:, P * t:P * (t + 1)], wgat[:, :],
                         start=True, stop=True)
            ins.then_inc(sem("tables_turned"), 1)

            pe.wait_ge(sem("ffn0_weights_in"), 144)
            pe.wait_ge(sem("ones_made"), 1)
            pe.wait_ge(sem("bias0_made"), 1)
            pe.wait_ge(sem("tables_read"), 4)
            for k in range(2):
                mm(PS[:, k, 0:FH * LO], zeros[:, 0:P], zeros[:, :], start=True, stop=False)
            mm(PS[:, 2, 0:LO], zeros[:, 0:P], zeros[:, 0:LO], start=True, stop=False).then_inc(sem("sums_cleared"), 1)
            for name in ["prod_used"] * 2 + ["hist_used"] * HB:
                mm(PS[:, 7, 0:P], zeros[:, 0:P], zeros[:, 0:P], start=True, stop=True).then_inc(sem(name), 1)

            def scatter(it, a):
                pe.wait_ge(sem("prod_made"), nth(it, a))
                pe.wait_ge(sem("const0"), 2)
                for j in range(EB):
                    for k in range(2):
                        ins = mm(PS[:, k, 0:FH * LO], one_hi[:, a % 2, j, :], prod[:, a % 2, j, FH * k:FH * (k + 1), :],
                                 start=False, stop=False, skip_group_check=True)
                ins.then_inc(sem("prod_used"), 1)

            def histogram(it, k):
                h = (k + HP) % HB
                pe.wait_ge(sem("hist_made"), it * (2 * HI) + 2 * (k + HP + 1))
                pe.wait_ge(sem("const0"), 2)
                for c in range(HC):
                    ins = mm(PS[:, 2, 0:LO], hist_hi[h][:, :, c], hist_lo[h][:, :, c],
                             start=False, stop=False, skip_group_check=True)
                ins.then_inc(sem("hist_used"), 1)

            def hidden0(t, g, e):
                if e >= 2 or g >= 1:
                    pe.wait_ge(sem("h0_gelu"), t * (NE0 * G0) + (NE0 * g + e - 1))
                    nc.tensor.sem_inc(sem("h0_room"), 1)
                mm(PS[:, 3 + e % 2, 0:XT0], w1_0[:, e, :], xc[:, bass.ds(t * (XT0 * G0) + g * XT0, XT0)],
                   start=True, stop=True).then_inc(sem("h0_made"), 1)

            def second0(t, g, i):
                pe.wait_ge(sem("h0_gelu"), t * (NE0 * G0) + NE0 * (g + 1))
                if i >= 3 or g >= 1:
                    pe.wait_ge(sem("oute_made"), t * (OT * G0) + (OT * g + i - 2 if i >= 3 else OT * g))
                mm(PS[:, 5 + i % 3, 0:NE0 * C], ones[:, :], b2bias[:, :], start=True, stop=False, skip_group_check=True)
                for e in range(NE0):
                    ins = mm(PS[:, 5 + i % 3, C * e:C * (e + 1)], hid0[:, e, P * i:P * (i + 1)], w2_0[:, e, :],
                             start=False, stop=(e == NE0 - 1), skip_group_check=True)
                ins.then_inc(sem("o0_made"), 1)

            for k in range(-HP, 0):
                histogram(0, k)
            with nc.tensor.Fori(0, ITERS) as t:
                for a in range(NB):
                    g, part = a * G0 // NB, a % (NB // G0)
                    for n in range(2) if part < 2 else ():
                        hidden0(t, g, 2 * part + n)
                    for n in range(OT) if part == 2 else ():
                        second0(t, g, n)
                    for k in range(HB):
                        histogram(t, a * HB + k)
                    scatter(t, a)
                pe.wait_ge(sem("oute_made"), t * (OT * G0) + OT * G0)
            pe.wait_ge(sem("flag_made"), 1)
            left = nc.tensor.value_load(flagi[0:1, 0:1], min_val=0, max_val=1)
            with nc.tensor.If(left > 0):
                with nc.tensor.Fori(0, REST) as g:
                    with nc.tensor.Fori(0, ITERS) as t:
                        for a in range(NB):
                            scatter((g + 1) * ITERS + t, a)
            for k in range(2):
                mm(PS[:, k, 0:FH * LO], zeros[:, 0:P], zeros[:, :], start=False, stop=True)
            mm(PS[:, 2, 0:LO], zeros[:, 0:P], zeros[:, 0:LO], start=False, stop=True)\
                .then_inc(sem("sums_made"), 1)

            pe.wait_ge(sem("sums_read"), 1)
            for q in range(NQ):
                pe.wait_ge(sem("oute_gated"), q + 1)
                for e in range(NE0):
                    ins = mm(PS[:, q, :].rearrange("p (t c) -> p t c", c=C), ident[:, :],
                             oute[:, QT * q:QT * (q + 1), e, :], start=(e == 0), stop=(e == NE0 - 1))
                ins.then_inc(sem("oute_summed"), 1)

            channel_major("ln2", lambda: None)
            for u in range(8 + 2):
                if u < 8:
                    pe.wait_ge(sem("ln2_xc"), u + 1)
                    if u >= 3:
                        pe.wait_ge(sem("q_shifted"), u - 2)
                    for i in range(4):
                        t = 4 * u + i
                        ins = mm(queries(u)[:, P * i:P * (i + 1)], xc[:, P * t:P * (t + 1)], wqkvT1[:, 0:P],
                                 start=True, stop=True)
                    ins.then_inc(sem("q_made"), 1)
                if u >= 2:
                    v = u - 2
                    pe.wait_ge(sem("q_soft"), v + 1)
                    if v >= 2:
                        pe.wait_ge(sem("qc_made"), v - 1)
                    for i in range(4):
                        ins = tr(PS[:, 2 + v % 2, P * i:P * (i + 1)],
                                 qe(v)[:, 4 * i:4 * (i + 1), :].rearrange("p k d -> p (k d)"), ident[:, :])
                    ins.then_inc(sem("q_turned"), 1)
            pe.wait_ge(sem("qc_made"), 8)

            def output1(q):
                pe.wait_ge(sem("c1_t"), q + 1)
                pe.wait_ge(sem("c1_kexp"), QB * NQ)
                for i in range(QT):
                    t = QT * q + i
                    ins = mm(PS[:, q, C * i:C * (i + 1)], qc[:, P * t:P * (t + 1)], T[:, 0, t // 2, :], start=True, stop=True)
                ins.then_inc(sem("c1_out"), 1)

            attention("c1", 1, lambda g: wqkvT1[:, P:2 * P], lambda g: wqkvT1[:, 2 * P:3 * P], woT1, "ln2",
                      after=lambda u: output1(u - NQ) if u >= NQ else None)
            output1(NQ - 1)

            pe.wait_ge(sem("ident_b_made"), 1)
            for j in range(16):
                pe.wait_ge(sem("xs_made"), j // 4 + 1)
                if j >= 4:
                    pe.wait_ge(sem("xst_made"), j - 3)
                k, a = j // 2, j % 2
                for i in range(4):
                    ins = tr(turned(j)[:, P * i:P * (i + 1)],
                             xs[:, 4 * k + i, 2 * a:2 * a + 2, :].rearrange("p a c -> p (a c)"), ident_b[:, :])
                ins.then_inc(sem("xs_turned"), 1)
            pe.wait_ge(sem("xst_made"), 16)
            pe.wait_ge(sem("weights_split"), 1)
            PARTS = ((0, 0), (0, 1), (1, 2))
            for t in range(NT):
                for n, (a, k) in enumerate(PARTS):
                    ins = mm(PS[:, 7, NE1 * t:NE1 * (t + 1)], xst[:, a, P * t:P * (t + 1)], wg_s[:, k, :],
                             start=(n == 0), stop=(n == 2))
            ins.then_inc(sem("logits_made"), 1)
            def hidden1(m):
                n, k = m // (NE1 * NH1), m % (NE1 * NH1)
                if m >= 3:
                    pe.wait_ge(sem("h1_gelu"), m - 2)
                for j, (a, w) in enumerate(PARTS):
                    ins = mm(PS[:, m % 3, :], w1s[:, w, P * k:P * (k + 1)], xst[:, a, 512 * n:512 * (n + 1)],
                             start=(j == 0), stop=(j == 2))
                ins.then_inc(sem("h1_made"), 1)

            def spread(g):
                if g >= 2:
                    pe.wait_ge(sem("h1_gated"), NH1 * (g - 1))
                n = g // NE1
                pe.wait_ge(sem("gT_made"), n // 2 + 1)
                mm(PS[:, 3 + g % 2, :], pick[:, g % NE1, :], gT[:, 512 * n:512 * (n + 1)],
                   start=True, stop=True).then_inc(sem("g_spread"), 1)

            def second1(m):
                n, k = m // (NE1 * NH1), m % (NE1 * NH1)
                if k == 0:
                    pe.wait_ge(sem("gT_made"), 4 if n >= 1 else 1)
                    if n >= 2:
                        pe.wait_ge(sem("y_made"), n - 1)
                    for j in range(3):
                        mm(PS[0:C, 5 + n % 2, :], b2s[:, j, :], gT[:, 512 * n:512 * (n + 1)], start=(j == 0), stop=False)
                pe.wait_ge(sem("h1_gated"), m + 1)
                ins = mm(PS[0:C, 5 + n % 2, :], w2_1[:, k // NH1, k % NH1, :], rings[m % RING],
                         start=False, stop=(k == NE1 * NH1 - 1))
                ins.then_inc(sem("h1_used"), 1)

            M1 = 8 * NE1 * NH1
            for m in range(RING):
                hidden1(m)
                if m < 8:
                    if m >= 2:
                        pe.wait_ge(sem("x3_made"), m - 1)
                    for i in range(4):
                        ins = tr(PS[0:C, 5 + m % 2, P * i:P * (i + 1)], xt[:, 4 * m + i, :], ident[:, :])
                    ins.then_inc(sem("x3_turned"), 1)
            pe.wait_ge(sem("x3_made"), 8)
            def turn_gates(k):
                if k >= 2:
                    pe.wait_ge(sem("gT_made"), k - 1)
                for i in range(8):
                    ins = tr(gates_turned(k)[:, P * i:P * (i + 1)],
                             gparts[:, 8 * k + i, :, :].rearrange("p a e -> p (a e)"), ident_b[:, :])
                ins.then_inc(sem("g_turned"), 1)

            pe.wait_ge(sem("gates1"), 1)
            turn_gates(0)
            for g in range(2):
                spread(g)
            for m in range(M1):
                second1(m)
                if m + RING < M1:
                    hidden1(m + RING)
                if m in (1, 3, 5):
                    turn_gates((m + 1) // 2)
                if m % NH1 == 1 and m // NH1 + 2 < M1 // NH1:
                    spread(m // NH1 + 2)

        @block.vector
        def _(dve):
            V = nc.vector
            steps = [0]

            def then(ins):
                steps[0] += 1
                ins.then_inc(sem("dve_steps"), 1)
                dve.wait_ge(sem("dve_steps"), steps[0])

            for g in range(4):
                s = slice(32 * g, 32 * g + 32)
                if g == 0:
                    then(V.memset(blocks[:, :], 0.0))
                ins = V.memset(blocks[s, s], 1.0)
            then(ins)
            dve.wait_ge(sem("const0"), 2)
            then(V.tensor_copy(iota[:, :], iota_i[:, :]))
            then(V.tensor_copy(iota_h[:, :, :], bc(iota[:, :], 2, HC)))
            dve.wait_ge(sem("ident_made"), 1)
            V.tensor_copy(ident_b[:, :], ident[:, :]).then_inc(sem("ident_b_made"), 1)
            for a in range(RB):
                V.memset(gs[:, a, :, :], 0.0).then_inc(sem("rows_used"), 1)

            def compact(r):
                if r == 0:
                    dve.wait_ge(sem("pad_made"), 1)
                S, first = ROUNDS[r], sum(ROUNDS[:r])
                segs = [rows[:, EC // S * k:EC // S * (k + 1)] for k in range(S)]
                tops = [keys[:, TOP * (first + k):TOP * (first + k + 1)] for k in range(S)]
                for k in range(S):
                    V.max(tops[k], segs[k]).then_inc(sem("top_found"), 1)
                dve.wait_ge(sem("top_found"), first + S)
                for k in range(S):
                    V.match_replace(segs[k], tops[k], segs[k], 0.0).then_inc(sem("top_removed"), 1)
                dve.wait_ge(sem("top_removed"), first + S)

            def decode(col):
                k0 = keys[:, bass.ds(col, GC)]
                k = dec[:, 0, :]
                ki, hi_i, lo_i = deci[:, 0, :], deci[:, 1, :], deci[:, 2, :]
                yield V.tensor_scalar(dec[:, 1, :], k0, 0.5, None, ALU.is_gt)
                yield V.tensor_scalar(ki, k0, -1.0, 0.0, ALU.add, ALU.max)
                yield V.tensor_scalar(idx_s, ki, 12, None, ALU.logical_shift_right)
                yield V.tensor_scalar(idx_d, ki, NODES - 1, None, ALU.bitwise_and)
                yield V.tensor_scalar(hi_i, idx_d, P - 1, None, ALU.bitwise_and)
                yield V.tensor_scalar(lo_i, idx_d, 7, None, ALU.logical_shift_right)
                yield V.scalar_tensor_tensor(out=k, in0=hi_i, scalar=1.0, in1=dec[:, 1, :], op0=ALU.add, op1=ALU.mult)
                yield V.tensor_scalar(dhi[:, :], k, -1.0, None, ALU.add)
                yield V.tensor_copy(dlo[:, :], lo_i)

            DECODE_STEPS = 8

            def edges_ready():
                V.tensor_reduce(flagf[:, 0:1], rows, X, ALU.max).then_inc(sem("rest_max"), 1)
                for n, ins in enumerate(decode(0)):
                    if n < DECODE_STEPS:
                        then(ins)
                ins.then_inc(sem("decoded"), 1)

            def sums(q, src, stage):
                T8 = slice(QT * q, QT * (q + 1))
                then(V.tensor_reduce(red[:, 0, T8], src[:, T8, :], X, ALU.add))
                then(V.tensor_scalar(red[:, 1, T8], red[:, 0, T8], -1.0 / C, None, ALU.mult))
                V.tensor_tensor(xn[:, T8, :], src[:, T8, :], bc(red[:, 1, T8], 2, C), ALU.add)\
                    .then_inc(sem(f"{stage}_centred"), 1)

            def scaled(q, stage, signal):
                T8 = slice(QT * q, QT * (q + 1))
                dve.wait_ge(sem(f"{stage}_rstd"), q + 1)
                V.tensor_tensor(xn[:, T8, :], xn[:, T8, :], bc(red[:, 3, T8], 2, C), ALU.mult)\
                    .then_inc(sem(signal), 1)

            def layer_norm(stage, ready, after=None):
                for q in range(NQ):
                    ready(q)
                    sums(q, xt, stage)
                for q in range(NQ):
                    scaled(q, stage, f"{stage}_xn")
                    if after:
                        after(q)

            layer_norm("ln0", lambda q: dve.wait_ge(sem("xt_made"), q + 1))
            dve.wait_ge(sem("edges_in"), 16)
            src_i, dst_i = ebi[:, 0, :], ebi[:, 1, :]
            V.tensor_scalar(live, src_i, float(NODES - 1) - 0.5, None, ALU.is_lt)
            then(V.scalar_tensor_tensor(out=rows, in0=src_i, scalar=float(NODES), in1=dst_i, op0=ALU.mult, op1=ALU.add))
            then(V.scalar_tensor_tensor(out=key2, in0=dst_i, scalar=float(NODES) - 0.5, in1=live, op0=ALU.is_lt,
                                        op1=ALU.mult))
            ins = V.scalar_tensor_tensor(out=rows, in0=rows, scalar=1.0, in1=key2, op0=ALU.add, op1=ALU.mult)
            ins.then_inc(sem("keys_made"), 1)
            dve.wait_ge(sem("keys_made"), 1)

            def pixel_attention(L, G, between=lambda u: None):
                N = NQ * G
                for u in range(N + 3):
                    if u < N:
                        dve.wait_ge(sem(f"{L}_kmade"), u + 1)
                        V.tensor_reduce(nmx[:, u, :], PS[:, 2 * (u % 2):2 * (u % 2) + 2, :]
                                        .rearrange("p a (b n) -> p (a b) n", n=HW), X, ALU.max,
                                        negate=True).then_inc(sem(f"{L}_kmax"), 1)
                    if 1 <= u <= N:
                        v = u - 1
                        dve.wait_ge(sem(f"{L}_kturned"), v + 1)
                        if v >= 2:
                            dve.wait_ge(sem(f"{L}_ymade"), v - 1)
                        V.tensor_copy(ekt[:, v % 2, 0:4, :], PS[:, 4, :].rearrange("p (t n) -> p t n", n=P))\
                            .then_inc(sem(f"{L}_ekt_v"), 1)
                    between(u)
                    if 2 <= u <= N + 1:
                        v = u - 2
                        q, g = v // G, v % G
                        dve.wait_ge(sem(f"{L}_cmade"), v + 1)
                        V.tensor_tensor(ctxT[:, g, QB * q:QB * (q + 1), :],
                                        PS[:, 7, :].rearrange("p (b n) -> p b n", n=P), bc(blocks[:, :], 1, QB),
                                        ALU.mult).then_inc(sem(f"{L}_ctx"), 1)
                    if u >= 3:
                        v = u - 3
                        q, g = v // G, v % G
                        dve.wait_ge(sem(f"{L}_kexp"), QB * (v + 1))
                        r = rks[:, g, QB * q:QB * (q + 1)]
                        then(V.reciprocal(r, ksum[:, g, QB * q:QB * (q + 1)]))
                        if G == 1:
                            then(V.tensor_scalar(r, r, HEAD_DIM ** -0.5, None, ALU.mult))
                        dve.wait_ge(sem(f"{L}_tmade"), v + 1)
                        V.tensor_tensor(T[:, g, QB * q:QB * (q + 1), :],
                                        PS[:, 4, 0:QB * C].rearrange("p (b n) -> p b n", n=C),
                                        bc(r, 2, C), ALU.mult).then_inc(sem(f"{L}_t"), 1)

            def between0(u):
                R = len(ROUNDS) - 3
                for r in range(R * u // 8, R * (u + 1) // 8) if u < 8 else ():
                    compact(r)

            pixel_attention("c0", 2, between0)
            compact(len(ROUNDS) - 3)
            dve.wait_ge(sem("bias_added"), 1)

            def add_attention(q):
                dve.wait_ge(sem("c0_out"), q + 1)
                T8 = slice(QT * q, QT * (q + 1))
                then(V.tensor_tensor(xt[:, T8, :], xt[:, T8, :], PS[:, q, :].rearrange("p (t c) -> p t c", c=C), ALU.add))

            dve.wait_ge(sem("ffn0_weights_in"), 144)
            then(V.tensor_tensor(attm[:, :, :], attr[:, :, :], bc(wgat[:, HEADS:FS], 1, 2), ALU.mult))
            for k, c in ((0, 0), (1, FS)):
                V.tensor_reduce(wgat[:, c:c + HEADS], attm[:, k, :].rearrange("p (h e) -> p h e", e=NE0), X, ALU.add)\
                    .then_inc(sem("wgat_made"), 1)
            layer_norm("ln1", add_attention)

            compact(len(ROUNDS) - 2)
            compact(len(ROUNDS) - 1)
            edges_ready()
            then(V.tensor_copy(b2parts[:, 0, :], b2row[:, :]))
            then(V.tensor_tensor(b2rest, b2row[:, :], b2parts[:, 0, :], ALU.subtract))
            then(V.tensor_copy(b2parts[:, 1, :], b2rest))
            then(V.tensor_tensor(b2parts[:, 2, :], b2rest, b2parts[:, 1, :], ALU.subtract))
            then(V.tensor_scalar(b2bias[:, :], b2parts[:, 0, :], ident[0:3, 0:1], None, ALU.mult))
            for k in range(1, 3):
                ins = V.scalar_tensor_tensor(out=b2bias[:, :], in0=b2parts[:, k, :], scalar=ident[0:3, k:k + 1],
                                             in1=b2bias[:, :], op0=ALU.mult, op1=ALU.add)
                if k == 1:
                    then(ins)
            ins.then_inc(sem("bias0_made"), 1)

            dve.wait_ge(sem("tables_turned"), 1)
            W24 = FS + HEADS
            for k in range(2):
                src = PS[:, k, 0:16 * W24].rearrange("p (t f) -> p t f", f=W24)
                V.tensor_copy(tab_s[:, 16 * k:16 * (k + 1), :], src[:, :, 0:FS]).then_inc(sem("tables_read"), 1)
                V.tensor_copy(tab_d[:, 16 * k:16 * (k + 1), 0:HEADS], src[:, :, FS:W24]).then_inc(sem("tables_read"), 1)
            dve.wait_ge(sem("tables_read"), 4)
            V.tensor_reduce(gmax[:, 0, :], tab_s[:, :, 0:HEADS].rearrange("p t h -> p h t"), X, ALU.max)\
                .then_inc(sem("score_max"), 1)

            dve.wait_ge(sem("score_all"), 1)
            then(V.tensor_tensor(nod[:, 4, :, :], tab_d[:, :, 0:HEADS], bc(gmax[:, 1, :], 1, NT), ALU.add))
            V.scalar_tensor_tensor(out=tab_d[:, :, HEADS:FD], in0=nod[:, 4, :, :], scalar=SLOPE, in1=nod[:, 4, :, :],
                                   op0=ALU.mult, op1=ALU.max).then_inc(sem("tables_made"), 1)
            dve.wait_ge(sem("rest_all"), 1)
            V.tensor_scalar(flagi[:, :], flagf[:, 1:2], 0.5, None, ALU.is_gt).then_inc(sem("flag_made"), 1)
            dve.wait_ge(sem("tables_made"), 1)
            ad, guard = tab_d[:, :, 0:HEADS], tab_d[:, :, HEADS:FD]
            for k in range(2):
                if k:
                    dve.wait_ge(sem("last_in"), 16)
                a = tab_s[:, :, 0:HEADS] if k == 0 else bc(last[:, 0:HEADS], 1, NT)
                st = list(leaky_steps(V, nod[:, k, :, :], nod[:, 4, :, :], a, ad, guard))
                for n, f in enumerate(st):
                    ins = f()
                    if n < 2:
                        then(ins)
                    else:
                        ins.then_inc(sem("node_scores"), 1)
                dve.wait_ge(sem("node_scores"), k + 1)

            dve.wait_ge(sem("sums_cleared"), 1)

            EDGE_STEPS = 4 * NB

            def one_hots(t, k):
                h = (k + HP) % HB
                dve.wait_ge(sem("hist_used"), t * HI + (k + HP + 1))
                c = t * (HI * HC) + (k + HP) * HC
                V.tensor_tensor(hist_hi[h], bc(dhi_h[:, bass.ds(c, HC)], 1, P), iota_h[:, :, :],
                                ALU.is_equal).then_inc(sem("hist_made"), 1)
                V.tensor_tensor(hist_lo[h], bc(dlo_h[:, bass.ds(c, HC)], 1, LO), iota_h[:, 0:LO, :],
                                ALU.is_equal).then_inc(sem("hist_made"), 1)

            def edge_block(it, t, with_hist):
                n = [0]

                def step(ins):
                    n[0] += 1
                    ins.then_inc(sem("dve_edge"), 1)

                def settle():
                    dve.wait_ge(sem("dve_edge"), it * EDGE_STEPS + n[0])

                for a in range(NB):
                    b, r = a % 2, a % RB
                    if with_hist:
                        for k in range(HB):
                            one_hots(t, a * HB + k)
                    dve.wait_ge(sem(f"rows_in{r}"), it * (32 * EB * NB // RB) + 32 * EB * (a // RB + 1))
                    dve.wait_ge(sem("const0"), 2)
                    e1, e2, e3 = (es[:, b, k, :, :] for k in range(3))
                    step(V.tensor_tensor(e1, gs[:, r, :, 0:HEADS], gd[:, r, :, 0:HEADS], ALU.add))
                    settle()
                    step(V.scalar_tensor_tensor(out=e2, in0=e1, scalar=SLOPE, in1=e1, op0=ALU.mult, op1=ALU.max))
                    settle()
                    V.tensor_tensor(e3, e2, gd[:, r, :, HEADS:FD], ALU.subtract).then_inc(sem("edge_scores"), 1)
                    dve.wait_ge(sem("prod_used"), nth(it, a))
                    c0 = t * ITC + a * EB
                    step(V.tensor_tensor(one_hi[:, b, :, :], bc(dhi[:, bass.ds(c0, EB)], 2, P), bc(iota[:, :], 1, EB),
                                         ALU.is_equal))
                    step(V.tensor_tensor(one_lo[:, b, :, :], bc(dlo[:, bass.ds(c0, EB)], 2, LO),
                                         bc(iota[:, 0:LO], 1, EB), ALU.is_equal))
                    dve.wait_ge(sem("edge_exps"), nth(it, a))
                    v = val[:, b, :, :]
                    V.tensor_tensor(v[:, :, 0:F0].rearrange("p j (h e) -> p j h e", e=NE0),
                                    gs[:, r, :, HEADS:FS].rearrange("p j (h e) -> p j h e", e=NE0),
                                    bc(v[:, :, F0:FV], 3, NE0), ALU.mult).then_inc(sem("rows_used"), 1)
                    settle()
                    dve.wait_ge(sem("rows_used"), nth(it, a) + RB)
                    V.tensor_tensor(prod[:, b, :, :, :], bc(one_lo[:, b, :, :], 2, FV), bc(v, 3, LO), ALU.mult)\
                        .then_inc(sem("prod_made"), 1)
                assert n[0] == EDGE_STEPS

            dve.wait_ge(sem("hist_indices"), 1)
            for k in range(-HP, 0):
                one_hots(0, k)
            with V.Fori(0, ITERS) as t:
                edge_block(t, t, True)
            left = V.value_load(flagi[0:1, 0:1], min_val=0, max_val=1)
            with V.If(left > 0):
                with V.Fori(0, REST) as g:
                    for n, ins in enumerate(decode(GC + g * GC)):
                        if n < DECODE_STEPS:
                            ins.then_inc(sem("rest_steps"), 1)
                            dve.wait_ge(sem("rest_steps"), g * DECODE_STEPS + (n + 1))
                    ins.then_inc(sem("decoded"), 1)
                    dve.wait_ge(sem("decoded"), g + 2)
                    V.sem_inc(sem("decode_seen"), 1)
                    with V.Fori(0, ITERS) as t:
                        edge_block((g + 1) * ITERS + t, t, False)

            dve.wait_ge(sem("node_exps"), 2)
            h_self, h_last = tab_s[:, :, HEADS:FS], last[:, HEADS:FS]

            def by_head(ap):
                return ap.rearrange("p t (h e) -> p t h e", e=NE0)

            dve.wait_ge(sem("sums_made"), 1)
            for k in range(2):
                V.tensor_copy(num[:, 0, :, FH * k:FH * (k + 1)], PS[:, k, 0:FH * LO].rearrange("p (f t) -> p t f", t=LO))
            ins = V.tensor_tensor(nod[:, 3, :, :], nod[:, 3, :, :], bc(PS[:, 2, 0:LO], 2, HEADS), ALU.mult)
            ins.then_inc(sem("sums_read"), 1)
            dve.wait_ge(sem("sums_read"), 1)
            then(V.tensor_tensor(by_head(num[:, 1, :, 0:F0]), by_head(h_self), bc(nod[:, 2, :, :], 3, NE0), ALU.mult))
            then(V.tensor_tensor(num[:, 0, :, 0:F0], num[:, 0, :, 0:F0], num[:, 1, :, 0:F0], ALU.add))
            then(V.tensor_tensor(by_head(num[:, 1, :, 0:F0]), by_head(bc(h_last, 1, NT)), bc(nod[:, 3, :, :], 3, NE0),
                                 ALU.mult))
            then(V.tensor_tensor(num[:, 0, :, 0:F0], num[:, 0, :, 0:F0], num[:, 1, :, 0:F0], ALU.add))
            then(V.tensor_tensor(num[:, 0, :, F0:FV], num[:, 0, :, F0:FV], nod[:, 2, :, :], ALU.add))
            then(V.scalar_tensor_tensor(out=num[:, 0, :, F0:FV], in0=num[:, 0, :, F0:FV], scalar=1e-16,
                                        in1=nod[:, 3, :, :], op0=ALU.add, op1=ALU.add))
            then(V.reciprocal(nod[:, 4, :, :], num[:, 0, :, F0:FV]))
            then(V.tensor_tensor(by_head(num[:, 0, :, 0:F0]), by_head(num[:, 0, :, 0:F0]), bc(nod[:, 4, :, :], 3, NE0),
                                 ALU.mult))
            agg = num[:, 0, :, 0:F0]
            tmp = num[:, 1, :, 0:F0]
            then(V.tensor_tensor(agg, agg, bc(gat_rows[:, 0, :], 1, NT), ALU.add))
            then(V.tensor_reduce(red[:, 0, :], agg, X, ALU.add))
            then(V.tensor_scalar(red[:, 1, :], red[:, 0, :], -1.0 / F0, None, ALU.mult))
            then(V.tensor_tensor(agg, agg, bc(red[:, 1, :], 2, F0), ALU.add))
            then(V.tensor_tensor(tmp, agg, agg, ALU.mult))
            then(V.tensor_reduce(red[:, 0, :], tmp, X, ALU.add))
            V.tensor_scalar(red[:, 2, :], red[:, 0, :], 1.0 / F0, LN_EPS, ALU.mult, ALU.add).then_inc(sem("gat_var"), 1)
            dve.wait_ge(sem("gat_rstd"), 1)
            then(V.tensor_tensor(agg, agg, bc(red[:, 3, :], 2, F0), ALU.mult))
            then(V.tensor_tensor(agg, agg, bc(gat_rows[:, 1, :], 1, NT), ALU.mult))
            then(V.tensor_tensor(agg, agg, bc(gat_rows[:, 2, :], 1, NT), ALU.add))
            then(V.tensor_reduce(sc[:, 0, :, 0:NE0], agg.rearrange("p t (h e) -> p t e h", e=NE0), X, ALU.add))
            then(V.tensor_scalar(sc[:, 0, :, 0:NE0], sc[:, 0, :, 0:NE0], 1.0 / HEADS, None, ALU.mult))

            def gates(n, N, tmp, parts=False):
                s = sc[:, 0, :, 0:N]
                over = tmp.rearrange("p (t e j) -> p t e j", e=N, j=N)
                for j in range(N):
                    sj = s[:, :, j:j + 1]
                    ins = V.tensor_tensor(over[:, :, 0:j + 1, j], sj.broadcast_to([P, NT, j + 1]), s[:, :, 0:j + 1],
                                          ALU.is_gt)
                    if j + 1 < N:
                        ins = V.tensor_tensor(over[:, :, j + 1:, j], sj.broadcast_to([P, NT, N - 1 - j]),
                                              s[:, :, j + 1:], ALU.is_ge)
                then(ins)
                then(V.tensor_reduce(sc[:, 3, :, 0:N], over, X, ALU.add))
                then(V.tensor_reduce(red[:, 4, :], s, X, ALU.max))
                V.tensor_tensor(sc[:, 1, :, 0:N], s, bc(red[:, 4, :], 2, N), ALU.subtract).then_inc(sem(f"gate_in{n}"), 1)
                dve.wait_ge(sem(f"gate_exp{n}"), 1)
                then(V.scalar_tensor_tensor(out=sc[:, 2, :, 0:N], in0=sc[:, 3, :, 0:N], scalar=1.5,
                                            in1=sc[:, 2, :, 0:N], op0=ALU.is_lt, op1=ALU.mult))
                then(V.tensor_reduce(red[:, 5, :], sc[:, 2, :, 0:N], X, ALU.add))
                then(V.reciprocal(red[:, 6, :], red[:, 5, :]))
                g = sc[:, 3, :, 0:N]
                then(V.tensor_tensor(g, sc[:, 2, :, 0:N], bc(red[:, 6, :], 2, N), ALU.mult))
                if parts:
                    then(V.tensor_copy(gparts[:, :, 0, :], g))
                    then(V.tensor_tensor(sc[:, 1, :, :], g, gparts[:, :, 0, :], ALU.subtract))
                    then(V.tensor_copy(gparts[:, :, 1, :], sc[:, 1, :, :]))
                    V.tensor_tensor(gparts[:, :, 2, :], sc[:, 1, :, :], gparts[:, :, 1, :], ALU.subtract)\
                        .then_inc(sem("gates1"), 1)

            gate_tmp = num[:, :, :, :].rearrange("p a t f -> p (a t f)")
            gates(0, NE0, gate_tmp[:, 0:512])
            dve.wait_ge(sem("oute_made"), NT)
            for q in range(NQ):
                T8 = slice(QT * q, QT * (q + 1))
                V.tensor_tensor(oute[:, T8, :, :], oute[:, T8, :, :], bc(sc[:, 3, T8, 0:NE0], 3, C), ALU.mult)\
                    .then_inc(sem("oute_gated"), 1)

            def add_experts(q):
                T8 = slice(QT * q, QT * (q + 1))
                dve.wait_ge(sem("oute_summed"), q + 1)
                then(V.tensor_tensor(xt[:, T8, :], xt[:, T8, :], PS[:, q, :].rearrange("p (t c) -> p t c", c=C), ALU.add))

            dve.wait_ge(sem("layer1_weights_in"), 144)
            then(V.tensor_scalar(gn1[:, :], gn1[:, :], float(C) ** 0.5, None, ALU.mult))
            then(V.tensor_scalar(go1[:, :], go1[:, :], float(C) ** 0.5, None, ALU.mult))
            layer_norm("ln2", add_experts)
            for u in range(8 + 1):
                if u < 8:
                    dve.wait_ge(sem("q_made"), u + 1)
                    if u >= 4:
                        dve.wait_ge(sem("q_turned"), u - 3)
                    src = queries(u).rearrange("p (k d) -> p k d", d=HEAD_DIM)
                    top = red[:, 4, 16 * (u % 2):16 * (u % 2) + 16]
                    then(V.tensor_reduce(top, src, X, ALU.max))
                    V.tensor_tensor(qe(u), src, bc(top, 2, HEAD_DIM), ALU.subtract).then_inc(sem("q_shifted"), 1)
                if u >= 1:
                    dve.wait_ge(sem("q_exp"), u)
                    then(V.tensor_reduce(red[:, 5, 0:16], qe(u - 1), X, ALU.add))
                    then(V.reciprocal(red[:, 6, 0:16], red[:, 5, 0:16]))
                    V.tensor_tensor(qe(u - 1), qe(u - 1), bc(red[:, 6, 0:16], 2, HEAD_DIM), ALU.mult)\
                        .then_inc(sem("q_soft"), 1)
            pixel_attention("c1", 1)
            for q in range(NQ):
                dve.wait_ge(sem("c1_out"), q + 1)
                T8 = slice(QT * q, QT * (q + 1))
                V.tensor_tensor(xn[:, T8, :], PS[:, q, :].rearrange("p (t c) -> p t c", c=C),
                                bc(bo1[:, :], 1, QT), ALU.add).then_inc(sem("ln3r_centred"), 1)

            def add_attention1(q):
                scaled(q, "ln3r", "z_scaled")
                dve.wait_ge(sem("z_scaled"), q + 1)
                T8 = slice(QT * q, QT * (q + 1))
                then(V.tensor_tensor(sq[:, T8, :], xn[:, T8, :], bc(go1[:, :], 1, QT), ALU.mult))
                then(V.tensor_tensor(xt[:, T8, :], xt[:, T8, :], sq[:, T8, :], ALU.add))

            def split_tokens(q):
                T8 = slice(QT * q, QT * (q + 1))
                dve.wait_ge(sem("ln4_xn"), q + 1)
                V.tensor_copy(xs[:, T8, 2, :], xn[:, T8, :])
                then(V.tensor_copy(xs[:, T8, 0, :], xn[:, T8, :]))
                then(V.tensor_tensor(sq[:, T8, :], xn[:, T8, :], xs[:, T8, 0, :], ALU.subtract))
                then(V.tensor_copy(xs[:, T8, 1, :], sq[:, T8, :]))
                V.tensor_tensor(xs[:, T8, 3, :], sq[:, T8, :], xs[:, T8, 1, :], ALU.subtract).then_inc(sem("xs_made"), 1)

            layer_norm("ln4", add_attention1, after=split_tokens)

            dve.wait_ge(sem("logits_made"), 1)
            then(V.tensor_tensor(sc[:, 0, :, :], PS[:, 7, 0:NE1 * NT].rearrange("p (t e) -> p t e", e=NE1),
                                 bc(bgb[:, :], 1, NT), ALU.add))
            gates(1, NE1, sq[:, :, :].rearrange("p t c -> p (t c)"), parts=True)

            def last_sum(n):
                dve.wait_ge(sem("h1_used"), NE1 * NH1 * (n + 1))
                y = ob[0:C, 512 * n:512 * (n + 1)]
                V.tensor_tensor(y, y, PS[0:C, 5 + n % 2, :], ALU.add).then_inc(sem("y_made"), 1)

            for m in range(8 * NE1 * NH1):
                dve.wait_ge(sem("h1_gelu"), m + 1)
                dve.wait_ge(sem("g_spread"), m // NH1 + 1)
                h = rings[m % RING]
                V.tensor_tensor(h, h, PS[:, 3 + (m // NH1) % 2, :], ALU.mult).then_inc(sem("h1_gated"), 1)
                n, k = m // (NE1 * NH1), m % (NE1 * NH1)
                if n >= 1 and k == 6 or m == 8 * NE1 * NH1 - 1:
                    last_sum(n - 1 if m < 8 * NE1 * NH1 - 1 else n)


def leaky_steps(V, dst, tmp, a, b, guard):
    return (lambda: V.tensor_tensor(tmp, a, b, ALU.add),
            lambda: V.scalar_tensor_tensor(out=tmp, in0=tmp, scalar=SLOPE, in1=tmp, op0=ALU.mult, op1=ALU.max),
            lambda: V.tensor_tensor(dst, tmp, guard, ALU.subtract))


_INS = ['x', 'L0_conv_w_qkv', 'L0_conv_w_out', 'L0_conv_b_out', 'L0_ffn_W_gat', 'L0_ffn_att_src', 'L0_ffn_att_dst',
        'L0_ffn_b_gat', 'L0_ffn_ln_gamma', 'L0_ffn_ln_beta', 'L0_ffn_W1', 'L0_ffn_b1', 'L0_ffn_W2', 'L0_ffn_b2',
        'L0_ffn_edge_index', 'L1_conv_W_qkv', 'L1_conv_W_out', 'L1_conv_b_out', 'L1_conv_g_norm', 'L1_conv_g_out',
        'L1_ffn_Wg', 'L1_ffn_bg', 'L1_ffn_W1', 'L1_ffn_b1', 'L1_ffn_W2', 'L1_ffn_b2']


def kernel(**inputs):
    import numpy as _np
    import concourse.bacc as _bacc
    from concourse.bass_utils import run_bass_kernel_spmd as _run

    nc = _bacc.Bacc("TRN2", target_bir_lowering=False, num_devices=1)
    arrays, args = {}, []
    for name in _INS:
        a = _np.ascontiguousarray(inputs[name])
        arrays[f"in_{name}_dram"] = a
        args.append(nc.dram_tensor(f"in_{name}_dram", a.shape, mybir.dt.from_np(a.dtype), kind="ExternalInput").ap())
    out = nc.dram_tensor("out_0_dram", (B, C, 16, 16), F32, kind="ExternalOutput").ap()
    table_s = nc.dram_tensor("table_s_dram", (NODES, FS), F32, kind="Internal").ap()
    table_d = nc.dram_tensor("table_d_dram", (NODES, FD), F32, kind="Internal").ap()
    metaformer(nc, args, table_s, table_d, out)
    r = _run(nc, [arrays], core_ids=[0])
    return r.results[0]["out_0_dram"]
```
